# Optimizing a Trainium2 kernel written in Bass

```python
import numpy as np
import jax
import jax.numpy as jnp

def _softmax(x, axis=-1):
    return jax.nn.softmax(x, axis=axis)

def _gelu(x):
    return jax.nn.gelu(x, approximate=True)

def _silu(x):
    return jax.nn.silu(x)

def _sigmoid(x):
    return jax.nn.sigmoid(x)

def _layernorm(x, axis=-1, eps=1e-05):
    m = jnp.mean(x, axis=axis, keepdims=True)
    v = jnp.var(x, axis=axis, keepdims=True)
    return (x - m) / jnp.sqrt(v + eps)

def _scatter_add(tgt, idx, src, axis=0):
    return tgt.at[idx].add(src)

def _segment_sum(src, seg, n):
    return jax.ops.segment_sum(src, seg, n)
kernel_name = 'mk_gnn_resnorm_d2_gnn_r64_480b40'

def setup_inputs(seed: int=0):
    np.random.seed(seed)
    _w = jnp.asarray

    def _rec_inputs():
        import jax
        import jax.numpy as jnp
        _gk = jax.random.key(seed)
        x = -0.000202 + 1 * jax.random.normal(jax.random.fold_in(_gk, 1), (100000, 128), jnp.float32)
        _s = jax.random.randint(jax.random.fold_in(_gk, 2), (25000,), 0, 100000, jnp.int32)
        _d = jax.random.randint(jax.random.fold_in(_gk, 3), (25000,), 0, 100000, jnp.int32)
        _loop = jnp.arange(100000, dtype=jnp.int32)
        src = jnp.concatenate([_s, _d, _loop])
        dst = jnp.concatenate([_d, _s, _loop])
        _o = jnp.argsort(dst, stable=True)
        src = src[_o]
        dst = dst[_o]
        return (x, src, dst)
    x, src, dst = _rec_inputs()

    def _L0_gnn_setup():
        import jax, jax.numpy as jnp
        import numpy as np
        N_NODES = 50000
        N_EDGES = 12500
        D = 128
        EPS_LN = 1e-05
        EPS_BN = 1e-05
        LEAKY_SLOPE = 0.01

        def _layer_norm(x, g, b):
            mu = jnp.mean(x, axis=-1, keepdims=True)
            var = jnp.mean(jnp.square(x - mu), axis=-1, keepdims=True)
            return g * (x - mu) * jax.lax.rsqrt(var + EPS_LN) + b

        def _gcn_conv(x, edge_index, w, b):
            n = x.shape[0]
            loops = jnp.arange(n, dtype=edge_index.dtype)
            row = jnp.concatenate([edge_index[0], loops])
            col = jnp.concatenate([edge_index[1], loops])
            deg = jax.ops.segment_sum(jnp.ones_like(col, dtype=x.dtype), col, num_segments=n)
            dinv = jnp.where(deg > 0, jax.lax.rsqrt(jnp.maximum(deg, 1.0)), 0.0)
            norm = dinv[row] * dinv[col]
            h = x @ w
            msg = h[row] * norm[:, None]
            agg = jax.ops.segment_sum(msg, col, num_segments=n)
            return agg + b
        key = jax.random.key(seed)
        ks = jax.random.split(key, 8)
        x = jax.random.normal(ks[0], (N_NODES, D), dtype=jnp.float32)
        edge_index = jax.random.randint(ks[1], (2, N_EDGES), 0, N_NODES, dtype=jnp.int32)
        gcn_w = jax.random.normal(ks[2], (D, D), dtype=jnp.float32) * 0.05
        gcn_b = jnp.zeros((D,), dtype=jnp.float32)
        rs_w = jax.random.normal(ks[3], (D, D), dtype=jnp.float32) * 0.05
        rs_b = jnp.zeros((D,), dtype=jnp.float32)
        ln_g = jnp.ones((D,), dtype=jnp.float32)
        ln_b = jnp.zeros((D,), dtype=jnp.float32)
        bn_g = jnp.ones((D,), dtype=jnp.float32)
        bn_b = jnp.zeros((D,), dtype=jnp.float32)
        return {'x': x, 'edge_index': edge_index, 'gcn_w': gcn_w, 'gcn_b': gcn_b, 'rs_w': rs_w, 'rs_b': rs_b, 'ln_g': ln_g, 'ln_b': ln_b, 'bn_g': bn_g, 'bn_b': bn_b}
    _L0_gnn_all = _L0_gnn_setup()
    _L0_gnn_in = {k: v for k, v in _L0_gnn_all.items() if k in ('gcn_w', 'gcn_b', 'rs_w', 'rs_b', 'ln_g', 'ln_b', 'bn_g', 'bn_b')}
    del _L0_gnn_all

    def _L1_gnn_setup():
        import jax, jax.numpy as jnp
        import numpy as np
        LN_EPS = 1e-05
        N_NODES = 50000
        IN_DIM = 128
        OUT_DIM = 128
        N_EDGES = 12500

        def _ln(x, g, b):
            m = jnp.mean(x, axis=-1, keepdims=True)
            v = jnp.mean((x - m) ** 2, axis=-1, keepdims=True)
            return (x - m) * jax.lax.rsqrt(v + LN_EPS) * g + b
        key = jax.random.key(seed)
        ks = jax.random.split(key, 16)

        def lin(k, fan_in, fan_out):
            return jax.random.normal(k, (fan_in, fan_out), dtype=jnp.float32) / np.sqrt(fan_in)
        x = jax.random.normal(ks[0], (N_NODES, IN_DIM), dtype=jnp.float32)
        edge_index = jax.random.randint(ks[1], (2, N_EDGES), 0, N_NODES, dtype=jnp.int64)
        return {'x': x, 'edge_index': edge_index, 'W1': lin(ks[2], IN_DIM, OUT_DIM), 'b1': jnp.zeros((OUT_DIM,), jnp.float32), 'g1': jnp.ones((OUT_DIM,), jnp.float32), 'bt1': jnp.zeros((OUT_DIM,), jnp.float32), 'We1': lin(ks[3], 2 * OUT_DIM, OUT_DIM), 'be1': jnp.zeros((OUT_DIM,), jnp.float32), 'We2': lin(ks[4], OUT_DIM, 1), 'be2': jnp.zeros((1,), jnp.float32), 'Wn1': lin(ks[5], OUT_DIM, OUT_DIM), 'bn1': jnp.zeros((OUT_DIM,), jnp.float32), 'Wn2': lin(ks[6], OUT_DIM, 1), 'bn2': jnp.zeros((1,), jnp.float32), 'Wg': lin(ks[7], 2 * OUT_DIM, OUT_DIM), 'bg': jnp.zeros((OUT_DIM,), jnp.float32), 'g2': jnp.ones((OUT_DIM,), jnp.float32), 'bt2': jnp.zeros((OUT_DIM,), jnp.float32)}
    _L1_gnn_all = _L1_gnn_setup()
    _L1_gnn_in = {k: v for k, v in _L1_gnn_all.items() if k in ('W1', 'b1', 'g1', 'bt1', 'We1', 'be1', 'We2', 'be2', 'Wn1', 'bn1', 'Wn2', 'bn2', 'Wg', 'bg', 'g2', 'bt2')}
    del _L1_gnn_all
    return {'x': x, 'src': src, 'dst': dst, 'L0_gnn_gcn_w': _L0_gnn_in['gcn_w'], 'L0_gnn_gcn_b': _L0_gnn_in['gcn_b'], 'L0_gnn_rs_w': _L0_gnn_in['rs_w'], 'L0_gnn_rs_b': _L0_gnn_in['rs_b'], 'L0_gnn_ln_g': _L0_gnn_in['ln_g'], 'L0_gnn_ln_b': _L0_gnn_in['ln_b'], 'L0_gnn_bn_g': _L0_gnn_in['bn_g'], 'L0_gnn_bn_b': _L0_gnn_in['bn_b'], 'L1_gnn_W1': _L1_gnn_in['W1'], 'L1_gnn_b1': _L1_gnn_in['b1'], 'L1_gnn_g1': _L1_gnn_in['g1'], 'L1_gnn_bt1': _L1_gnn_in['bt1'], 'L1_gnn_We1': _L1_gnn_in['We1'], 'L1_gnn_be1': _L1_gnn_in['be1'], 'L1_gnn_We2': _L1_gnn_in['We2'], 'L1_gnn_be2': _L1_gnn_in['be2'], 'L1_gnn_Wn1': _L1_gnn_in['Wn1'], 'L1_gnn_bn1': _L1_gnn_in['bn1'], 'L1_gnn_Wn2': _L1_gnn_in['Wn2'], 'L1_gnn_bn2': _L1_gnn_in['bn2'], 'L1_gnn_Wg': _L1_gnn_in['Wg'], 'L1_gnn_bg': _L1_gnn_in['bg'], 'L1_gnn_g2': _L1_gnn_in['g2'], 'L1_gnn_bt2': _L1_gnn_in['bt2']}

def reference(x, src, dst, L0_gnn_gcn_w, L0_gnn_gcn_b, L0_gnn_rs_w, L0_gnn_rs_b, L0_gnn_ln_g, L0_gnn_ln_b, L0_gnn_bn_g, L0_gnn_bn_b, L1_gnn_W1, L1_gnn_b1, L1_gnn_g1, L1_gnn_bt1, L1_gnn_We1, L1_gnn_be1, L1_gnn_We2, L1_gnn_be2, L1_gnn_Wn1, L1_gnn_bn1, L1_gnn_Wn2, L1_gnn_bn2, L1_gnn_Wg, L1_gnn_bg, L1_gnn_g2, L1_gnn_bt2):
    import jax
    import jax.numpy as jnp

    def _L0_gnn_ref(x, edge_index, gcn_w, gcn_b, rs_w, rs_b, ln_g, ln_b, bn_g, bn_b):
        import jax, jax.numpy as jnp
        import numpy as np
        N_NODES = 50000
        N_EDGES = 12500
        D = 128
        EPS_LN = 1e-05
        EPS_BN = 1e-05
        LEAKY_SLOPE = 0.01

        def _layer_norm(x, g, b):
            mu = jnp.mean(x, axis=-1, keepdims=True)
            var = jnp.mean(jnp.square(x - mu), axis=-1, keepdims=True)
            return g * (x - mu) * jax.lax.rsqrt(var + EPS_LN) + b

        def _gcn_conv(x, edge_index, w, b):
            n = x.shape[0]
            loops = jnp.arange(n, dtype=edge_index.dtype)
            row = jnp.concatenate([edge_index[0], loops])
            col = jnp.concatenate([edge_index[1], loops])
            deg = jax.ops.segment_sum(jnp.ones_like(col, dtype=x.dtype), col, num_segments=n)
            dinv = jnp.where(deg > 0, jax.lax.rsqrt(jnp.maximum(deg, 1.0)), 0.0)
            norm = dinv[row] * dinv[col]
            h = x @ w
            msg = h[row] * norm[:, None]
            agg = jax.ops.segment_sum(msg, col, num_segments=n)
            return agg + b
        xl = _layer_norm(x, ln_g, ln_b)
        out = _gcn_conv(xl, edge_index, gcn_w, gcn_b)
        out = out + xl @ rs_w + rs_b
        mu = jnp.mean(out, axis=0)
        var = jnp.mean(jnp.square(out - mu), axis=0)
        out = bn_g * (out - mu) * jax.lax.rsqrt(var + EPS_BN) + bn_b
        out = jnp.where(out >= 0, out, LEAKY_SLOPE * out)
        return out

    def _L1_gnn_ref(x, edge_index, W1, b1, g1, bt1, We1, be1, We2, be2, Wn1, bn1, Wn2, bn2, Wg, bg, g2, bt2):
        import jax, jax.numpy as jnp
        import numpy as np
        LN_EPS = 1e-05
        N_NODES = 50000
        IN_DIM = 128
        OUT_DIM = 128
        N_EDGES = 12500

        def _ln(x, g, b):
            m = jnp.mean(x, axis=-1, keepdims=True)
            v = jnp.mean((x - m) ** 2, axis=-1, keepdims=True)
            return (x - m) * jax.lax.rsqrt(v + LN_EPS) * g + b
        n = x.shape[0]
        h = jax.nn.relu(_ln(x @ W1 + b1, g1, bt1))
        row, col = (edge_index[0], edge_index[1])
        h_src = h[row]
        ef = jnp.concatenate([h_src, h[col]], axis=1)
        edge_weights = jax.nn.sigmoid(jax.nn.relu(ef @ We1 + be1) @ We2 + be2)[:, 0]
        node_weights = jax.nn.sigmoid(jax.nn.relu(h @ Wn1 + bn1) @ Wn2 + bn2)[:, 0]
        _ = node_weights
        aggr = jax.ops.segment_sum(edge_weights[:, None] * h_src, col, num_segments=n)
        gate = jax.nn.sigmoid(jnp.concatenate([h, aggr], axis=-1) @ Wg + bg)
        h_new = gate * aggr + (1.0 - gate) * h
        return _ln(h_new, g2, bt2)
    edge_index = jnp.stack([src, dst])
    x = _layernorm(x + _L0_gnn_ref(x, edge_index, L0_gnn_gcn_w, L0_gnn_gcn_b, L0_gnn_rs_w, L0_gnn_rs_b, L0_gnn_ln_g, L0_gnn_ln_b, L0_gnn_bn_g, L0_gnn_bn_b), axis=-1)
    x = _layernorm(x + _L1_gnn_ref(x, edge_index, L1_gnn_W1, L1_gnn_b1, L1_gnn_g1, L1_gnn_bt1, L1_gnn_We1, L1_gnn_be1, L1_gnn_We2, L1_gnn_be2, L1_gnn_Wn1, L1_gnn_bn1, L1_gnn_Wn2, L1_gnn_bn2, L1_gnn_Wg, L1_gnn_bg, L1_gnn_g2, L1_gnn_bt2), axis=-1)
    return x

_drawn_inputs = setup_inputs


def setup_inputs(seed=0):
    import zlib

    import numpy as np

    out = dict(_drawn_inputs(seed))
    spreads = {'L0_gnn_gcn_b': (0.0, 0.8),
     'L0_gnn_rs_b': (0.0, 0.8),
     'L0_gnn_ln_g': (1.0, 0.2),
     'L0_gnn_ln_b': (0.0, 0.8),
     'L0_gnn_bn_g': (1.0, 0.2),
     'L0_gnn_bn_b': (0.0, 0.1),
     'L1_gnn_b1': (0.0, 0.1),
     'L1_gnn_g1': (1.0, 0.2),
     'L1_gnn_bt1': (0.0, 0.1),
     'L1_gnn_be1': (0.0, 0.8),
     'L1_gnn_bn1': (0.0, 0.1),
     'L1_gnn_bg': (0.0, 0.54),
     'L1_gnn_g2': (1.0, 0.2),
     'L1_gnn_bt2': (0.0, 0.1)}
    factors = {}
    for name, (base, spread) in spreads.items():
        noise = np.random.default_rng([zlib.crc32(name.encode()), seed]).standard_normal(out[name].shape)
        drawn = base * np.exp(spread * noise) if base else spread * noise
        out[name] = jnp.asarray(drawn.astype(out[name].dtype))
    for name, factor in factors.items():
        out[name] = (out[name] * factor).astype(out[name].dtype)
    return out
```

```python
from contextlib import ExitStack

import numpy as np

import concourse.bass as bass
from concourse import mybir

P = 128
D = 128
TILES = 4
UNIT = TILES * P
RING = 4
EPS = 1e-5
SLOPE = 0.01

ALU = mybir.AluOpType
ACT = mybir.ActivationFunctionType
F32 = mybir.dt.float32
I32 = mybir.dt.int32


class Step:

    def __init__(self, lap, slot):
        self.lap, self.slot = lap, slot
        self.u = lap * RING + slot

    def back(self, lag):
        slot = self.slot - lag
        return Step(self.lap + slot // RING, slot % RING)


def over_units(eng, units, stages):
    peeled = RING * (1 + -(-max(lag for lag, _ in stages) // RING))
    assert units % RING == 0 and units >= 2 * peeled
    for u in range(peeled):
        for lag, stage in stages:
            if u >= lag:
                stage(Step(u // RING, u % RING).back(lag))
    with eng.Fori(peeled // RING, units // RING) as lap:
        for slot in range(RING):
            for lag, stage in stages:
                stage(Step(lap, slot).back(lag))
    for u in range(units, units + peeled):
        for lag, stage in stages:
            if u - lag < units:
                stage(Step(u // RING, u % RING).back(lag))


def late(s, n):
    return not (isinstance(s.u, int) and s.u < n)


def over_pairs(eng, chunks, wanted):
    def run(body):
        with eng.If(wanted):
            body(0)
            with eng.Fori(1, chunks // 2) as pair:
                body(pair)
    return run


def not_first(n):
    return not (isinstance(n, int) and n == 0)


class Chain:

    def __init__(self, eng, sem, start):
        self.eng, self.sem, self.value, self.given = eng, sem, start, 0

    def mark(self, instruction):
        instruction.then_inc(self.sem, 1)
        self.given += 1
        self.value = self.value + 1

    def settle(self):
        self.eng.wait_ge(self.sem, self.value)


class Memory:

    def __init__(self, nc, stack, name):
        self.nc, self.stack, self.name, self.semaphores = nc, stack, name, []
        stack.callback(self.clear)

    def sb(self, name, shape, dtype=F32):
        return self.stack.enter_context(self.nc.sbuf_tensor(f"{self.name}_{name}", shape, dtype))

    def ps(self, name, shape, dtype=F32):
        return self.stack.enter_context(self.nc.psum_tensor(f"{self.name}_{name}", shape, dtype))

    def sem(self, name):
        self.semaphores.append(self.nc.alloc_semaphore(name=f"{self.name}_{name}"))
        return self.semaphores[-1]

    def sems(self, name, n):
        return [self.sem(f"{name}{i}") for i in range(n)]

    def clear(self):
        if self.semaphores:
            self.nc.clear_and_free_semaphores(self.semaphores)
            self.nc.all_engine_barrier()


NORM_STEPS = 10


def norm_stats(dve, chain, source, stats, small):
    for t in range(TILES):
        chain.mark(dve.bn_stats(stats[:, t, :], source[:, t, :]))
    chain.settle()
    chain.mark(dve.tensor_tensor(small[:, 0, :], stats[:, :, 1], stats[:, :, 4], ALU.add))
    chain.mark(dve.tensor_tensor(small[:, 1, :], stats[:, :, 1], stats[:, :, 4], ALU.subtract))
    chain.mark(dve.tensor_tensor(small[:, 2, :], stats[:, :, 2], stats[:, :, 5], ALU.add))
    chain.settle()
    chain.mark(dve.tensor_tensor(small[:, 1, :], small[:, 1, :], small[:, 1, :], ALU.mult))
    chain.mark(dve.tensor_scalar(small[:, 2, :], small[:, 2, :], 1.0 / D, EPS, ALU.mult, ALU.add))
    chain.settle()
    chain.mark(dve.scalar_tensor_tensor(small[:, 3, :], small[:, 1, :], 0.25, small[:, 2, :],
                                        ALU.mult, ALU.add))


APPLY_STEPS = 1 + TILES


def norm_apply(dve, chain, source, out, small):
    chain.mark(dve.scalar_tensor_tensor(small[:, 5, :], small[:, 0, :], -0.5, small[:, 4, :],
                                        ALU.mult, ALU.mult))
    chain.settle()
    for t in range(TILES):
        chain.mark(dve.tensor_scalar(out[:, t, :], source[:, t, :], small[:, 4, t:t + 1],
                                     small[:, 5, t:t + 1], ALU.mult, ALU.add))


def spread(column, width):
    return column.unsqueeze(2).to_broadcast([P, column.shape[1], width])


def by_unit(table):
    return table.rearrange("(u t p) f -> u p t f", t=TILES, p=P)


def build_constants(nc, memory, weights):
    m = Memory(nc, memory.stack, "c")
    ident = m.sb("ident", [P, P])
    earlier = m.sb("earlier", [P, P])
    trash = m.sb("trash", [P, 1])
    power = m.sb("power", [P, TILES])
    lane = m.sb("lane", [P, P])
    ones = m.sb("ones", [P, 1])
    held = {n: m.sb(n, [P, a.shape[1]]) for n, a in weights.items() if len(a.shape) == 2 and a.shape[0] == P}
    loaded, made = m.sem("loaded"), m.sem("made")
    for n, a in weights.items():
        if len(a.shape) == 1:
            held[n] = m.sb(n, [P, 1])
        elif a.shape[0] == 2 * P:
            held[n] = m.sb(n, [P, 2, a.shape[1]])
    with nc.Block() as block:
        @block.sync
        def _(sp):
            for n, a in weights.items():
                if len(a.shape) == 1 and a.shape[0] == 1:
                    src = a.rearrange("(a b) -> a b", a=1).to_broadcast([P, 1])
                elif len(a.shape) == 1:
                    src = a.rearrange("(a b) -> a b", b=1)
                elif a.shape[0] == 2 * P:
                    src = a.rearrange("(h p) f -> p h f", h=2)
                else:
                    src = a
                sp.dma_start(held[n][:], src).then_inc(loaded, 16)
            sp.wait_ge(loaded, 16 * len(weights))

        @block.vector
        def _(dve):
            dve.memset(power[:], -0.5)
            dve.memset(ones[:], 1.0)

        @block.gpsimd
        def _(pool):
            pool.memset(ident[:], 1.0).then_inc(made, 1)
            pool.memset(earlier[:], 1.0).then_inc(made, 1)
            pool.iota(trash[:], [[0, 1]], base=0, channel_multiplier=1,
                      allow_small_or_imprecise_dtypes=True).then_inc(made, 1)
            pool.iota(lane[:], [[1, P]], base=0, channel_multiplier=0, allow_small_or_imprecise_dtypes=True)
            pool.wait_ge(made, 3)
            pool.affine_select(out=ident[:], in_=ident[:], compare_op=ALU.is_equal, fill=0.0,
                               base=0, pattern=[[1, P]], channel_multiplier=-1)
            pool.affine_select(out=earlier[:], in_=earlier[:], compare_op=ALU.is_gt, fill=0.0,
                               base=0, pattern=[[-1, P]], channel_multiplier=1)
    return dict(held, ident=ident, earlier=earlier, trash=trash, power=power, lane=lane, ones=ones)


WINDOW_ROWS = 5
HALF = 64
WINDOW = WINDOW_ROWS * HALF
SLOTS = P
SRC_BITS = 17


def index_edges(nc, k, ends, heads, line, rel_rows, tiles):
    rows = heads.shape[0]
    per = next(q for q in range(P, 0, -1) if tiles % q == 0)
    batches = tiles // per
    span = line.shape[1] // P
    ROUND = 2 * batches + 1
    with ExitStack() as stack:
        m = Memory(nc, stack, "idx")
        head = m.sb("head", [per, rows], I32)
        below = m.sb("below", [per, rows])
        base = m.sb("base", [per, batches])
        start = m.sb("start", [per, batches])
        row_of = m.sb("row_of", [per, batches, WINDOW_ROWS], I32)
        window = m.sb("window", [per, batches, WINDOW_ROWS, 2 * HALF], I32)
        shape = [per, batches, WINDOW_ROWS, HALF]
        dstw, srcw, inside, after, loop, key = (m.sb(n, [per, batches, WINDOW]) for n in ("dstw", "srcw", "inside", "after", "loop", "key"))
        count = m.sb("count", [per, 4, batches])
        bad = m.sb("bad", [P, 4])
        top = m.sb("top", [per, batches, 8])
        keys = m.sb("keys", [per, batches, SLOTS])
        keys_int = m.sb("keys_int", [per, batches, SLOTS], I32)
        rel_out = m.sb("rel_out", [per, batches, SLOTS])
        slot_key = m.sb("slot_key", [P, batches, per], I32)
        order = m.sb("order", [P, 2, span], I32)
        orderf = m.sb("orderf", [P, span])
        turned = m.ps("turned", [P, -(-batches // 4) * 4, P])
        wrong = m.ps("wrong", [P, 512])
        loaded, based, started, gathered, own, round_own, passed, keys_turned, summed, rel_stored = (
            m.sem(n) for n in ("loaded", "based", "started", "gathered", "own", "round_own", "passed", "keys_turned", "summed", "rel_stored"))
        with nc.Block() as block:
            @block.sync
            def _(sp):
                sp.dma_start(head[:], heads.rearrange("(a r) -> a r", a=1).to_broadcast([per, rows])).then_inc(loaded, 16)
                for i in range(2):
                    sp.dma_start(order[:, i, :], line[i].rearrange("(p e) -> p e", p=P)).then_inc(loaded, 16)
                sp.wait_ge(summed, 1)
                sp.dma_start(rel_rows.rearrange("(b q) s -> q b s", q=per), rel_out[:]).then_inc(rel_stored, 16)
                sp.wait_ge(rel_stored, 16)

            @block.gpsimd
            def _(pool):
                pool.iota(base[:], [[per * P, batches]], base=0, channel_multiplier=P,
                          allow_small_or_imprecise_dtypes=True).then_inc(based, 1)
                pool.wait_ge(started, 1)
                for b in range(batches):
                    for r in range(WINDOW_ROWS):
                        pool.indirect_dma_start(out=window[:, b, r, :], out_offset=None, in_=ends,
                                                in_offset=bass.IndirectOffsetOnAxis(ap=row_of[:, b, r:r + 1], axis=0)
                                                ).then_inc(gathered, 16)

            @block.vector
            def _(dve):
                chain = Chain(dve, own, 0)

                def do(*instructions):
                    for instruction in instructions:
                        chain.mark(instruction)
                    chain.settle()

                dve.wait_ge(loaded, 48)
                dve.wait_ge(based, 1)
                do(dve.memset(bad[:], 0.0))
                do(dve.tensor_tensor(orderf[:], order[:, 1, :], order[:, 0, :], ALU.is_lt))
                do(dve.tensor_reduce(bad[:, 3:4], orderf[:], mybir.AxisListType.X, ALU.add))
                for b in range(batches):
                    do(dve.tensor_scalar(below[:], head[:], base[:, b:b + 1], None, ALU.is_lt))
                    do(dve.tensor_reduce(start[:, b:b + 1], below[:], mybir.AxisListType.X, ALU.add))
                do(dve.tensor_scalar(start[:], start[:], -1.0, 0.0, ALU.add, ALU.max))
                for r in range(WINDOW_ROWS):
                    last = dve.tensor_scalar(row_of[:, :, r], start[:], float(r), None, ALU.add)
                    chain.mark(last)
                chain.settle()
                dve.sem_inc(started, 1)
                dve.wait_ge(gathered, 16 * batches * WINDOW_ROWS)
                split = lambda ap: ap.rearrange("q b (r e) -> q b r e", e=HALF)
                for b in range(batches):
                    chain.mark(dve.tensor_copy(dstw[:, b].rearrange("q (r e) -> q r e", e=HALF), window[:, b, :, 0:HALF]))
                    chain.mark(dve.tensor_copy(srcw[:, b].rearrange("q (r e) -> q r e", e=HALF), window[:, b, :, HALF:2 * HALF]))
                chain.settle()
                do(dve.memset(after[:, :, WINDOW - 1:WINDOW], 0.0),
                   dve.tensor_tensor(after[:, :, 0:WINDOW - 1], dstw[:, :, 1:WINDOW], dstw[:, :, 0:WINDOW - 1], ALU.not_equal),
                   dve.tensor_tensor(loop[:], srcw[:], dstw[:], ALU.is_equal))
                do(dve.tensor_tensor(dstw[:], dstw[:], base[:].unsqueeze(2).to_broadcast([per, batches, WINDOW]), ALU.subtract))
                do(dve.tensor_tensor(loop[:], loop[:], after[:], ALU.mult))
                do(dve.tensor_scalar(inside[:], dstw[:], 0.0, None, ALU.is_ge),
                   dve.tensor_scalar(after[:], dstw[:], float(P), None, ALU.is_lt),
                   dve.scalar_tensor_tensor(key[:], dstw[:], float(1 << SRC_BITS), srcw[:], ALU.mult, ALU.add),
                   dve.tensor_scalar(count[:, 2, :], dstw[:, :, WINDOW - 1], float(P), None, ALU.is_lt))
                do(dve.tensor_tensor(inside[:], inside[:], after[:], ALU.mult))
                do(dve.tensor_tensor(loop[:], loop[:], inside[:], ALU.mult))
                do(dve.tensor_tensor(inside[:], inside[:], loop[:], ALU.subtract),
                   dve.tensor_reduce(count[:, 0, :], loop[:], mybir.AxisListType.X, ALU.add))
                do(dve.scalar_tensor_tensor(key[:], key[:], 1.0, inside[:], ALU.add, ALU.mult),
                   dve.tensor_reduce(count[:, 1, :], inside[:], mybir.AxisListType.X, ALU.add))
                do(dve.tensor_scalar(key[:], key[:], -1.0, None, ALU.add),
                   dve.tensor_scalar(count[:, 0, :], count[:, 0, :], float(P), None, ALU.not_equal),
                   dve.tensor_scalar(count[:, 1, :], count[:, 1, :], float(SLOTS), None, ALU.is_gt))
                do(dve.tensor_reduce(bad[0:per, 0:3], count[:, 0:3, :], mybir.AxisListType.X, ALU.add))

                def take(r):
                    start_of = r * ROUND
                    if not_first(r):
                        dve.wait_ge(round_own, start_of)
                        dve.sem_inc(passed, 1)
                    for b in range(batches):
                        dve.max(top[:, b, :], key[:, b, :]).then_inc(round_own, 1)
                    dve.wait_ge(round_own, start_of + batches)
                    dve.tensor_copy(keys[:, :, bass.ds(r * 8, 8)], top[:]).then_inc(round_own, 1)
                    for b in range(batches):
                        dve.match_replace(key[:, b, :], top[:, b, :], key[:, b, :], -1.0).then_inc(round_own, 1)

                take(0)
                with dve.Fori(1, SLOTS // 8) as r:
                    take(r)
                dve.wait_ge(round_own, SLOTS // 8 * ROUND)
                do(dve.tensor_copy(keys_int[:], keys[:]))
                do(dve.tensor_scalar(keys_int[:], keys_int[:], SRC_BITS, None, ALU.arith_shift_right))
                dve.tensor_copy(rel_out[:], keys_int[:]).then_inc(summed, 1)
                dve.wait_ge(keys_turned, 2)
                shaped = lambda ap: ap.rearrange("p (b q) -> p b q", q=per)
                do(dve.tensor_copy(slot_key[:], turned[:, 0:batches, 0:per]),
                   dve.tensor_scalar(k["regular"][0:1, 0:1], wrong[0:1, 0:1], 0.0, None, ALU.is_equal),
                   dve.tensor_scalar(k["regular"][0:1, 1:2], wrong[0:1, 0:1], 0.0, None, ALU.not_equal))
                do(dve.tensor_scalar(shaped(k["slot_src"][:]), slot_key[:], (1 << SRC_BITS) - 1, None, ALU.bitwise_and),
                   dve.tensor_scalar(slot_key[:], slot_key[:], SRC_BITS, None, ALU.arith_shift_right))
                do(dve.tensor_copy(shaped(k["slot_rel"][:]), slot_key[:]))

            @block.tensor
            def _(pe):
                pe.wait_ge(summed, 1)
                for b in range(batches):
                    last = pe.transpose(turned[:, b, 0:per], keys[:, b, :], k["ident"][0:per, 0:per])
                last.then_inc(keys_turned, 1)
                for c in range(4):
                    last = pe.matmul(wrong[0:1, 0:1], bad[:, c:c + 1], k["ones"][:], start=(c == 0), stop=(c == 3))
                last.then_inc(keys_turned, 1)


def count_slots(nc, k, tiles):
    with ExitStack() as stack:
        m = Memory(nc, stack, "cs")
        hot = m.sb("hot", [P, 2, 8, P], mybir.dt.bfloat16)
        one = m.sb("one", [P, 1], mybir.dt.bfloat16)
        rel = k["slot_rel"]
        sums = m.ps("sums", [P, -(-tiles // 512) * 512])
        hot_ready, summed, ready = m.sem("hot_ready"), m.sem("summed"), m.sem("ready")
        groups = tiles // 8
        with nc.Block() as block:
            @block.vector
            def _(dve):
                with dve.If(k["is_regular"]):
                    dve.memset(one[:], 1.0).then_inc(ready, 1)
                    for g in range(groups):
                        if g >= 2:
                            dve.wait_ge(summed, g - 1)
                        dve.tensor_tensor(hot[:, g % 2], k["lane"][:].unsqueeze(1).to_broadcast([P, 8, P]),
                                          spread(rel[:, g * 8:g * 8 + 8], P), ALU.is_equal).then_inc(hot_ready, 1)
                    dve.wait_ge(summed, groups)
                    dve.tensor_scalar(k["edges"][:], sums[:, 0:tiles], 1.0, None, ALU.add)

            @block.tensor
            def _(pe):
                with pe.If(k["is_regular"]):
                    pe.wait_ge(ready, 1)
                    for g in range(groups):
                        pe.wait_ge(hot_ready, g + 1)
                        for t in range(8):
                            last = pe.matmul(sums[:, g * 8 + t:g * 8 + t + 1], hot[:, g % 2, t, :], one[:], start=True, stop=True)
                        last.then_inc(summed, 1)


def clear_tables(nc, k, tables):
    WIDTH = 8 * D
    with ExitStack() as stack:
        m = Memory(nc, stack, "clear")
        zeros = m.sb("zeros", [P, WIDTH])
        cleared, stored = m.sem("cleared"), m.sem("stored")
        with nc.Block() as block:
            @block.vector
            def _(dve):
                dve.memset(zeros[:], 0.0).then_inc(cleared, 1)

            @block.sync
            def _(sp):
                with sp.If(k["irregular"]):
                    sp.wait_ge(cleared, 1)
                    stores = 0
                    for table in tables:
                        flat = table.rearrange("a b -> (a b)")
                        size = P * WIDTH
                        whole, rest = divmod(flat.shape[0], size)
                        for i in range(whole + (rest > 0)):
                            n = size if i < whole else rest
                            sp.dma_start(flat[i * size:i * size + n].rearrange("(p f) -> p f", p=P),
                                         zeros[:, 0:n // P]).then_inc(stored, 16)
                        stores += whole + (rest > 0)
                    sp.wait_ge(stored, 16 * stores)


def count_edges(nc, k, counts, chunks, rows, tiles):
    dst, place = k["dst"], k["place"]
    with ExitStack() as stack:
        m = Memory(nc, stack, "cnt")
        dstf = m.sb("dstf", [P, 2])
        same = m.sb("same", [P, 2, P])
        ranks = m.sb("ranks", [P, 2, P])
        small = m.sb("small", [P, 2, 4])
        total = m.sb("total", [P, 2])
        target = m.sb("target", [P, 2], I32)
        row = m.ps("row", [P, 2, 512])
        dst_ready, row_ready, own, fetched = (m.sem(n) for n in ("dst_ready", "row_ready", "own", "fetched"))
        added = m.sems("added", 2)
        passed = m.sem("passed")
        with nc.Block() as block:
            @block.vector
            def _(dve):
                @over_pairs(dve, chunks, k["irregular"])
                def _(pair):
                    for b in range(2):
                        c = pair * 2 + b
                        chain = Chain(dve, own, c * 8)
                        if not_first(pair):
                            dve.wait_ge(added[b], pair * 16)
                        dve.tensor_copy(dstf[:, b:b + 1], dst[:, bass.ds(c, 1)]).then_inc(dst_ready, 1)
                        dve.wait_ge(row_ready, c + 1)
                        dve.wait_ge(dst_ready, c + 1)
                        chain.mark(dve.tensor_scalar(same[:, b, :], row[:, b, 0:P], dstf[:, b:b + 1], None, ALU.is_equal))
                        chain.settle()
                        chain.mark(dve.tensor_reduce(total[:, b:b + 1], same[:, b, :], mybir.AxisListType.X, ALU.add))
                        chain.mark(dve.tensor_tensor(ranks[:, b, :], same[:, b, :], k["earlier"][:], ALU.mult))
                        chain.settle()
                        chain.mark(dve.tensor_reduce(small[:, b, 0:1], ranks[:, b, :], mybir.AxisListType.X, ALU.max))
                        chain.mark(dve.scalar_tensor_tensor(small[:, b, 1:2], k["trash"][:], float(rows), dstf[:, b:b + 1], ALU.add, ALU.subtract))
                        chain.settle()
                        chain.mark(dve.tensor_tensor(small[:, b, 2:3], small[:, b, 0:1], small[:, b, 1:2], ALU.mult))
                        chain.settle()
                        chain.mark(dve.tensor_tensor(target[:, b:b + 1], small[:, b, 2:3], dstf[:, b:b + 1], ALU.add))
                        chain.settle()
                        chain.mark(dve.tensor_copy(place[:, bass.ds(c, 1)], target[:, b:b + 1]))

            @block.tensor
            def _(pe):
                @over_pairs(pe, chunks, k["irregular"])
                def _(pair):
                    for b in range(2):
                        c = pair * 2 + b
                        pe.wait_ge(dst_ready, c + 1)
                        pe.matmul(row[:, b, 0:P], dstf[:, b:b + 1].to_broadcast([P, P]), k["ident"][:],
                                  start=True, stop=True).then_inc(row_ready, 1)

            @block.gpsimd
            def _(pool):
                @over_pairs(pool, chunks, k["irregular"])
                def _(pair):
                    for b in range(2):
                        pool.wait_ge(own, (pair * 2 + b + 1) * 8)
                        if b or not_first(pair):
                            pool.wait_ge(added[1 - b], (pair + b) * 16)
                        pool.sem_inc(passed, 1)
                        pool.indirect_dma_start(
                            out=counts, out_offset=bass.IndirectOffsetOnAxis(ap=target[:, b:b + 1], axis=0),
                            in_=total[:, b:b + 1], in_offset=None, compute_op=ALU.add).then_inc(added[b], 16)
                with pool.If(k["irregular"]):
                    for b in range(2):
                        pool.wait_ge(added[b], chunks // 2 * 16)

            @block.sync
            def _(sp):
                with sp.If(k["irregular"]):
                    for b in range(2):
                        sp.wait_ge(added[b], chunks // 2 * 16)
                    sp.dma_start(k["edges"][:], counts[0:tiles * P, :].rearrange("(t p) o -> p (t o)", p=P),
                                 allow_slow_non_contiguous=True).then_inc(fetched, 16)
                    sp.wait_ge(fetched, 16)


def degrees(nc, k, tiles):
    with ExitStack() as stack:
        m = Memory(nc, stack, "deg")
        counted, rooted = m.sem("counted"), m.sem("rooted")
        with nc.Block() as block:
            @block.vector
            def _(dve):
                dve.tensor_scalar(k["edges"][:], k["edges"][:], 1.0, 1.0, ALU.add, ALU.max).then_inc(counted, 1)
                dve.wait_ge(rooted, 1)
                dve.reciprocal(k["dinv"][:], k["root"][:])

            @block.scalar
            def _(act):
                act.wait_ge(counted, 1)
                act.activation(k["root"][:], k["edges"][:], ACT.Sqrt).then_inc(rooted, 1)


def make_messages(nc, k, x, y, units):
    X, Y = by_unit(x), by_unit(y)
    with ExitStack() as stack:
        m = Memory(nc, stack, "msg")
        x_in = m.sb("x_in", [P, RING, TILES, D])
        stats = m.sb("stats", [P, 2, TILES, 6])
        small = m.sb("small", [P, 2, 6, TILES])
        xn = m.sb("xn", [P, 2, TILES, D])
        xlT = m.sb("xlT", [P, 2, UNIT])
        y_out = m.sb("y_out", [P, RING, TILES, D])
        turned = m.ps("turned", [P, 2, UNIT])
        back = m.ps("back", [P, 2, UNIT])
        x_loaded, y_stored = m.sems("x_loaded", RING), m.sems("y_stored", RING)
        stat_own, apply_own, rstd_ready, turned_ready, xlT_ready, back_ready, y_ready = (
            m.sem(n) for n in ("stat_own", "apply_own", "rstd_ready", "turned_ready", "xlT_ready", "back_ready", "y_ready"))
        with nc.Block() as block:
            @block.sync
            def _(sp):
                def load(s):
                    if late(s, RING):
                        sp.wait_ge(apply_own, (s.u - RING + 1) * APPLY_STEPS)
                    sp.dma_start(x_in[:, s.slot], X[s.u]).then_inc(x_loaded[s.slot], 16)

                def store(s):
                    sp.wait_ge(y_ready, s.u + 1)
                    sp.dma_start(Y[s.u], y_out[:, s.slot]).then_inc(y_stored[s.slot], 16)

                over_units(sp, units, [(4, store), (0, load)])
                for q in y_stored:
                    sp.wait_ge(q, units // RING * 16)

            @block.vector
            def _(dve):
                def statistics(s):
                    b = s.slot % 2
                    dve.wait_ge(x_loaded[s.slot], (s.lap + 1) * 16)
                    norm_stats(dve, Chain(dve, stat_own, s.u * NORM_STEPS), x_in[:, s.slot], stats[:, b], small[:, b])

                def apply(s):
                    b = s.slot % 2
                    dve.wait_ge(rstd_ready, s.u + 1)
                    if late(s, 2):
                        dve.wait_ge(turned_ready, s.u - 1)
                    norm_apply(dve, Chain(dve, apply_own, s.u * APPLY_STEPS), x_in[:, s.slot], xn[:, b], small[:, b])

                def scale(s):
                    b = s.slot % 2
                    dve.wait_ge(back_ready, s.u + 1)
                    if late(s, RING):
                        dve.wait_ge(y_stored[s.slot], s.lap * 16)
                    dve.tensor_tensor(y_out[:, s.slot], back[:, b].rearrange("p (t f) -> p t f", t=TILES),
                                      spread(k["dinv"][:, bass.ds(s.u * TILES, TILES)], D), ALU.mult).then_inc(y_ready, 1)

                over_units(dve, units, [(3, scale), (1, apply), (0, statistics)])

            @block.gpsimd
            def _(pool):
                def root(s):
                    b = s.slot % 2
                    pool.wait_ge(stat_own, (s.u + 1) * NORM_STEPS)
                    pool.tensor_tensor(small[:, b, 4, :], small[:, b, 3, :], k["power"][:], ALU.pow).then_inc(rstd_ready, 1)

                over_units(pool, units, [(0, root)])

            @block.tensor
            def _(pe):
                def turn(s):
                    b = s.slot % 2
                    pe.wait_ge(apply_own, (s.u + 1) * APPLY_STEPS)
                    if late(s, 2):
                        pe.wait_ge(xlT_ready, s.u - 1)
                    for t in range(TILES):
                        last = pe.transpose(turned[:, b, t * P:(t + 1) * P], xn[:, b, t, :], k["ident"][:])
                    last.then_inc(turned_ready, 1)

                def turn_back(s):
                    b = s.slot % 2
                    pe.wait_ge(xlT_ready, s.u + 1)
                    if late(s, 2):
                        pe.wait_ge(y_ready, s.u - 1)
                    for t in range(TILES):
                        last = pe.transpose(back[:, b, t * P:(t + 1) * P], xlT[:, b, t * P:(t + 1) * P], k["ident"][:])
                    last.then_inc(back_ready, 1)

                over_units(pe, units, [(1, turn_back), (0, turn)])

            @block.scalar
            def _(act):
                def affine(s):
                    b = s.slot % 2
                    act.wait_ge(turned_ready, s.u + 1)
                    if late(s, 2):
                        act.wait_ge(back_ready, s.u - 1)
                    act.activation(xlT[:, b], turned[:, b], ACT.Identity, bias=k["ln_b"][:], scale=k["ln_g"][:]).then_inc(xlT_ready, 1)

                over_units(act, units, [(0, affine)])


def add_messages(nc, k, y, sums, chunks, edge_net=None):
    src, dst, place = k["src"], k["dst"], k["place"]
    with ExitStack() as stack:
        m = Memory(nc, stack, "add1" if edge_net is None else "add2")
        dstf = m.sb("dstf", [P, 2])
        src_row, dst_row, target = (m.sb(n, [P, 2], I32) for n in ("src_row", "dst_row", "target"))
        same = m.sb("same", [P, 2, P])
        from_src = m.sb("from_src", [P, 2, D])
        from_dst = m.sb("from_dst", [P, 2, D])
        bothT = m.sb("bothT", [P, 2, 2, P])
        hidden = m.sb("hidden", [P, 2, P])
        weight = m.sb("weight", [P, 2])
        message = m.sb("message", [P, 2, D])
        out = m.sb("out", [P, 2, D])
        row = m.ps("row", [P, 2, 512])
        total = m.ps("total", [P, 2, 512])
        turned = m.ps("turned", [P, 512])
        pre = m.ps("pre", [P, 512])
        dots = m.ps("dots", [P, 512])
        (index_ready, row_ready, same_ready, total_ready, out_ready, turned_ready, bothT_ready, pre_ready,
         hidden_ready, dot_ready, weight_ready, message_ready) = (
            m.sem(n) for n in ("index_ready", "row_ready", "same_ready", "total_ready", "out_ready", "turned_ready",
                               "bothT_ready", "pre_ready", "hidden_ready", "dot_ready", "weight_ready", "message_ready"))
        src_in, dst_in, added = m.sems("src_in", 2), m.sems("dst_in", 2), m.sems("added", 2)
        passed = m.sem("passed")

        def over_chunks(eng, body):
            @over_pairs(eng, chunks, k["irregular"])
            def _(pair):
                for b in range(2):
                    body(pair, b, pair * 2 + b)

        with nc.Block() as block:
            @block.vector
            def _(dve):
                def chunk(pair, b, c):
                    if not_first(pair):
                        dve.wait_ge(added[b], pair * 16)
                    dve.tensor_copy(dstf[:, b:b + 1], dst[:, bass.ds(c, 1)]).then_inc(index_ready, 1)
                    dve.tensor_copy(src_row[:, b:b + 1], src[:, bass.ds(c, 1)]).then_inc(index_ready, 1)
                    dve.tensor_copy(dst_row[:, b:b + 1], dst[:, bass.ds(c, 1)]).then_inc(index_ready, 1)
                    dve.tensor_copy(target[:, b:b + 1], place[:, bass.ds(c, 1)]).then_inc(index_ready, 1)
                    dve.wait_ge(row_ready, c + 1)
                    dve.wait_ge(index_ready, (c + 1) * 4)
                    dve.tensor_scalar(same[:, b, :], row[:, b, 0:P], dstf[:, b:b + 1], None, ALU.is_equal).then_inc(same_ready, 1)
                    if edge_net is not None:
                        dve.wait_ge(weight_ready, c + 1)
                        dve.wait_ge(src_in[b], (pair + 1) * 16)
                        dve.tensor_scalar(message[:, b, :], from_src[:, b, :], weight[:, b:b + 1], None, ALU.mult).then_inc(message_ready, 1)

                over_chunks(dve, chunk)

            @block.gpsimd
            def _(pool):
                @over_pairs(pool, chunks, k["irregular"])
                def _(pair):
                    for b in range(2):
                        pool.wait_ge(index_ready, (pair * 2 + b + 1) * 4)
                        pool.sem_inc(passed, 1)
                        pool.indirect_dma_start(out=from_src[:, b, :], out_offset=None, in_=y,
                                                in_offset=bass.IndirectOffsetOnAxis(ap=src_row[:, b:b + 1], axis=0)
                                                ).then_inc(src_in[b], 16)
                        if edge_net is not None:
                            pool.indirect_dma_start(out=from_dst[:, b, :], out_offset=None, in_=y,
                                                    in_offset=bass.IndirectOffsetOnAxis(ap=dst_row[:, b:b + 1], axis=0)
                                                    ).then_inc(dst_in[b], 16)
                    for b in range(2):
                        pool.wait_ge(out_ready, pair * 2 + b + 1)
                        if b or not_first(pair):
                            pool.wait_ge(added[1 - b], (pair + b) * 16)
                        pool.sem_inc(passed, 1)
                        pool.indirect_dma_start(
                            out=sums, out_offset=bass.IndirectOffsetOnAxis(ap=target[:, b:b + 1], axis=0),
                            in_=out[:, b, :], in_offset=None, compute_op=ALU.add).then_inc(added[b], 16)
                with pool.If(k["irregular"]):
                    for b in range(2):
                        pool.wait_ge(added[b], chunks // 2 * 16)

            @block.tensor
            def _(pe):
                def chunk(pair, b, c):
                    pe.wait_ge(index_ready, c * 4 + 1)
                    pe.matmul(row[:, b, 0:P], dstf[:, b:b + 1].to_broadcast([P, P]), k["ident"][:],
                              start=True, stop=True).then_inc(row_ready, 1)
                    pe.wait_ge(src_in[b], (pair + 1) * 16)
                    if edge_net is not None:
                        pe.wait_ge(dst_in[b], (pair + 1) * 16)
                        if not_first(c):
                            pe.wait_ge(bothT_ready, c)
                        pe.transpose(turned[:, 0:P], from_src[:, b, :], k["ident"][:])
                        pe.transpose(turned[:, P:2 * P], from_dst[:, b, :], k["ident"][:]).then_inc(turned_ready, 1)
                        pe.wait_ge(bothT_ready, c + 1)
                        if not_first(c):
                            pe.wait_ge(hidden_ready, c)
                        for half in range(2):
                            last = pe.matmul(pre[:, 0:P], edge_net["We1"][:, half, :], bothT[:, b, half, :],
                                             start=(half == 0), stop=(half == 1))
                        last.then_inc(pre_ready, 1)
                        pe.wait_ge(hidden_ready, c + 1)
                        if not_first(c):
                            pe.wait_ge(weight_ready, c)
                        pe.matmul(dots[:, 0:1], hidden[:, b, :], edge_net["We2"][:], start=True, stop=True).then_inc(dot_ready, 1)
                        pe.wait_ge(message_ready, c + 1)
                    pe.wait_ge(same_ready, c + 1)
                    pe.matmul(total[:, b, 0:D], same[:, b, :], from_src[:, b, :] if edge_net is None else message[:, b, :],
                              start=True, stop=True).then_inc(total_ready, 1)

                over_chunks(pe, chunk)

            @block.scalar
            def _(act):
                def chunk(pair, b, c):
                    if edge_net is not None:
                        act.wait_ge(turned_ready, c + 1)
                        act.activation(bothT[:, b].rearrange("p a b -> p (a b)"), turned[:, 0:2 * P], ACT.Copy).then_inc(bothT_ready, 1)
                        act.wait_ge(pre_ready, c + 1)
                        act.activation(hidden[:, b, :], pre[:, 0:P], ACT.Relu, bias=edge_net["be1"][:]).then_inc(hidden_ready, 1)
                        act.wait_ge(dot_ready, c + 1)
                        act.activation(weight[:, b:b + 1], dots[:, 0:1], ACT.Sigmoid, bias=edge_net["be2"][:]).then_inc(weight_ready, 1)
                    act.wait_ge(total_ready, c + 1)
                    act.activation(out[:, b, :], total[:, b, 0:D], ACT.Copy).then_inc(out_ready, 1)

                over_chunks(act, chunk)


def convolve(nc, k, y, sums, outT, units, nodes):
    Y, SUMS = by_unit(y), by_unit(sums[0:units * UNIT, :])
    STAT_OWN = 4
    last_valid = nodes - (units - 1) * UNIT
    with ExitStack() as stack:
        m = Memory(nc, stack, "conv")
        y_in = m.sb("y_in", [P, RING, TILES, D])
        s_in = m.sb("s_in", [P, RING, TILES, D])
        gathered = m.sb("gathered", [P, 2, TILES, D])
        rows = m.sb("rows", [P, RING, TILES, D])
        hot = m.sb("hot", [P, 2, TILES, P])
        slot_src = m.sb("slot_src", [P, RING, TILES], I32)
        sum_ps = m.ps("sum_ps", [P, 2, UNIT])
        rows_loaded = m.sems("rows_loaded", RING)
        (rows_clear, slots_ready, hot_ready, sums_ready, passed) = (
            m.sem(n) for n in ("rows_clear", "slots_ready", "hot_ready", "sums_ready", "passed"))
        own_x = m.sb("own_x", [P, 2, TILES, D])
        gT = m.sb("gT", [P, 2, UNIT])
        xT = m.sb("xT", [P, 2, UNIT])
        o_out = m.sb("o_out", [P, RING, UNIT])
        stats = m.sb("stats", [P, units, 6])
        bn = m.sb("bn", [P, 8])
        g_turned, x_turned, o_ps = (m.ps(n, [P, 2, UNIT]) for n in ("g_turned", "x_turned", "o_ps"))
        y_loaded, s_loaded, o_stored = (m.sems(n, RING) for n in ("y_loaded", "s_loaded", "o_stored"))
        summed, scaled, turned, copied, product, o_ready, measured, bn_own, bn_var, bn_rstd = (
            m.sem(n) for n in ("summed", "scaled", "turned", "copied", "product", "o_ready", "measured", "bn_own", "bn_var", "bn_rstd"))
        with nc.Block() as block:
            @block.sync
            def _(sp):
                def load(s):
                    if late(s, RING):
                        sp.wait_ge(scaled, (s.u - RING + 1) * 2)
                    sp.dma_start(y_in[:, s.slot], Y[s.u]).then_inc(y_loaded[s.slot], 16)

                def load_both(s):
                    load(s)
                    sp.dma_start(s_in[:, s.slot], SUMS[s.u]).then_inc(s_loaded[s.slot], 16)

                def store(s):
                    sp.wait_ge(o_ready, s.u + 1)
                    sp.dma_start(outT[:, bass.ds(s.u * UNIT, UNIT)], o_out[:, s.slot]).then_inc(o_stored[s.slot], 16)

                with sp.If(k["is_regular"]):
                    over_units(sp, units, [(4, store), (0, load)])
                with sp.If(k["irregular"]):
                    over_units(sp, units, [(4, store), (0, load_both)])
                for q in o_stored:
                    sp.wait_ge(q, units // RING * 16)

            @block.vector
            def _(dve):
                def one_hot(s):
                    if late(s, 2):
                        dve.wait_ge(sums_ready, s.u - 1)
                    dve.tensor_tensor(hot[:, s.slot % 2], k["lane"][:].unsqueeze(1).to_broadcast([P, TILES, P]),
                                      spread(k["slot_rel"][:, bass.ds(s.u * TILES, TILES)], P), ALU.is_equal).then_inc(hot_ready, 1)

                def scale_made(s):
                    dve.wait_ge(y_loaded[s.slot], (s.lap + 1) * 16)
                    dve.wait_ge(sums_ready, s.u + 1)
                    if late(s, RING):
                        dve.wait_ge(scaled, (s.u - RING + 1) * 2)
                    dve.scalar_tensor_tensor(s_in[:, s.slot], y_in[:, s.slot], 2.0,
                                             sum_ps[:, s.slot % 2].rearrange("p (t f) -> p t f", t=TILES), ALU.mult, ALU.add).then_inc(summed, 1)
                    scale(s)

                def scale_read(s):
                    dve.wait_ge(y_loaded[s.slot], (s.lap + 1) * 16)
                    dve.wait_ge(s_loaded[s.slot], (s.lap + 1) * 16)
                    dve.tensor_tensor(s_in[:, s.slot], s_in[:, s.slot], y_in[:, s.slot], ALU.add).then_inc(summed, 1)
                    scale(s)

                def scale(s):
                    b = s.slot % 2
                    if late(s, 2):
                        dve.wait_ge(turned, s.u - 1)
                    dve.tensor_tensor(own_x[:, b], y_in[:, s.slot], spread(k["root"][:, bass.ds(s.u * TILES, TILES)], D),
                                      ALU.mult).then_inc(scaled, 1)
                    dve.wait_ge(summed, s.u + 1)
                    dve.tensor_tensor(gathered[:, b], s_in[:, s.slot], spread(k["dinv"][:, bass.ds(s.u * TILES, TILES)], D),
                                      ALU.mult).then_inc(scaled, 1)

                def measure(s):
                    dve.wait_ge(o_ready, s.u + 1)
                    dve.bn_stats(stats[:, bass.ds(s.u, 1), :].rearrange("p a b -> p (a b)"), o_out[:, s.slot]).then_inc(measured, 1)

                with dve.If(k["is_regular"]):
                    dve.memset(rows[:], 0.0).then_inc(rows_clear, 1)
                    over_units(dve, units, [(0, one_hot), (2, measure), (1, scale_made)])
                with dve.If(k["irregular"]):
                    over_units(dve, units, [(2, measure), (0, scale_read)])
                dve.wait_ge(measured, units)
                dve.bn_stats(stats[:, units - 1, :], o_out[:, RING - 1, 0:last_valid]).then_inc(bn_own, 1)
                dve.wait_ge(bn_own, 1)
                dve.bn_aggr(bn[:, 0:2], stats[:].rearrange("p a b -> p (a b)")).then_inc(bn_own, 1)
                dve.wait_ge(bn_own, 2)
                dve.tensor_scalar(bn[:, 2:3], bn[:, 1:2], EPS, None, ALU.add).then_inc(bn_var, 1)
                dve.wait_ge(bn_rstd, 1)
                dve.tensor_tensor(k["bn_scale"][:], bn[:, 3:4], k["bn_g"][:], ALU.mult).then_inc(bn_own, 1)
                dve.wait_ge(bn_own, 3)
                dve.tensor_tensor(bn[:, 4:5], bn[:, 0:1], k["bn_scale"][:], ALU.mult).then_inc(bn_own, 1)
                dve.wait_ge(bn_own, 4)
                dve.tensor_tensor(k["bn_shift"][:], k["bn_b"][:], bn[:, 4:5], ALU.subtract)

            @block.gpsimd
            def _(pool):
                def gather(s):
                    if late(s, RING):
                        pool.wait_ge(rows_loaded[s.slot], s.lap * 16 * TILES)
                        pool.wait_ge(sums_ready, s.u - RING + 1)
                    pool.tensor_copy(slot_src[:, s.slot, :], k["slot_src"][:, bass.ds(s.u * TILES, TILES)]).then_inc(slots_ready, 1)
                    pool.wait_ge(slots_ready, s.u + 1)
                    pool.sem_inc(passed, 1)
                    for t in range(TILES):
                        pool.indirect_dma_start(out=rows[:, s.slot, t, :], out_offset=None, in_=y,
                                                in_offset=bass.IndirectOffsetOnAxis(ap=slot_src[:, s.slot, t:t + 1], axis=0),
                                                bounds_check=units * UNIT - 1, oob_is_err=False).then_inc(rows_loaded[s.slot], 16)

                with pool.If(k["is_regular"]):
                    pool.wait_ge(rows_clear, 1)
                    over_units(pool, units, [(0, gather)])
                pool.wait_ge(bn_var, 1)
                pool.tensor_tensor(bn[:, 3:4], bn[:, 2:3], k["power"][:, 0:1], ALU.pow).then_inc(bn_rstd, 1)

            @block.tensor
            def _(pe):
                def turn(s):
                    b = s.slot % 2
                    pe.wait_ge(scaled, (s.u + 1) * 2)
                    if late(s, 2):
                        pe.wait_ge(copied, (s.u - 1) * 2)
                    for t in range(TILES):
                        pe.transpose(g_turned[:, b, t * P:(t + 1) * P], gathered[:, b, t, :], k["ident"][:])
                        last = pe.transpose(x_turned[:, b, t * P:(t + 1) * P], own_x[:, b, t, :], k["ident"][:])
                    last.then_inc(turned, 1)

                def multiply(s):
                    b = s.slot % 2
                    pe.wait_ge(copied, (s.u + 1) * 2)
                    if late(s, 2):
                        pe.wait_ge(o_ready, s.u - 1)
                    pe.matmul(o_ps[:, b], k["gcn_w"][:], gT[:, b], start=True, stop=False)
                    pe.matmul(o_ps[:, b], k["rs_w"][:], xT[:, b], start=False, stop=True).then_inc(product, 1)

                def gather_sums(s):
                    b = s.slot % 2
                    pe.wait_ge(hot_ready, s.u + 1)
                    pe.wait_ge(rows_loaded[s.slot], (s.lap + 1) * 16 * TILES)
                    if late(s, 2):
                        pe.wait_ge(summed, s.u - 1)
                    for t in range(TILES):
                        last = pe.matmul(sum_ps[:, b, t * P:(t + 1) * P], hot[:, b, t, :], rows[:, s.slot, t, :], start=True, stop=True)
                    last.then_inc(sums_ready, 1)

                with pe.If(k["is_regular"]):
                    over_units(pe, units, [(0, gather_sums), (2, multiply), (1, turn)])
                with pe.If(k["irregular"]):
                    over_units(pe, units, [(1, multiply), (0, turn)])

            @block.scalar
            def _(act):
                def copy(s):
                    b = s.slot % 2
                    act.wait_ge(turned, s.u + 1)
                    if late(s, 2):
                        act.wait_ge(product, s.u - 1)
                    act.activation(gT[:, b], g_turned[:, b], ACT.Copy).then_inc(copied, 1)
                    act.activation(xT[:, b], x_turned[:, b], ACT.Copy).then_inc(copied, 1)

                def bias(s):
                    b = s.slot % 2
                    act.wait_ge(product, s.u + 1)
                    if late(s, RING):
                        act.wait_ge(o_stored[s.slot], s.lap * 16)
                        act.wait_ge(measured, s.u - RING + 1)
                    act.activation(o_out[:, s.slot], o_ps[:, b], ACT.Identity, bias=k["conv_b"][:]).then_inc(o_ready, 1)

                over_units(act, units, [(1, bias), (0, copy)])


def embed(nc, k, x, outT, x1, h, units):
    X, X1, H = by_unit(x), by_unit(x1), by_unit(h)
    with ExitStack() as stack:
        m = Memory(nc, stack, "emb")
        x_in = m.sb("x_in", [P, RING, TILES, D])
        o_in = m.sb("o_in", [P, RING, UNIT])
        bnT = m.sb("bnT", [P, 2, UNIT])
        leaky = m.sb("leaky", [P, 2, UNIT])
        mixed = m.sb("mixed", [P, 2, TILES, D])
        stats1, stats2 = (m.sb(n, [P, 2, TILES, 6]) for n in ("stats1", "stats2"))
        small1, small2 = (m.sb(n, [P, 2, 6, TILES]) for n in ("small1", "small2"))
        x1_out = m.sb("x1_out", [P, RING, TILES, D])
        x1T = m.sb("x1T", [P, 2, UNIT])
        hidden = m.sb("hidden", [P, 2, TILES, D])
        hn = m.sb("hn", [P, 2, TILES, D])
        hT = m.sb("hT", [P, 2, UNIT])
        h_out = m.sb("h_out", [P, RING, TILES, D])
        pair_hidden = m.sb("pair_hidden", [P, 2, UNIT])
        leaky_ps, x1_turned, w1_ps, h_turned, pair_ps, dots = (
            m.ps(n, [P, UNIT]) for n in ("leaky_ps", "x1_turned", "w1_ps", "h_turned", "pair_ps", "dots"))
        pair_product, pair_ready, dot_product, dot_kept = (m.sem(n) for n in ("pair_product", "pair_ready", "dot_product", "dot_kept"))
        h_back = m.ps("h_back", [P, 2, UNIT])
        x_loaded, o_loaded, x1_stored, h_stored = (m.sems(n, RING) for n in ("x_loaded", "o_loaded", "x1_stored", "h_stored"))
        (bn_ready, leaky_ready, leaky_turned, mixed_ready, stat1_own, stat2_own, rstd1, rstd2, x1_own, hn_own,
         x1_turn_ready, x1T_ready, w1_ready, hidden_ready, h_turn_ready, hT_ready, h_back_ready, h_ready) = (
            m.sem(n) for n in ("bn_ready", "leaky_ready", "leaky_turned", "mixed_ready", "stat1_own", "stat2_own",
                               "rstd1", "rstd2", "x1_own", "hn_own", "x1_turn_ready", "x1T_ready", "w1_ready",
                               "hidden_ready", "h_turn_ready", "hT_ready", "h_back_ready", "h_ready"))
        tiled = lambda ap: ap.rearrange("p (t f) -> p t f", t=TILES)
        with nc.Block() as block:
            @block.sync
            def _(sp):
                def load(s):
                    if late(s, RING):
                        sp.wait_ge(mixed_ready, s.u - RING + 1)
                        sp.wait_ge(bn_ready, s.u - RING + 1)
                    sp.dma_start(x_in[:, s.slot], X[s.u]).then_inc(x_loaded[s.slot], 16)
                    sp.dma_start(o_in[:, s.slot], outT[:, bass.ds(s.u * UNIT, UNIT)]).then_inc(o_loaded[s.slot], 16)

                def store_x1(s):
                    sp.wait_ge(x1_own, (s.u + 1) * APPLY_STEPS)
                    sp.dma_start(X1[s.u], x1_out[:, s.slot]).then_inc(x1_stored[s.slot], 16)

                def store_h(s):
                    sp.wait_ge(h_ready, s.u + 1)
                    sp.dma_start(H[s.u], h_out[:, s.slot]).then_inc(h_stored[s.slot], 16)

                over_units(sp, units, [(4, store_h), (2, store_x1), (0, load)])
                for q in x1_stored + h_stored:
                    sp.wait_ge(q, units // RING * 16)

            @block.scalar
            def _(act):
                def normalise(s):
                    b = s.slot % 2
                    act.wait_ge(o_loaded[s.slot], (s.lap + 1) * 16)
                    if late(s, 2):
                        act.wait_ge(leaky_ready, s.u - 1)
                    act.activation(bnT[:, b], o_in[:, s.slot], ACT.Identity, bias=k["bn_shift"][:],
                                   scale=k["bn_scale"][:]).then_inc(bn_ready, 1)

                def copy_x1(s):
                    b = s.slot % 2
                    act.wait_ge(x1_turn_ready, s.u + 1)
                    if late(s, 2):
                        act.wait_ge(w1_ready, s.u - 1)
                    act.activation(x1T[:, b], x1_turned[:], ACT.Copy).then_inc(x1T_ready, 1)

                def affine(s):
                    b = s.slot % 2
                    act.wait_ge(h_turn_ready, s.u + 1)
                    if late(s, 2):
                        act.wait_ge(h_back_ready, s.u - 1)
                        act.wait_ge(pair_product, s.u - 1)
                    act.activation(hT[:, b], h_turned[:], ACT.Relu, bias=k["bt1"][:], scale=k["g1"][:]).then_inc(hT_ready, 1)

                def copy_h(s):
                    b = s.slot % 2
                    act.wait_ge(h_back_ready, s.u + 1)
                    if late(s, RING):
                        act.wait_ge(h_stored[s.slot], s.lap * 16)
                    act.activation(h_out[:, s.slot], tiled(h_back[:, b]), ACT.Copy).then_inc(h_ready, 1)

                def pair(s):
                    b = s.slot % 2
                    act.wait_ge(pair_product, s.u + 1)
                    if late(s, 2):
                        act.wait_ge(dot_product, s.u - 1)
                    act.activation(pair_hidden[:, b], pair_ps[:], ACT.Relu, bias=k["be1"][:]).then_inc(pair_ready, 1)

                over_units(act, units, [(3, affine), (3, copy_h), (0, normalise), (3, pair), (1, copy_x1)])

            @block.vector
            def _(dve):
                def activate(s):
                    b = s.slot % 2
                    dve.wait_ge(bn_ready, s.u + 1)
                    if late(s, 2):
                        dve.wait_ge(leaky_turned, s.u - 1)
                    dve.scalar_tensor_tensor(leaky[:, b], bnT[:, b], SLOPE, bnT[:, b], ALU.mult, ALU.max).then_inc(leaky_ready, 1)

                def mix(s):
                    b = s.slot % 2
                    dve.wait_ge(leaky_turned, s.u + 1)
                    dve.wait_ge(x_loaded[s.slot], (s.lap + 1) * 16)
                    dve.tensor_tensor(mixed[:, b], tiled(leaky_ps[:]), x_in[:, s.slot], ALU.add).then_inc(mixed_ready, 1)
                    dve.wait_ge(mixed_ready, s.u + 1)
                    norm_stats(dve, Chain(dve, stat1_own, s.u * NORM_STEPS), mixed[:, b], stats1[:, b], small1[:, b])

                def apply1(s):
                    b = s.slot % 2
                    dve.wait_ge(rstd1, s.u + 1)
                    if late(s, RING):
                        dve.wait_ge(x1_stored[s.slot], s.lap * 16)
                        dve.wait_ge(x1_turn_ready, s.u - RING + 1)
                    norm_apply(dve, Chain(dve, x1_own, s.u * APPLY_STEPS), mixed[:, b], x1_out[:, s.slot], small1[:, b])

                def hide(s):
                    b = s.slot % 2
                    dve.wait_ge(w1_ready, s.u + 1)
                    dve.tensor_tensor(hidden[:, b], tiled(w1_ps[:]), k["b1_row"][:].unsqueeze(1).to_broadcast([P, TILES, D]),
                                      ALU.add).then_inc(hidden_ready, 1)
                    dve.wait_ge(hidden_ready, s.u + 1)
                    norm_stats(dve, Chain(dve, stat2_own, s.u * NORM_STEPS), hidden[:, b], stats2[:, b], small2[:, b])

                def apply2(s):
                    b = s.slot % 2
                    dve.wait_ge(rstd2, s.u + 1)
                    if late(s, 2):
                        dve.wait_ge(h_turn_ready, s.u - 1)
                    norm_apply(dve, Chain(dve, hn_own, s.u * APPLY_STEPS), hidden[:, b], hn[:, b], small2[:, b])

                def keep_dot(s):
                    dve.wait_ge(dot_product, s.u + 1)
                    dve.tensor_copy(k["loop_dot"][:, bass.ds(s.u * TILES, TILES)], dots[:, 0:TILES]).then_inc(dot_kept, 1)

                over_units(dve, units, [(3, apply2), (2, hide), (1, apply1), (0, activate), (4, keep_dot), (0, mix)])

            @block.gpsimd
            def _(pool):
                def root1(s):
                    b = s.slot % 2
                    pool.wait_ge(stat1_own, (s.u + 1) * NORM_STEPS)
                    pool.tensor_tensor(small1[:, b, 4, :], small1[:, b, 3, :], k["power"][:], ALU.pow).then_inc(rstd1, 1)

                def root2(s):
                    b = s.slot % 2
                    pool.wait_ge(stat2_own, (s.u + 1) * NORM_STEPS)
                    pool.tensor_tensor(small2[:, b, 4, :], small2[:, b, 3, :], k["power"][:], ALU.pow).then_inc(rstd2, 1)

                over_units(pool, units, [(2, root2), (0, root1)])

            @block.tensor
            def _(pe):
                def turn_leaky(s):
                    b = s.slot % 2
                    pe.wait_ge(leaky_ready, s.u + 1)
                    if late(s, 1):
                        pe.wait_ge(mixed_ready, s.u)
                    for t in range(TILES):
                        last = pe.transpose(leaky_ps[:, t * P:(t + 1) * P], leaky[:, b, t * P:(t + 1) * P], k["ident"][:])
                    last.then_inc(leaky_turned, 1)

                def turn_x1(s):
                    pe.wait_ge(x1_own, (s.u + 1) * APPLY_STEPS)
                    if late(s, 1):
                        pe.wait_ge(x1T_ready, s.u)
                    for t in range(TILES):
                        last = pe.transpose(x1_turned[:, t * P:(t + 1) * P], x1_out[:, s.slot, t, :], k["ident"][:])
                    last.then_inc(x1_turn_ready, 1)

                def multiply(s):
                    b = s.slot % 2
                    pe.wait_ge(x1T_ready, s.u + 1)
                    if late(s, 1):
                        pe.wait_ge(hidden_ready, s.u)
                    for t in range(TILES):
                        last = pe.matmul(w1_ps[:, t * P:(t + 1) * P], x1T[:, b, t * P:(t + 1) * P], k["W1"][:], start=True, stop=True)
                    last.then_inc(w1_ready, 1)

                def turn_h(s):
                    b = s.slot % 2
                    pe.wait_ge(hn_own, (s.u + 1) * APPLY_STEPS)
                    if late(s, 1):
                        pe.wait_ge(hT_ready, s.u)
                    for t in range(TILES):
                        last = pe.transpose(h_turned[:, t * P:(t + 1) * P], hn[:, b, t, :], k["ident"][:])
                    last.then_inc(h_turn_ready, 1)

                def turn_back(s):
                    b = s.slot % 2
                    pe.wait_ge(hT_ready, s.u + 1)
                    if late(s, 2):
                        pe.wait_ge(h_ready, s.u - 1)
                    for t in range(TILES):
                        last = pe.transpose(h_back[:, b, t * P:(t + 1) * P], hT[:, b, t * P:(t + 1) * P], k["ident"][:])
                    last.then_inc(h_back_ready, 1)

                def pair(s):
                    b = s.slot % 2
                    pe.wait_ge(hT_ready, s.u + 1)
                    if late(s, 1):
                        pe.wait_ge(pair_ready, s.u)
                    for half in range(2):
                        last = pe.matmul(pair_ps[:], k["We1"][:, half, :], hT[:, b], start=(half == 0), stop=(half == 1))
                    last.then_inc(pair_product, 1)

                def dot(s):
                    b = s.slot % 2
                    pe.wait_ge(pair_ready, s.u + 1)
                    if late(s, 1):
                        pe.wait_ge(dot_kept, s.u)
                    for t in range(TILES):
                        last = pe.matmul(dots[:, t:t + 1], pair_hidden[:, b, t * P:(t + 1) * P], k["We2"][:], start=True, stop=True)
                    last.then_inc(dot_product, 1)

                over_units(pe, units, [(3, turn_h), (4, dot), (1, turn_x1), (3, turn_back), (0, turn_leaky), (3, pair), (1, multiply)])


def gate(nc, k, x1, h, sums, out, units):
    X1, H, SUMS, OUT = by_unit(x1), by_unit(h), by_unit(sums[0:units * UNIT, :]), by_unit(out)
    MIX = 3
    with ExitStack() as stack:
        m = Memory(nc, stack, "gate")
        h_in, s_in, x1_in = (m.sb(n, [P, RING, TILES, D]) for n in ("h_in", "s_in", "x1_in"))
        hT, sT, gT, nT = (m.sb(n, [P, 2, UNIT]) for n in ("hT", "sT", "gT", "nT"))
        change, n1, n1n, n2 = (m.sb(n, [P, 2, TILES, D]) for n in ("change", "n1", "n1n", "n2"))
        out_sb = m.sb("out_sb", [P, RING, TILES, D])
        stats1, stats2 = (m.sb(n, [P, 2, TILES, 6]) for n in ("stats1", "stats2"))
        small1, small2 = (m.sb(n, [P, 2, 6, TILES]) for n in ("small1", "small2"))
        h_turned, s_turned, g_ps, n_turned = (m.ps(n, [P, UNIT]) for n in ("h_turned", "s_turned", "g_ps", "n_turned"))
        g_back, n_back = (m.ps(n, [P, 2, UNIT]) for n in ("g_back", "n_back"))
        h_loaded, s_loaded, x1_loaded, stored = (m.sems(n, RING) for n in ("h_loaded", "s_loaded", "x1_loaded", "stored"))
        (in_turned, in_copied, g_product, g_ready, g_turned, mix_own, stat1_own, stat2_own, rstd1, rstd2, n1_own, out_own,
         n_turn_ready, nT_ready, n_back_ready, n2_ready) = (
            m.sem(n) for n in ("in_turned", "in_copied", "g_product", "g_ready", "g_turned", "mix_own", "stat1_own",
                               "stat2_own", "rstd1", "rstd2", "n1_own", "out_own", "n_turn_ready", "nT_ready",
                               "n_back_ready", "n2_ready"))
        tiled = lambda ap: ap.rearrange("p (t f) -> p t f", t=TILES)
        with nc.Block() as block:
            @block.sync
            def _(sp):
                def load(s):
                    if late(s, RING):
                        sp.wait_ge(mix_own, (s.u - RING + 1) * MIX)
                        sp.wait_ge(in_turned, s.u - RING + 1)
                    sp.dma_start(h_in[:, s.slot], H[s.u]).then_inc(h_loaded[s.slot], 16)
                    sp.dma_start(s_in[:, s.slot], SUMS[s.u]).then_inc(s_loaded[s.slot], 16)

                def load_x1(s):
                    if late(s, RING):
                        sp.wait_ge(n2_ready, s.u - RING + 1)
                    sp.dma_start(x1_in[:, s.slot], X1[s.u]).then_inc(x1_loaded[s.slot], 16)

                def store(s):
                    sp.wait_ge(out_own, (s.u + 1) * APPLY_STEPS)
                    sp.dma_start(OUT[s.u], out_sb[:, s.slot]).then_inc(stored[s.slot], 16)

                with sp.If(k["irregular"]):
                    over_units(sp, units, [(6, store), (2, load_x1), (0, load)])
                    for q in stored:
                        sp.wait_ge(q, units // RING * 16)

            @block.tensor
            def _(pe):
                def turn_in(s):
                    pe.wait_ge(h_loaded[s.slot], (s.lap + 1) * 16)
                    pe.wait_ge(s_loaded[s.slot], (s.lap + 1) * 16)
                    if late(s, 1):
                        pe.wait_ge(in_copied, s.u * 2)
                    for t in range(TILES):
                        pe.transpose(h_turned[:, t * P:(t + 1) * P], h_in[:, s.slot, t, :], k["ident"][:])
                        last = pe.transpose(s_turned[:, t * P:(t + 1) * P], s_in[:, s.slot, t, :], k["ident"][:])
                    last.then_inc(in_turned, 1)

                def multiply(s):
                    b = s.slot % 2
                    pe.wait_ge(in_copied, (s.u + 1) * 2)
                    if late(s, 1):
                        pe.wait_ge(g_ready, s.u)
                    pe.matmul(g_ps[:], k["Wg"][:, 0, :], hT[:, b], start=True, stop=False)
                    pe.matmul(g_ps[:], k["Wg"][:, 1, :], sT[:, b], start=False, stop=True).then_inc(g_product, 1)

                def turn_gate(s):
                    b = s.slot % 2
                    pe.wait_ge(g_ready, s.u + 1)
                    if late(s, 2):
                        pe.wait_ge(mix_own, (s.u - 1) * MIX)
                    for t in range(TILES):
                        last = pe.transpose(g_back[:, b, t * P:(t + 1) * P], gT[:, b, t * P:(t + 1) * P], k["ident"][:])
                    last.then_inc(g_turned, 1)

                def turn_n(s):
                    b = s.slot % 2
                    pe.wait_ge(n1_own, (s.u + 1) * APPLY_STEPS)
                    if late(s, 1):
                        pe.wait_ge(nT_ready, s.u)
                    for t in range(TILES):
                        last = pe.transpose(n_turned[:, t * P:(t + 1) * P], n1n[:, b, t, :], k["ident"][:])
                    last.then_inc(n_turn_ready, 1)

                def turn_back(s):
                    b = s.slot % 2
                    pe.wait_ge(nT_ready, s.u + 1)
                    if late(s, 2):
                        pe.wait_ge(n2_ready, s.u - 1)
                    for t in range(TILES):
                        last = pe.transpose(n_back[:, b, t * P:(t + 1) * P], nT[:, b, t * P:(t + 1) * P], k["ident"][:])
                    last.then_inc(n_back_ready, 1)

                with pe.If(k["irregular"]):
                    over_units(pe, units, [(4, turn_back), (3, turn_n), (2, turn_gate), (1, multiply), (0, turn_in)])

            @block.scalar
            def _(act):
                def copy(s):
                    b = s.slot % 2
                    act.wait_ge(in_turned, s.u + 1)
                    if late(s, 2):
                        act.wait_ge(g_product, s.u - 1)
                    act.activation(hT[:, b], h_turned[:], ACT.Copy).then_inc(in_copied, 1)
                    act.activation(sT[:, b], s_turned[:], ACT.Copy).then_inc(in_copied, 1)

                def squash(s):
                    b = s.slot % 2
                    act.wait_ge(g_product, s.u + 1)
                    if late(s, 2):
                        act.wait_ge(g_turned, s.u - 1)
                    act.activation(gT[:, b], g_ps[:], ACT.Sigmoid, bias=k["bg"][:]).then_inc(g_ready, 1)

                def affine(s):
                    b = s.slot % 2
                    act.wait_ge(n_turn_ready, s.u + 1)
                    if late(s, 2):
                        act.wait_ge(n_back_ready, s.u - 1)
                    act.activation(nT[:, b], n_turned[:], ACT.Identity, bias=k["bt2"][:], scale=k["g2"][:]).then_inc(nT_ready, 1)

                with act.If(k["irregular"]):
                    over_units(act, units, [(3, affine), (1, squash), (0, copy)])

            @block.vector
            def _(dve):
                def mix(s):
                    b = s.slot % 2
                    chain = Chain(dve, mix_own, s.u * MIX)
                    dve.wait_ge(h_loaded[s.slot], (s.lap + 1) * 16)
                    dve.wait_ge(s_loaded[s.slot], (s.lap + 1) * 16)
                    chain.mark(dve.tensor_tensor(change[:, b], s_in[:, s.slot], h_in[:, s.slot], ALU.subtract))
                    chain.settle()
                    dve.wait_ge(g_turned, s.u + 1)
                    chain.mark(dve.tensor_tensor(change[:, b], tiled(g_back[:, b]), change[:, b], ALU.mult))
                    chain.settle()
                    chain.mark(dve.tensor_tensor(n1[:, b], change[:, b], h_in[:, s.slot], ALU.add))
                    chain.settle()
                    norm_stats(dve, Chain(dve, stat1_own, s.u * NORM_STEPS), n1[:, b], stats1[:, b], small1[:, b])

                def apply1(s):
                    b = s.slot % 2
                    dve.wait_ge(rstd1, s.u + 1)
                    if late(s, 2):
                        dve.wait_ge(n_turn_ready, s.u - 1)
                    norm_apply(dve, Chain(dve, n1_own, s.u * APPLY_STEPS), n1[:, b], n1n[:, b], small1[:, b])

                def residual(s):
                    b = s.slot % 2
                    dve.wait_ge(n_back_ready, s.u + 1)
                    dve.wait_ge(x1_loaded[s.slot], (s.lap + 1) * 16)
                    dve.tensor_tensor(n2[:, b], tiled(n_back[:, b]), x1_in[:, s.slot], ALU.add).then_inc(n2_ready, 1)
                    dve.wait_ge(n2_ready, s.u + 1)
                    norm_stats(dve, Chain(dve, stat2_own, s.u * NORM_STEPS), n2[:, b], stats2[:, b], small2[:, b])

                def apply2(s):
                    b = s.slot % 2
                    dve.wait_ge(rstd2, s.u + 1)
                    if late(s, RING):
                        dve.wait_ge(stored[s.slot], s.lap * 16)
                    norm_apply(dve, Chain(dve, out_own, s.u * APPLY_STEPS), n2[:, b], out_sb[:, s.slot], small2[:, b])

                with dve.If(k["irregular"]):
                    over_units(dve, units, [(5, apply2), (4, residual), (3, apply1), (2, mix)])

            @block.gpsimd
            def _(pool):
                def root1(s):
                    b = s.slot % 2
                    pool.wait_ge(stat1_own, (s.u + 1) * NORM_STEPS)
                    pool.tensor_tensor(small1[:, b, 4, :], small1[:, b, 3, :], k["power"][:], ALU.pow).then_inc(rstd1, 1)

                def root2(s):
                    b = s.slot % 2
                    pool.wait_ge(stat2_own, (s.u + 1) * NORM_STEPS)
                    pool.tensor_tensor(small2[:, b, 4, :], small2[:, b, 3, :], k["power"][:], ALU.pow).then_inc(rstd2, 1)

                with pool.If(k["irregular"]):
                    over_units(pool, units, [(4, root2), (2, root1)])


def attend(nc, k, x1, h, rel_rows, out, units):
    X1, H, OUT = by_unit(x1), by_unit(h), by_unit(out)
    REL = rel_rows.rearrange("(u t) s -> u (t s)", t=TILES)
    SUM, MIX = TILES, 3
    with ExitStack() as stack:
        m = Memory(nc, stack, "att")
        h_in, x1_in, rows = (m.sb(n, [P, RING, TILES, D]) for n in ("h_in", "x1_in", "rows"))
        rel_in = m.sb("rel_in", [P, RING, UNIT])
        slot_src = m.sb("slot_src", [P, RING, TILES], I32)
        hT, rowsT, value, pick, hidden, sT, gT, nT = (
            m.sb(n, [P, 2, UNIT]) for n in ("hT", "rowsT", "value", "pick", "hidden", "sT", "gT", "nT"))
        weight = m.sb("weight", [P, 2, 2, TILES])
        weighted = m.sb("weighted", [P, 2, TILES, P])
        sums, change, n1, n1n, n2 = (m.sb(n, [P, 2, TILES, D]) for n in ("sums", "change", "n1", "n1n", "n2"))
        out_sb = m.sb("out_sb", [P, RING, TILES, D])
        stats1, stats2 = (m.sb(n, [P, 2, TILES, 6]) for n in ("stats1", "stats2"))
        small1, small2 = (m.sb(n, [P, 2, 6, TILES]) for n in ("small1", "small2"))
        h_or_sums, rows_or_n, value_or_sums, pre, g_ps, g_back, n_back, dots = (
            m.ps(n, [P, UNIT]) for n in ("h_or_sums", "rows_or_n", "value_or_sums", "pre", "g_ps", "g_back", "n_back", "dots"))
        h_loaded, rel_loaded, x1_loaded, rows_loaded, stored = (
            m.sems(n, RING) for n in ("h_loaded", "rel_loaded", "x1_loaded", "rows_loaded", "stored"))
        (rows_clear, slots_ready, passed, h_turned, rows_turned, hT_ready, rowsT_ready, value_product, value_ready,
         pick_ready, pre_product, hidden_ready, dot_product, weight_ready, weighted_ready, sum_product, sums_own,
         sums_turned, sT_ready, g_product, g_ready, g_turned, mix_own, stat1_own, stat2_own, rstd1, rstd2, n1_own,
         out_own, n_turned, nT_ready, n_back_ready, n2_ready) = (
            m.sem(n) for n in ("rows_clear", "slots_ready", "passed", "h_turned", "rows_turned", "hT_ready", "rowsT_ready",
                               "value_product", "value_ready", "pick_ready", "pre_product", "hidden_ready", "dot_product",
                               "weight_ready", "weighted_ready", "sum_product", "sums_own", "sums_turned", "sT_ready",
                               "g_product", "g_ready", "g_turned", "mix_own", "stat1_own", "stat2_own", "rstd1", "rstd2",
                               "n1_own", "out_own", "n_turned", "nT_ready", "n_back_ready", "n2_ready"))
        tiled = lambda ap: ap.rearrange("p (t f) -> p t f", t=TILES)

        def ahead(s, n):
            return min(s.u + n + 1, units) if isinstance(s.u, int) else s.u + n + 1

        with nc.Block() as block:
            @block.sync
            def _(sp):
                def load(s):
                    if late(s, RING):
                        sp.wait_ge(mix_own, (s.u - RING + 1) * MIX)
                        sp.wait_ge(pick_ready, s.u - RING + 1)
                    sp.dma_start(h_in[:, s.slot], H[s.u]).then_inc(h_loaded[s.slot], 16)
                    sp.dma_start(rel_in[:, s.slot], REL[bass.ds(s.u, 1), :].to_broadcast([P, UNIT])).then_inc(rel_loaded[s.slot], 16)

                def load_x1(s):
                    if late(s, RING):
                        sp.wait_ge(n2_ready, s.u - RING + 1)
                    sp.dma_start(x1_in[:, s.slot], X1[s.u]).then_inc(x1_loaded[s.slot], 16)

                def store(s):
                    sp.wait_ge(out_own, (s.u + 1) * APPLY_STEPS)
                    sp.dma_start(OUT[s.u], out_sb[:, s.slot]).then_inc(stored[s.slot], 16)

                with sp.If(k["is_regular"]):
                    over_units(sp, units, [(7, store), (2, load_x1), (0, load)])
                    for q in stored:
                        sp.wait_ge(q, units // RING * 16)

            @block.gpsimd
            def _(pool):
                def gather(s):
                    if late(s, RING):
                        pool.wait_ge(rows_loaded[s.slot], s.lap * 16 * TILES)
                        pool.wait_ge(sum_product, s.u - RING + 1)
                    pool.tensor_copy(slot_src[:, s.slot, :], k["slot_src"][:, bass.ds(s.u * TILES, TILES)]).then_inc(slots_ready, 1)
                    pool.wait_ge(slots_ready, s.u + 1)
                    pool.sem_inc(passed, 1)
                    for t in range(TILES):
                        pool.indirect_dma_start(out=rows[:, s.slot, t, :], out_offset=None, in_=h,
                                                in_offset=bass.IndirectOffsetOnAxis(ap=slot_src[:, s.slot, t:t + 1], axis=0),
                                                bounds_check=units * UNIT - 1, oob_is_err=False).then_inc(rows_loaded[s.slot], 16)

                def root1(s):
                    b = s.slot % 2
                    pool.wait_ge(stat1_own, (s.u + 1) * NORM_STEPS)
                    pool.tensor_tensor(small1[:, b, 4, :], small1[:, b, 3, :], k["power"][:], ALU.pow).then_inc(rstd1, 1)

                def root2(s):
                    b = s.slot % 2
                    pool.wait_ge(stat2_own, (s.u + 1) * NORM_STEPS)
                    pool.tensor_tensor(small2[:, b, 4, :], small2[:, b, 3, :], k["power"][:], ALU.pow).then_inc(rstd2, 1)

                with pool.If(k["is_regular"]):
                    pool.wait_ge(rows_clear, 1)
                    over_units(pool, units, [(0, gather), (6, root2), (4, root1)])

            @block.tensor
            def _(pe):
                def turn_in(s):
                    pe.wait_ge(h_loaded[s.slot], (s.lap + 1) * 16)
                    if late(s, 2):
                        pe.wait_ge(sT_ready, s.u - 1)
                    for t in range(TILES):
                        last = pe.transpose(h_or_sums[:, t * P:(t + 1) * P], h_in[:, s.slot, t, :], k["ident"][:])
                    last.then_inc(h_turned, 1)
                    pe.wait_ge(rows_loaded[s.slot], (s.lap + 1) * 16 * TILES)
                    if late(s, RING):
                        pe.wait_ge(nT_ready, s.u - 3)
                    for t in range(TILES):
                        last = pe.transpose(rows_or_n[:, t * P:(t + 1) * P], rows[:, s.slot, t, :], k["ident"][:])
                    last.then_inc(rows_turned, 1)

                def dot(s):
                    b = s.slot % 2
                    pe.wait_ge(hidden_ready, s.u + 1)
                    if late(s, 2):
                        pe.wait_ge(weight_ready, (s.u - 1) * 2)
                    for t in range(TILES):
                        last = pe.matmul(dots[:, b * TILES + t:b * TILES + t + 1], hidden[:, b, t * P:(t + 1) * P], k["We2"][:], start=True, stop=True)
                    last.then_inc(dot_product, 1)

                def values(s):
                    b = s.slot % 2
                    pe.wait_ge(hT_ready, s.u + 1)
                    if late(s, 2):
                        pe.wait_ge(sums_own, (s.u - 1) * SUM)
                    for t in range(TILES):
                        last = pe.matmul(value_or_sums[:, t * P:(t + 1) * P], hT[:, b, t * P:(t + 1) * P], k["We1"][:, 1, :], start=True, stop=True)
                    last.then_inc(value_product, 1)

                def turn_n(s):
                    b = s.slot % 2
                    pe.wait_ge(n1_own, (s.u + 1) * APPLY_STEPS)
                    pe.wait_ge(rowsT_ready, ahead(s, 3))
                    for t in range(TILES):
                        last = pe.transpose(rows_or_n[:, t * P:(t + 1) * P], n1n[:, b, t, :], k["ident"][:])
                    last.then_inc(n_turned, 1)

                def sum_rows(s):
                    b = s.slot % 2
                    pe.wait_ge(weighted_ready, s.u + 1)
                    pe.wait_ge(value_ready, ahead(s, 1))
                    for t in range(TILES):
                        last = pe.matmul(value_or_sums[:, t * P:(t + 1) * P], weighted[:, b, t, :], rows[:, s.slot, t, :], start=True, stop=True)
                    last.then_inc(sum_product, 1)

                def turn_gate(s):
                    b = s.slot % 2
                    pe.wait_ge(g_ready, s.u + 1)
                    if late(s, 1):
                        pe.wait_ge(mix_own, s.u * MIX)
                    for t in range(TILES):
                        last = pe.transpose(g_back[:, t * P:(t + 1) * P], gT[:, b, t * P:(t + 1) * P], k["ident"][:])
                    last.then_inc(g_turned, 1)

                def pairs(s):
                    b = s.slot % 2
                    pe.wait_ge(rowsT_ready, s.u + 1)
                    if late(s, 1):
                        pe.wait_ge(hidden_ready, s.u)
                    pe.matmul(pre[:], k["We1"][:, 0, :], rowsT[:, b], start=True, stop=False, skip_group_check=True)
                    pe.wait_ge(value_ready, s.u + 1)
                    pe.wait_ge(pick_ready, s.u + 1)
                    for t in range(TILES):
                        last = pe.matmul(pre[:, t * P:(t + 1) * P], value[:, b, t * P:(t + 1) * P], pick[:, b, t * P:(t + 1) * P],
                                         start=False, stop=(t == TILES - 1), skip_group_check=True)
                    last.then_inc(pre_product, 1)

                def turn_sums(s):
                    b = s.slot % 2
                    pe.wait_ge(sums_own, (s.u + 1) * SUM)
                    pe.wait_ge(hT_ready, ahead(s, 1))
                    for t in range(TILES):
                        last = pe.transpose(h_or_sums[:, t * P:(t + 1) * P], sums[:, b, t, :], k["ident"][:])
                    last.then_inc(sums_turned, 1)

                def turn_back(s):
                    b = s.slot % 2
                    pe.wait_ge(nT_ready, s.u + 1)
                    if late(s, 1):
                        pe.wait_ge(n2_ready, s.u)
                    for t in range(TILES):
                        last = pe.transpose(n_back[:, t * P:(t + 1) * P], nT[:, b, t * P:(t + 1) * P], k["ident"][:])
                    last.then_inc(n_back_ready, 1)

                def gates(s):
                    b = s.slot % 2
                    if late(s, 1):
                        pe.wait_ge(g_ready, s.u)
                    pe.matmul(g_ps[:], k["Wg"][:, 0, :], hT[:, b], start=True, stop=False)
                    pe.wait_ge(sT_ready, s.u + 1)
                    pe.matmul(g_ps[:], k["Wg"][:, 1, :], sT[:, b], start=False, stop=True).then_inc(g_product, 1)

                with pe.If(k["is_regular"]):
                    over_units(pe, units, [(0, turn_in), (1, dot), (0, values), (3, turn_n), (1, sum_rows), (2, turn_gate),
                                           (0, pairs), (1, turn_sums), (3, turn_back), (1, gates)])

            @block.scalar
            def _(act):
                def copy_in(s):
                    b = s.slot % 2
                    act.wait_ge(h_turned, s.u + 1)
                    if late(s, 2):
                        act.wait_ge(g_product, s.u - 1)
                    act.activation(hT[:, b], h_or_sums[:], ACT.Copy).then_inc(hT_ready, 1)
                    act.wait_ge(rows_turned, s.u + 1)
                    if late(s, 2):
                        act.wait_ge(pre_product, s.u - 1)
                    act.activation(rowsT[:, b], rows_or_n[:], ACT.Copy).then_inc(rowsT_ready, 1)

                def weigh(s):
                    b = s.slot % 2
                    act.wait_ge(dot_product, s.u + 1)
                    if late(s, 2):
                        act.wait_ge(weighted_ready, s.u - 1)
                        act.wait_ge(sums_own, (s.u - 1) * SUM)
                    act.activation(weight[:, b, 0, :], dots[:, b * TILES:(b + 1) * TILES], ACT.Sigmoid, bias=k["be2"][:]).then_inc(weight_ready, 1)
                    act.activation(weight[:, b, 1, :], k["loop_dot"][:, bass.ds(s.u * TILES, TILES)], ACT.Sigmoid, bias=k["be2"][:]).then_inc(weight_ready, 1)

                def copy_values(s):
                    b = s.slot % 2
                    act.wait_ge(value_product, s.u + 1)
                    if late(s, 2):
                        act.wait_ge(pre_product, s.u - 1)
                    act.activation(value[:, b], value_or_sums[:], ACT.Copy).then_inc(value_ready, 1)

                def affine(s):
                    b = s.slot % 2
                    act.wait_ge(n_turned, s.u + 1)
                    if late(s, 2):
                        act.wait_ge(n_back_ready, s.u - 1)
                    act.activation(nT[:, b], rows_or_n[:], ACT.Identity, bias=k["bt2"][:], scale=k["g2"][:]).then_inc(nT_ready, 1)

                def rectify(s):
                    b = s.slot % 2
                    act.wait_ge(pre_product, s.u + 1)
                    if late(s, 2):
                        act.wait_ge(dot_product, s.u - 1)
                    act.activation(hidden[:, b], pre[:], ACT.Relu, bias=k["be1"][:]).then_inc(hidden_ready, 1)

                def copy_sums(s):
                    b = s.slot % 2
                    act.wait_ge(sums_turned, s.u + 1)
                    if late(s, 2):
                        act.wait_ge(g_product, s.u - 1)
                    act.activation(sT[:, b], h_or_sums[:], ACT.Copy).then_inc(sT_ready, 1)

                def squash(s):
                    b = s.slot % 2
                    act.wait_ge(g_product, s.u + 1)
                    if late(s, 2):
                        act.wait_ge(g_turned, s.u - 1)
                    act.activation(gT[:, b], g_ps[:], ACT.Sigmoid, bias=k["bg"][:]).then_inc(g_ready, 1)

                with act.If(k["is_regular"]):
                    over_units(act, units, [(0, copy_in), (1, weigh), (0, copy_values), (3, affine), (0, rectify),
                                            (1, copy_sums), (1, squash)])

            @block.vector
            def _(dve):
                def picks(s):
                    b = s.slot % 2
                    dve.wait_ge(rel_loaded[s.slot], (s.lap + 1) * 16)
                    if late(s, 2):
                        dve.wait_ge(pre_product, s.u - 1)
                    dve.tensor_scalar(pick[:, b], rel_in[:, s.slot], k["trash"][:], None, ALU.is_equal).then_inc(pick_ready, 1)

                def weigh_hot(s):
                    b = s.slot % 2
                    dve.wait_ge(weight_ready, (s.u + 1) * 2)
                    if late(s, 2):
                        dve.wait_ge(sum_product, s.u - 1)
                    for t in range(TILES):
                        last = dve.tensor_scalar(weighted[:, b, t, :], k["lane"][:], k["slot_rel"][:, bass.ds(s.u * TILES + t, 1)],
                                                 weight[:, b, 0, t:t + 1], ALU.is_equal, ALU.mult)
                    last.then_inc(weighted_ready, 1)

                def add_loops(s):
                    b = s.slot % 2
                    dve.wait_ge(sum_product, s.u + 1)
                    dve.wait_ge(h_loaded[s.slot], (s.lap + 1) * 16)
                    if late(s, 2):
                        dve.wait_ge(mix_own, (s.u - 1) * MIX)
                        dve.wait_ge(sums_turned, s.u - 1)
                    for t in range(TILES):
                        dve.scalar_tensor_tensor(sums[:, b, t, :], h_in[:, s.slot, t, :], weight[:, b, 1, t:t + 1],
                                                 value_or_sums[:, t * P:(t + 1) * P], ALU.mult, ALU.add).then_inc(sums_own, 1)

                def mix(s):
                    b = s.slot % 2
                    chain = Chain(dve, mix_own, s.u * MIX)
                    if late(s, 2):
                        dve.wait_ge(n1_own, (s.u - 1) * APPLY_STEPS)
                    chain.mark(dve.tensor_tensor(change[:, b], sums[:, b], h_in[:, s.slot], ALU.subtract))
                    chain.settle()
                    dve.wait_ge(g_turned, s.u + 1)
                    chain.mark(dve.tensor_tensor(change[:, b], tiled(g_back[:]), change[:, b], ALU.mult))
                    chain.settle()
                    chain.mark(dve.tensor_tensor(n1[:, b], change[:, b], h_in[:, s.slot], ALU.add))
                    chain.settle()
                    norm_stats(dve, Chain(dve, stat1_own, s.u * NORM_STEPS), n1[:, b], stats1[:, b], small1[:, b])

                def apply1(s):
                    b = s.slot % 2
                    dve.wait_ge(rstd1, s.u + 1)
                    if late(s, 2):
                        dve.wait_ge(n_turned, s.u - 1)
                    norm_apply(dve, Chain(dve, n1_own, s.u * APPLY_STEPS), n1[:, b], n1n[:, b], small1[:, b])

                def residual(s):
                    b = s.slot % 2
                    dve.wait_ge(n_back_ready, s.u + 1)
                    dve.wait_ge(x1_loaded[s.slot], (s.lap + 1) * 16)
                    if late(s, 2):
                        dve.wait_ge(out_own, (s.u - 1) * APPLY_STEPS)
                    dve.tensor_tensor(n2[:, b], tiled(n_back[:]), x1_in[:, s.slot], ALU.add).then_inc(n2_ready, 1)
                    dve.wait_ge(n2_ready, s.u + 1)
                    norm_stats(dve, Chain(dve, stat2_own, s.u * NORM_STEPS), n2[:, b], stats2[:, b], small2[:, b])

                def apply2(s):
                    b = s.slot % 2
                    dve.wait_ge(rstd2, s.u + 1)
                    if late(s, RING):
                        dve.wait_ge(stored[s.slot], s.lap * 16)
                    norm_apply(dve, Chain(dve, out_own, s.u * APPLY_STEPS), n2[:, b], out_sb[:, s.slot], small2[:, b])

                with dve.If(k["is_regular"]):
                    dve.memset(rows[:], 0.0).then_inc(rows_clear, 1)
                    over_units(dve, units, [(3, apply1), (0, picks), (1, weigh_hot), (1, add_loops), (5, apply2), (2, mix),
                                            (4, residual)])


VECTORS = {"ln_g": "L0_gnn_ln_g", "ln_b": "L0_gnn_ln_b", "gcn_b": "L0_gnn_gcn_b", "rs_b": "L0_gnn_rs_b",
           "bn_g": "L0_gnn_bn_g", "bn_b": "L0_gnn_bn_b", "g1": "L1_gnn_g1", "bt1": "L1_gnn_bt1",
           "be1": "L1_gnn_be1", "bg": "L1_gnn_bg", "g2": "L1_gnn_g2", "bt2": "L1_gnn_bt2", "be2": "L1_gnn_be2"}
MATRICES = {"gcn_w": "L0_gnn_gcn_w", "rs_w": "L0_gnn_rs_w", "W1": "L1_gnn_W1", "We1": "L1_gnn_We1",
            "We2": "L1_gnn_We2", "Wg": "L1_gnn_Wg"}


def load_edges(nc, stack, src, dst, chunks, tiles, b1, k):
    m = Memory(nc, stack, "k")
    for name in ("src", "dst", "place"):
        k[name] = m.sb(name, [P, chunks], I32)
    k["slot_src"], k["slot_rel"] = m.sb("slot_src", [P, tiles], I32), m.sb("slot_rel", [P, tiles])
    k["regular"] = m.sb("regular", [1, 2], I32)
    for name in ("dinv", "root", "edges", "loop_dot"):
        k[name] = m.sb(name, [P, tiles])
    for name in ("bn_scale", "bn_shift", "conv_b"):
        k[name] = m.sb(name, [P, 1])
    k["b1_row"] = m.sb("b1_row", [P, D])
    loaded = m.sem("loaded")
    with nc.Block() as block:
        @block.sync
        def _(sp):
            sp.dma_start(k["src"][:], src).then_inc(loaded, 16)
            sp.dma_start(k["dst"][:], dst).then_inc(loaded, 16)
            sp.dma_start(k["b1_row"][:], b1.rearrange("(a f) -> a f", a=1).to_broadcast([P, D])).then_inc(loaded, 16)
            sp.wait_ge(loaded, 48)

        @block.vector
        def _(dve):
            dve.tensor_tensor(k["conv_b"][:], k["gcn_b"][:], k["rs_b"][:], ALU.add)


def build(nc, nodes, x, src, dst, ends, heads, line, b1, weights, out):
    padded = x.shape[0]
    tiles, units, chunks = padded // P, padded // UNIT, src.shape[1]
    table = lambda name, shape: nc.dram_tensor(name, shape, F32).ap()
    y, x1, h = (table(n, [padded, D]) for n in ("messages", "x1", "h"))
    sums1, sums2 = (table(n, [padded + P, D]) for n in ("sums1", "sums2"))
    counts = table("counts", [padded + P, 1])
    outT = table("outT", [D, padded])
    with ExitStack() as stack:
        k = build_constants(nc, Memory(nc, stack, "k0"), weights)
        load_edges(nc, stack, src, dst, chunks, tiles, b1, k)
        rel_rows = table("rel_rows", [tiles, SLOTS])
        index_edges(nc, k, ends, heads, line, rel_rows, tiles)
        k["is_regular"] = nc.values_load(k["regular"][0:1, 0:1], min_val=0, max_val=1)
        k["irregular"] = nc.values_load(k["regular"][0:1, 1:2], min_val=0, max_val=1)
        count_slots(nc, k, tiles)
        clear_tables(nc, k, [sums1, sums2, counts])
        count_edges(nc, k, counts, chunks, padded, tiles)
        degrees(nc, k, tiles)
        make_messages(nc, k, x, y, units)
        add_messages(nc, k, y, sums1, chunks)
        convolve(nc, k, y, sums1, outT, units, nodes)
        embed(nc, k, x, outT, x1, h, units)
        attend(nc, k, x1, h, rel_rows, out, units)
        add_messages(nc, k, h, sums2, chunks, k)
        gate(nc, k, x1, h, sums2, out, units)


def kernel(**inputs):
    import concourse.bacc as bacc
    from concourse.bass_utils import run_bass_kernel_spmd

    nc = bacc.Bacc("TRN2", target_bir_lowering=False, num_devices=1)
    x = np.asarray(inputs["x"])
    nodes, edges = x.shape[0], inputs["src"].shape[0]
    padded = -(-nodes // (UNIT * RING)) * UNIT * RING
    chunks = -(-(edges + padded - nodes) // (2 * P)) * 2
    spare = chunks * P - edges
    arrays = {"x": np.zeros((padded, D), x.dtype)}
    arrays["x"][:nodes] = x
    loops = (nodes + np.arange(spare) * (padded - nodes) // spare).astype(np.int32)
    lines = {name: np.concatenate([np.asarray(inputs[name]), loops]) for name in ("src", "dst")}
    for name, ends in lines.items():
        arrays[name] = np.ascontiguousarray(ends.reshape(chunks, P).T)
    beyond = np.full((WINDOW_ROWS, 2 * HALF), padded, np.int32)
    arrays["ends"] = np.concatenate([np.hstack([lines["dst"].reshape(-1, HALF), lines["src"].reshape(-1, HALF)]), beyond])
    arrays["heads"] = np.ascontiguousarray(lines["dst"][::HALF])
    arrays["line"] = np.stack([lines["dst"], np.append(lines["dst"][1:], lines["dst"][-1:])])
    arrays["b1"] = np.asarray(inputs["L1_gnn_b1"])
    names = {**MATRICES, **VECTORS}
    for short, name in names.items():
        arrays[short] = np.ascontiguousarray(inputs[name])
    ap = {n: nc.dram_tensor(f"in_{n}", a.shape, mybir.dt.from_np(a.dtype), kind="ExternalInput").ap()
          for n, a in arrays.items()}
    out = nc.dram_tensor("out", (padded, D), F32, kind="ExternalOutput").ap()
    build(nc, nodes, ap["x"], ap["src"], ap["dst"], ap["ends"], ap["heads"], ap["line"], ap["b1"], {n: ap[n] for n in names}, out)
    result = run_bass_kernel_spmd(nc, [{f"in_{n}": a for n, a in arrays.items()}], core_ids=[0])
    return np.asarray(result.results[0]["out"])[:nodes]
```

```python
from contextlib import ExitStack

import numpy as np

import concourse.bass as bass
from concourse import mybir

P = 128
D = 128
TILES = 4
UNIT = TILES * P
RING = 4
EPS = 1e-5
SLOPE = 0.01

ALU = mybir.AluOpType
ACT = mybir.ActivationFunctionType
F32 = mybir.dt.float32
I32 = mybir.dt.int32


class Step:

    def __init__(self, lap, slot):
        self.lap, self.slot = lap, slot
        self.u = lap * RING + slot

    def back(self, lag):
        slot = self.slot - lag
        return Step(self.lap + slot // RING, slot % RING)


def over_units(eng, units, stages):
    stages = [(lag, stage, (more or [0])[0]) for lag, stage, *more in stages]
    peeled = RING * (1 + -(-max(lag for lag, _, _ in stages) // RING))
    last = max(lag + more for lag, _, more in stages)
    assert units % RING == 0 and units >= 2 * peeled
    for u in range(peeled):
        for lag, stage, _ in stages:
            if u >= lag:
                stage(Step(u // RING, u % RING).back(lag))
    with eng.Fori(peeled // RING, units // RING) as lap:
        for slot in range(RING):
            for lag, stage, _ in stages:
                stage(Step(lap, slot).back(lag))
    for u in range(units, units + last):
        for lag, stage, more in stages:
            if u - lag < units + more:
                stage(Step(u // RING, u % RING).back(lag))


def late(s, n):
    return not (isinstance(s.u, int) and s.u < n)


def over_pairs(eng, chunks, wanted):
    def run(body):
        with eng.If(wanted):
            body(0)
            with eng.Fori(1, chunks // 2) as pair:
                body(pair)
    return run


def not_first(n):
    return not (isinstance(n, int) and n == 0)


def before(s, n):
    return not (isinstance(s.u, int) and s.u >= n)


class Chain:

    def __init__(self, eng, sem, start):
        self.eng, self.sem, self.value, self.given = eng, sem, start, 0

    def mark(self, instruction):
        instruction.then_inc(self.sem, 1)
        self.given += 1
        self.value = self.value + 1

    def settle(self):
        self.eng.wait_ge(self.sem, self.value)


class Memory:

    def __init__(self, nc, stack, name):
        self.nc, self.stack, self.name, self.semaphores = nc, stack, name, []
        stack.callback(self.clear)

    def sb(self, name, shape, dtype=F32):
        return self.stack.enter_context(self.nc.sbuf_tensor(f"{self.name}_{name}", shape, dtype))

    def ps(self, name, shape, dtype=F32):
        return self.stack.enter_context(self.nc.psum_tensor(f"{self.name}_{name}", shape, dtype))

    def sem(self, name):
        self.semaphores.append(self.nc.alloc_semaphore(name=f"{self.name}_{name}"))
        return self.semaphores[-1]

    def sems(self, name, n):
        return [self.sem(f"{name}{i}") for i in range(n)]

    def clear(self):
        if self.semaphores:
            self.nc.clear_and_free_semaphores(self.semaphores)
            self.nc.all_engine_barrier()


NORM_STEPS = 10


def norm_stats(dve, chain, source, stats, small):
    for t in range(TILES):
        chain.mark(dve.bn_stats(stats[:, t, :], source[:, t, :]))
    chain.settle()
    chain.mark(dve.tensor_tensor(small[:, 0, :], stats[:, :, 1], stats[:, :, 4], ALU.add))
    chain.mark(dve.tensor_tensor(small[:, 1, :], stats[:, :, 1], stats[:, :, 4], ALU.subtract))
    chain.mark(dve.tensor_tensor(small[:, 2, :], stats[:, :, 2], stats[:, :, 5], ALU.add))
    chain.settle()
    chain.mark(dve.tensor_tensor(small[:, 1, :], small[:, 1, :], small[:, 1, :], ALU.mult))
    chain.mark(dve.tensor_scalar(small[:, 2, :], small[:, 2, :], 1.0 / D, EPS, ALU.mult, ALU.add))
    chain.settle()
    chain.mark(dve.scalar_tensor_tensor(small[:, 3, :], small[:, 1, :], 0.25, small[:, 2, :],
                                        ALU.mult, ALU.add))


MEANS, SQUARES, SMALLS = 3, 2, 6


class Norms:

    def __init__(self, dve, own, stats, small):
        self.dve, self.own, self.stats, self.small = dve, own, stats, small

    def means(self, j):
        stats, small = self.stats[:, j.slot % 2], self.small[:, j.slot % 2]
        for row, (a, b), op in ((0, (1, 4), ALU.add), (1, (1, 4), ALU.subtract), (2, (2, 5), ALU.add)):
            self.dve.tensor_tensor(small[:, row, :], stats[:, :, a], stats[:, :, b], op).then_inc(self.own, 1)

    def squares(self, j):
        small = self.small[:, j.slot % 2]
        self.dve.wait_ge(self.own, j.u * SMALLS + MEANS)
        self.dve.tensor_tensor(small[:, 1, :], small[:, 1, :], small[:, 1, :], ALU.mult).then_inc(self.own, 1)
        self.dve.tensor_scalar(small[:, 2, :], small[:, 2, :], 1.0 / D, EPS, ALU.mult, ALU.add).then_inc(self.own, 1)

    def variance(self, j):
        small = self.small[:, j.slot % 2]
        self.dve.wait_ge(self.own, j.u * SMALLS + MEANS + SQUARES)
        self.dve.scalar_tensor_tensor(small[:, 3, :], small[:, 1, :], 0.25, small[:, 2, :], ALU.mult, ALU.add).then_inc(self.own, 1)

    def shift(self, j):
        small = self.small[:, j.slot % 2]
        return self.dve.scalar_tensor_tensor(small[:, 5, :], small[:, 0, :], -0.5, small[:, 4, :], ALU.mult, ALU.mult)


APPLY_STEPS = 1 + TILES


def norm_apply(dve, chain, source, out, small):
    chain.mark(dve.scalar_tensor_tensor(small[:, 5, :], small[:, 0, :], -0.5, small[:, 4, :],
                                        ALU.mult, ALU.mult))
    chain.settle()
    for t in range(TILES):
        chain.mark(dve.tensor_scalar(out[:, t, :], source[:, t, :], small[:, 4, t:t + 1],
                                     small[:, 5, t:t + 1], ALU.mult, ALU.add))


def spread(column, width):
    return column.unsqueeze(2).to_broadcast([P, column.shape[1], width])


def by_unit(table):
    return table.rearrange("(u t p) f -> u p t f", t=TILES, p=P)


def build_constants(nc, memory, weights):
    m = Memory(nc, memory.stack, "c")
    ident = m.sb("ident", [P, P])
    earlier = m.sb("earlier", [P, P])
    trash = m.sb("trash", [P, 1])
    power = m.sb("power", [P, 2 * TILES])
    lane = m.sb("lane", [P, P])
    ones = m.sb("ones", [P, 1])
    held = {n: m.sb(n, [P, a.shape[1]]) for n, a in weights.items() if len(a.shape) == 2 and a.shape[0] == P}
    loaded, made = m.sem("loaded"), m.sem("made")
    for n, a in weights.items():
        if len(a.shape) == 1:
            held[n] = m.sb(n, [P, 1])
        elif a.shape[0] == 2 * P:
            held[n] = m.sb(n, [P, 2, a.shape[1]])
    with nc.Block() as block:
        @block.sync
        def _(sp):
            for n, a in weights.items():
                if len(a.shape) == 1 and a.shape[0] == 1:
                    src = a.rearrange("(a b) -> a b", a=1).to_broadcast([P, 1])
                elif len(a.shape) == 1:
                    src = a.rearrange("(a b) -> a b", b=1)
                elif a.shape[0] == 2 * P:
                    src = a.rearrange("(h p) f -> p h f", h=2)
                else:
                    src = a
                sp.dma_start(held[n][:], src).then_inc(loaded, 16)
            sp.wait_ge(loaded, 16 * len(weights))

        @block.vector
        def _(dve):
            dve.memset(power[:], -0.5)
            dve.memset(ones[:], 1.0)

        @block.gpsimd
        def _(pool):
            pool.memset(ident[:], 1.0).then_inc(made, 1)
            pool.memset(earlier[:], 1.0).then_inc(made, 1)
            pool.iota(trash[:], [[0, 1]], base=0, channel_multiplier=1,
                      allow_small_or_imprecise_dtypes=True).then_inc(made, 1)
            pool.iota(lane[:], [[1, P]], base=0, channel_multiplier=0, allow_small_or_imprecise_dtypes=True)
            pool.wait_ge(made, 3)
            pool.affine_select(out=ident[:], in_=ident[:], compare_op=ALU.is_equal, fill=0.0,
                               base=0, pattern=[[1, P]], channel_multiplier=-1)
            pool.affine_select(out=earlier[:], in_=earlier[:], compare_op=ALU.is_gt, fill=0.0,
                               base=0, pattern=[[-1, P]], channel_multiplier=1)
    return dict(held, ident=ident, earlier=earlier, trash=trash, power=power, lane=lane, ones=ones)


WINDOW_ROWS = 5
HALF = 64
WINDOW = WINDOW_ROWS * HALF
SLOTS = P
SRC_BITS = 17


def index_edges(nc, k, ends, heads, line, rel_rows, tiles):
    rows = heads.shape[0]
    per = next(q for q in range(P, 0, -1) if tiles % q == 0)
    batches = tiles // per
    span = line.shape[1] // P
    ROUND = 2 * batches + 1
    with ExitStack() as stack:
        m = Memory(nc, stack, "idx")
        head = m.sb("head", [per, rows], I32)
        below = m.sb("below", [per, rows])
        base = m.sb("base", [per, batches])
        start = m.sb("start", [per, batches])
        row_of = m.sb("row_of", [per, batches, WINDOW_ROWS], I32)
        window = m.sb("window", [per, batches, WINDOW_ROWS, 2 * HALF], I32)
        shape = [per, batches, WINDOW_ROWS, HALF]
        dstw, srcw, inside, after, loop, key = (m.sb(n, [per, batches, WINDOW]) for n in ("dstw", "srcw", "inside", "after", "loop", "key"))
        count = m.sb("count", [per, 4, batches])
        bad = m.sb("bad", [P, 4])
        top = m.sb("top", [per, batches, 8])
        keys = m.sb("keys", [per, batches, SLOTS])
        keys_int = m.sb("keys_int", [per, batches, SLOTS], I32)
        rel_out = m.sb("rel_out", [per, batches, SLOTS])
        slot_key = m.sb("slot_key", [P, batches, per], I32)
        order = m.sb("order", [P, 2, span], I32)
        orderf = m.sb("orderf", [P, span])
        turned = m.ps("turned", [P, -(-batches // 4) * 4, P])
        wrong = m.ps("wrong", [P, 512])
        loaded, based, started, gathered, own, round_own, passed, keys_turned, summed, rel_stored = (
            m.sem(n) for n in ("loaded", "based", "started", "gathered", "own", "round_own", "passed", "keys_turned", "summed", "rel_stored"))
        with nc.Block() as block:
            @block.sync
            def _(sp):
                sp.dma_start(head[:], heads.rearrange("(a r) -> a r", a=1).to_broadcast([per, rows])).then_inc(loaded, 16)
                for i in range(2):
                    sp.dma_start(order[:, i, :], line[i].rearrange("(p e) -> p e", p=P)).then_inc(loaded, 16)
                sp.wait_ge(summed, 1)
                sp.dma_start(rel_rows.rearrange("(b q) s -> q b s", q=per), rel_out[:]).then_inc(rel_stored, 16)
                sp.wait_ge(rel_stored, 16)

            @block.gpsimd
            def _(pool):
                pool.iota(base[:], [[per * P, batches]], base=0, channel_multiplier=P,
                          allow_small_or_imprecise_dtypes=True).then_inc(based, 1)
                pool.wait_ge(started, 1)
                for b in range(batches):
                    for r in range(WINDOW_ROWS):
                        pool.indirect_dma_start(out=window[:, b, r, :], out_offset=None, in_=ends,
                                                in_offset=bass.IndirectOffsetOnAxis(ap=row_of[:, b, r:r + 1], axis=0)
                                                ).then_inc(gathered, 16)

            @block.vector
            def _(dve):
                chain = Chain(dve, own, 0)

                def do(*instructions):
                    for instruction in instructions:
                        chain.mark(instruction)
                    chain.settle()

                dve.wait_ge(loaded, 48)
                dve.wait_ge(based, 1)
                do(dve.memset(bad[:], 0.0))
                do(dve.tensor_tensor(orderf[:], order[:, 1, :], order[:, 0, :], ALU.is_lt))
                do(dve.tensor_reduce(bad[:, 3:4], orderf[:], mybir.AxisListType.X, ALU.add))
                for b in range(batches):
                    do(dve.tensor_scalar(below[:], head[:], base[:, b:b + 1], None, ALU.is_lt))
                    do(dve.tensor_reduce(start[:, b:b + 1], below[:], mybir.AxisListType.X, ALU.add))
                do(dve.tensor_scalar(start[:], start[:], -1.0, 0.0, ALU.add, ALU.max))
                for r in range(WINDOW_ROWS):
                    last = dve.tensor_scalar(row_of[:, :, r], start[:], float(r), None, ALU.add)
                    chain.mark(last)
                chain.settle()
                dve.sem_inc(started, 1)
                dve.wait_ge(gathered, 16 * batches * WINDOW_ROWS)
                split = lambda ap: ap.rearrange("q b (r e) -> q b r e", e=HALF)
                for b in range(batches):
                    chain.mark(dve.tensor_copy(dstw[:, b].rearrange("q (r e) -> q r e", e=HALF), window[:, b, :, 0:HALF]))
                    chain.mark(dve.tensor_copy(srcw[:, b].rearrange("q (r e) -> q r e", e=HALF), window[:, b, :, HALF:2 * HALF]))
                chain.settle()
                do(dve.memset(after[:, :, WINDOW - 1:WINDOW], 0.0),
                   dve.tensor_tensor(after[:, :, 0:WINDOW - 1], dstw[:, :, 1:WINDOW], dstw[:, :, 0:WINDOW - 1], ALU.not_equal),
                   dve.tensor_tensor(loop[:], srcw[:], dstw[:], ALU.is_equal))
                do(dve.tensor_tensor(dstw[:], dstw[:], base[:].unsqueeze(2).to_broadcast([per, batches, WINDOW]), ALU.subtract))
                do(dve.tensor_tensor(loop[:], loop[:], after[:], ALU.mult))
                do(dve.tensor_scalar(inside[:], dstw[:], 0.0, None, ALU.is_ge),
                   dve.tensor_scalar(after[:], dstw[:], float(P), None, ALU.is_lt),
                   dve.scalar_tensor_tensor(key[:], dstw[:], float(1 << SRC_BITS), srcw[:], ALU.mult, ALU.add),
                   dve.tensor_scalar(count[:, 2, :], dstw[:, :, WINDOW - 1], float(P), None, ALU.is_lt))
                do(dve.tensor_tensor(inside[:], inside[:], after[:], ALU.mult))
                do(dve.tensor_tensor(loop[:], loop[:], inside[:], ALU.mult))
                do(dve.tensor_tensor(inside[:], inside[:], loop[:], ALU.subtract),
                   dve.tensor_reduce(count[:, 0, :], loop[:], mybir.AxisListType.X, ALU.add))
                do(dve.scalar_tensor_tensor(key[:], key[:], 1.0, inside[:], ALU.add, ALU.mult),
                   dve.tensor_reduce(count[:, 1, :], inside[:], mybir.AxisListType.X, ALU.add))
                do(dve.tensor_scalar(key[:], key[:], -1.0, None, ALU.add),
                   dve.tensor_scalar(count[:, 0, :], count[:, 0, :], float(P), None, ALU.not_equal),
                   dve.tensor_scalar(count[:, 1, :], count[:, 1, :], float(SLOTS), None, ALU.is_gt))
                do(dve.tensor_reduce(bad[0:per, 0:3], count[:, 0:3, :], mybir.AxisListType.X, ALU.add))

                def take(r):
                    start_of = r * ROUND
                    if not_first(r):
                        dve.wait_ge(round_own, start_of)
                        dve.sem_inc(passed, 1)
                    for b in range(batches):
                        dve.max(top[:, b, :], key[:, b, :]).then_inc(round_own, 1)
                    dve.wait_ge(round_own, start_of + batches)
                    dve.tensor_copy(keys[:, :, bass.ds(r * 8, 8)], top[:]).then_inc(round_own, 1)
                    for b in range(batches):
                        dve.match_replace(key[:, b, :], top[:, b, :], key[:, b, :], -1.0).then_inc(round_own, 1)

                take(0)
                with dve.Fori(1, SLOTS // 8) as r:
                    take(r)
                dve.wait_ge(round_own, SLOTS // 8 * ROUND)
                do(dve.tensor_copy(keys_int[:], keys[:]))
                do(dve.tensor_scalar(keys_int[:], keys_int[:], SRC_BITS, None, ALU.arith_shift_right))
                dve.tensor_copy(rel_out[:], keys_int[:]).then_inc(summed, 1)
                dve.wait_ge(keys_turned, 2)
                shaped = lambda ap: ap.rearrange("p (b q) -> p b q", q=per)
                do(dve.tensor_copy(slot_key[:], turned[:, 0:batches, 0:per]),
                   dve.tensor_scalar(k["regular"][0:1, 0:1], wrong[0:1, 0:1], 0.0, None, ALU.is_equal),
                   dve.tensor_scalar(k["regular"][0:1, 1:2], wrong[0:1, 0:1], 0.0, None, ALU.not_equal))
                do(dve.tensor_scalar(shaped(k["slot_src"][:]), slot_key[:], (1 << SRC_BITS) - 1, None, ALU.bitwise_and),
                   dve.tensor_scalar(slot_key[:], slot_key[:], SRC_BITS, None, ALU.arith_shift_right))
                do(dve.tensor_copy(shaped(k["slot_rel"][:]), slot_key[:]))

            @block.tensor
            def _(pe):
                pe.wait_ge(summed, 1)
                for b in range(batches):
                    last = pe.transpose(turned[:, b, 0:per], keys[:, b, :], k["ident"][0:per, 0:per])
                last.then_inc(keys_turned, 1)
                for c in range(4):
                    last = pe.matmul(wrong[0:1, 0:1], bad[:, c:c + 1], k["ones"][:], start=(c == 0), stop=(c == 3))
                last.then_inc(keys_turned, 1)


def count_slots(nc, k, tiles):
    with ExitStack() as stack:
        m = Memory(nc, stack, "cs")
        hot = m.sb("hot", [P, 2, 8, P], mybir.dt.bfloat16)
        one = m.sb("one", [P, 1], mybir.dt.bfloat16)
        rel = k["slot_rel"]
        sums = m.ps("sums", [P, -(-tiles // 512) * 512])
        hot_ready, summed, ready = m.sem("hot_ready"), m.sem("summed"), m.sem("ready")
        groups = tiles // 8
        with nc.Block() as block:
            @block.vector
            def _(dve):
                with dve.If(k["is_regular"]):
                    dve.memset(one[:], 1.0).then_inc(ready, 1)
                    for g in range(groups):
                        if g >= 2:
                            dve.wait_ge(summed, g - 1)
                        dve.tensor_tensor(hot[:, g % 2], k["lane"][:].unsqueeze(1).to_broadcast([P, 8, P]),
                                          spread(rel[:, g * 8:g * 8 + 8], P), ALU.is_equal).then_inc(hot_ready, 1)
                    dve.wait_ge(summed, groups)
                    dve.tensor_scalar(k["edges"][:], sums[:, 0:tiles], 1.0, None, ALU.add)

            @block.tensor
            def _(pe):
                with pe.If(k["is_regular"]):
                    pe.wait_ge(ready, 1)
                    for g in range(groups):
                        pe.wait_ge(hot_ready, g + 1)
                        for t in range(8):
                            last = pe.matmul(sums[:, g * 8 + t:g * 8 + t + 1], hot[:, g % 2, t, :], one[:], start=True, stop=True)
                        last.then_inc(summed, 1)


def clear_tables(nc, k, tables):
    WIDTH = 8 * D
    with ExitStack() as stack:
        m = Memory(nc, stack, "clear")
        zeros = m.sb("zeros", [P, WIDTH])
        cleared, stored = m.sem("cleared"), m.sem("stored")
        with nc.Block() as block:
            @block.vector
            def _(dve):
                dve.memset(zeros[:], 0.0).then_inc(cleared, 1)

            @block.sync
            def _(sp):
                with sp.If(k["irregular"]):
                    sp.wait_ge(cleared, 1)
                    stores = 0
                    for table in tables:
                        flat = table.rearrange("a b -> (a b)")
                        size = P * WIDTH
                        whole, rest = divmod(flat.shape[0], size)
                        for i in range(whole + (rest > 0)):
                            n = size if i < whole else rest
                            sp.dma_start(flat[i * size:i * size + n].rearrange("(p f) -> p f", p=P),
                                         zeros[:, 0:n // P]).then_inc(stored, 16)
                        stores += whole + (rest > 0)
                    sp.wait_ge(stored, 16 * stores)


def count_edges(nc, k, counts, chunks, rows, tiles):
    dst, place = k["dst"], k["place"]
    with ExitStack() as stack:
        m = Memory(nc, stack, "cnt")
        dstf = m.sb("dstf", [P, 2])
        same = m.sb("same", [P, 2, P])
        ranks = m.sb("ranks", [P, 2, P])
        small = m.sb("small", [P, 2, 4])
        total = m.sb("total", [P, 2])
        target = m.sb("target", [P, 2], I32)
        row = m.ps("row", [P, 2, 512])
        dst_ready, row_ready, own, fetched = (m.sem(n) for n in ("dst_ready", "row_ready", "own", "fetched"))
        added = m.sems("added", 2)
        passed = m.sem("passed")
        with nc.Block() as block:
            @block.vector
            def _(dve):
                @over_pairs(dve, chunks, k["irregular"])
                def _(pair):
                    for b in range(2):
                        c = pair * 2 + b
                        chain = Chain(dve, own, c * 8)
                        if not_first(pair):
                            dve.wait_ge(added[b], pair * 16)
                        dve.tensor_copy(dstf[:, b:b + 1], dst[:, bass.ds(c, 1)]).then_inc(dst_ready, 1)
                        dve.wait_ge(row_ready, c + 1)
                        dve.wait_ge(dst_ready, c + 1)
                        chain.mark(dve.tensor_scalar(same[:, b, :], row[:, b, 0:P], dstf[:, b:b + 1], None, ALU.is_equal))
                        chain.settle()
                        chain.mark(dve.tensor_reduce(total[:, b:b + 1], same[:, b, :], mybir.AxisListType.X, ALU.add))
                        chain.mark(dve.tensor_tensor(ranks[:, b, :], same[:, b, :], k["earlier"][:], ALU.mult))
                        chain.settle()
                        chain.mark(dve.tensor_reduce(small[:, b, 0:1], ranks[:, b, :], mybir.AxisListType.X, ALU.max))
                        chain.mark(dve.scalar_tensor_tensor(small[:, b, 1:2], k["trash"][:], float(rows), dstf[:, b:b + 1], ALU.add, ALU.subtract))
                        chain.settle()
                        chain.mark(dve.tensor_tensor(small[:, b, 2:3], small[:, b, 0:1], small[:, b, 1:2], ALU.mult))
                        chain.settle()
                        chain.mark(dve.tensor_tensor(target[:, b:b + 1], small[:, b, 2:3], dstf[:, b:b + 1], ALU.add))
                        chain.settle()
                        chain.mark(dve.tensor_copy(place[:, bass.ds(c, 1)], target[:, b:b + 1]))

            @block.tensor
            def _(pe):
                @over_pairs(pe, chunks, k["irregular"])
                def _(pair):
                    for b in range(2):
                        c = pair * 2 + b
                        pe.wait_ge(dst_ready, c + 1)
                        pe.matmul(row[:, b, 0:P], dstf[:, b:b + 1].to_broadcast([P, P]), k["ident"][:],
                                  start=True, stop=True).then_inc(row_ready, 1)

            @block.gpsimd
            def _(pool):
                @over_pairs(pool, chunks, k["irregular"])
                def _(pair):
                    for b in range(2):
                        pool.wait_ge(own, (pair * 2 + b + 1) * 8)
                        if b or not_first(pair):
                            pool.wait_ge(added[1 - b], (pair + b) * 16)
                        pool.sem_inc(passed, 1)
                        pool.indirect_dma_start(
                            out=counts, out_offset=bass.IndirectOffsetOnAxis(ap=target[:, b:b + 1], axis=0),
                            in_=total[:, b:b + 1], in_offset=None, compute_op=ALU.add).then_inc(added[b], 16)
                with pool.If(k["irregular"]):
                    for b in range(2):
                        pool.wait_ge(added[b], chunks // 2 * 16)

            @block.sync
            def _(sp):
                with sp.If(k["irregular"]):
                    for b in range(2):
                        sp.wait_ge(added[b], chunks // 2 * 16)
                    sp.dma_start(k["edges"][:], counts[0:tiles * P, :].rearrange("(t p) o -> p (t o)", p=P),
                                 allow_slow_non_contiguous=True).then_inc(fetched, 16)
                    sp.wait_ge(fetched, 16)


def degrees(nc, k, tiles):
    with ExitStack() as stack:
        m = Memory(nc, stack, "deg")
        counted, rooted = m.sem("counted"), m.sem("rooted")
        with nc.Block() as block:
            @block.vector
            def _(dve):
                dve.tensor_scalar(k["edges"][:], k["edges"][:], 1.0, 1.0, ALU.add, ALU.max).then_inc(counted, 1)
                dve.wait_ge(rooted, 1)
                dve.reciprocal(k["dinv"][:], k["root"][:])

            @block.scalar
            def _(act):
                act.wait_ge(counted, 1)
                act.activation(k["root"][:], k["edges"][:], ACT.Sqrt).then_inc(rooted, 1)


def make_messages(nc, k, x, y, units):
    X, Y = by_unit(x), by_unit(y)
    with ExitStack() as stack:
        m = Memory(nc, stack, "msg")
        x_in = m.sb("x_in", [P, RING, TILES, D])
        stats = m.sb("stats", [P, 2, TILES, 6])
        small = m.sb("small", [P, 2, 6, TILES])
        xn = m.sb("xn", [P, 2, TILES, D])
        xlT = m.sb("xlT", [P, 2, UNIT])
        y_out = m.sb("y_out", [P, RING, TILES, D])
        turned, back = (m.ps(n, [P, 2, UNIT]) for n in ("turned", "back"))
        x_loaded, y_stored = m.sems("x_loaded", RING), m.sems("y_stored", RING)
        measured, own, rooted, inverted, shifted, xn_ready, turned_ready, xlT_ready, back_ready, y_ready = (
            m.sem(n) for n in ("measured", "own", "rooted", "inverted", "shifted", "xn_ready", "turned_ready", "xlT_ready",
                               "back_ready", "y_ready"))
        with nc.Block() as block:
            @block.sync
            def _(sp):
                def load(s):
                    if late(s, RING):
                        sp.wait_ge(xn_ready, s.u - RING + 1)
                    sp.dma_start(x_in[:, s.slot], X[s.u]).then_inc(x_loaded[s.slot], 16)

                def store(s):
                    sp.wait_ge(y_ready, s.u + 1)
                    sp.dma_start(Y[s.u], y_out[:, s.slot]).then_inc(y_stored[s.slot], 16)

                over_units(sp, units, [(0, load), (5, store)])
                for q in y_stored:
                    sp.wait_ge(q, units // RING * 16)

            @block.vector
            def _(dve):
                norms = Norms(dve, own, stats, small)

                def measure(s, half):
                    if half == 0:
                        dve.wait_ge(x_loaded[s.slot], (s.lap + 1) * 16)
                    for t in range(2 * half, 2 * half + 2):
                        last = dve.bn_stats(stats[:, s.slot % 2, t, :], x_in[:, s.slot, t, :])
                    if half:
                        last.then_inc(measured, 1)

                def means(s):
                    dve.wait_ge(measured, s.u + 1)
                    if late(s, 2):
                        dve.wait_ge(xn_ready, s.u - 1)
                    norms.means(s)

                def invert(s):
                    b = s.slot % 2
                    dve.wait_ge(rooted, s.u + 1)
                    dve.reciprocal(small[:, b, 4, :], small[:, b, 4, :]).then_inc(inverted, 1)

                def shift(s):
                    dve.wait_ge(inverted, s.u + 1)
                    norms.shift(s).then_inc(shifted, 1)

                def scale(s):
                    dve.wait_ge(back_ready, s.u + 1)
                    if late(s, RING):
                        dve.wait_ge(y_stored[s.slot], s.lap * 16)
                    dve.tensor_tensor(y_out[:, s.slot], back[:, s.slot % 2].rearrange("p (t f) -> p t f", t=TILES),
                                      spread(k["dinv"][:, bass.ds(s.u * TILES, TILES)], D), ALU.mult).then_inc(y_ready, 1)

                over_units(dve, units, [(1, means), (3, scale), (1, norms.squares), (0, lambda s: measure(s, 0)),
                                        (1, norms.variance), (0, lambda s: measure(s, 1)), (1, invert), (1, shift)])

            @block.tensor
            def _(pe):
                def turn(s):
                    b = s.slot % 2
                    pe.wait_ge(xn_ready, s.u + 1)
                    if late(s, 2):
                        pe.wait_ge(xlT_ready, s.u - 1)
                    for t in range(TILES):
                        last = pe.transpose(turned[:, b, t * P:(t + 1) * P], xn[:, b, t, :], k["ident"][:])
                    last.then_inc(turned_ready, 1)

                def turn_back(s):
                    b = s.slot % 2
                    pe.wait_ge(xlT_ready, s.u + 1)
                    if late(s, 2):
                        pe.wait_ge(y_ready, s.u - 1)
                    for t in range(TILES):
                        last = pe.transpose(back[:, b, t * P:(t + 1) * P], xlT[:, b, t * P:(t + 1) * P], k["ident"][:])
                    last.then_inc(back_ready, 1)

                over_units(pe, units, [(3, turn_back), (2, turn)])

            @block.scalar
            def _(act):
                def root(s):
                    b = s.slot % 2
                    act.wait_ge(own, (s.u + 1) * SMALLS)
                    act.activation(small[:, b, 4, :], small[:, b, 3, :], ACT.Sqrt).then_inc(rooted, 1)

                def apply(s):
                    b = s.slot % 2
                    act.wait_ge(shifted, s.u + 1)
                    if late(s, 2):
                        act.wait_ge(turned_ready, s.u - 1)
                    for t in range(TILES):
                        last = act.activation(xn[:, b, t, :], x_in[:, s.slot, t, :], ACT.Identity, bias=small[:, b, 5, t:t + 1],
                                              scale=small[:, b, 4, t:t + 1])
                    last.then_inc(xn_ready, 1)

                def affine(s):
                    b = s.slot % 2
                    act.wait_ge(turned_ready, s.u + 1)
                    if late(s, 2):
                        act.wait_ge(back_ready, s.u - 1)
                    act.activation(xlT[:, b], turned[:, b], ACT.Identity, bias=k["ln_b"][:], scale=k["ln_g"][:]).then_inc(xlT_ready, 1)

                over_units(act, units, [(1, root), (2, affine), (1, apply)])


def add_messages(nc, k, y, sums, chunks, edge_net=None):
    src, dst, place = k["src"], k["dst"], k["place"]
    with ExitStack() as stack:
        m = Memory(nc, stack, "add1" if edge_net is None else "add2")
        dstf = m.sb("dstf", [P, 2])
        src_row, dst_row, target = (m.sb(n, [P, 2], I32) for n in ("src_row", "dst_row", "target"))
        same = m.sb("same", [P, 2, P])
        from_src = m.sb("from_src", [P, 2, D])
        from_dst = m.sb("from_dst", [P, 2, D])
        bothT = m.sb("bothT", [P, 2, 2, P])
        hidden = m.sb("hidden", [P, 2, P])
        weight = m.sb("weight", [P, 2])
        message = m.sb("message", [P, 2, D])
        out = m.sb("out", [P, 2, D])
        row = m.ps("row", [P, 2, 512])
        total = m.ps("total", [P, 2, 512])
        turned = m.ps("turned", [P, 512])
        pre = m.ps("pre", [P, 512])
        dots = m.ps("dots", [P, 512])
        (index_ready, row_ready, same_ready, total_ready, out_ready, turned_ready, bothT_ready, pre_ready,
         hidden_ready, dot_ready, weight_ready, message_ready) = (
            m.sem(n) for n in ("index_ready", "row_ready", "same_ready", "total_ready", "out_ready", "turned_ready",
                               "bothT_ready", "pre_ready", "hidden_ready", "dot_ready", "weight_ready", "message_ready"))
        src_in, dst_in, added = m.sems("src_in", 2), m.sems("dst_in", 2), m.sems("added", 2)
        passed = m.sem("passed")

        def over_chunks(eng, body):
            @over_pairs(eng, chunks, k["irregular"])
            def _(pair):
                for b in range(2):
                    body(pair, b, pair * 2 + b)

        with nc.Block() as block:
            @block.vector
            def _(dve):
                def chunk(pair, b, c):
                    if not_first(pair):
                        dve.wait_ge(added[b], pair * 16)
                    dve.tensor_copy(dstf[:, b:b + 1], dst[:, bass.ds(c, 1)]).then_inc(index_ready, 1)
                    dve.tensor_copy(src_row[:, b:b + 1], src[:, bass.ds(c, 1)]).then_inc(index_ready, 1)
                    dve.tensor_copy(dst_row[:, b:b + 1], dst[:, bass.ds(c, 1)]).then_inc(index_ready, 1)
                    dve.tensor_copy(target[:, b:b + 1], place[:, bass.ds(c, 1)]).then_inc(index_ready, 1)
                    dve.wait_ge(row_ready, c + 1)
                    dve.wait_ge(index_ready, (c + 1) * 4)
                    dve.tensor_scalar(same[:, b, :], row[:, b, 0:P], dstf[:, b:b + 1], None, ALU.is_equal).then_inc(same_ready, 1)
                    if edge_net is not None:
                        dve.wait_ge(weight_ready, c + 1)
                        dve.wait_ge(src_in[b], (pair + 1) * 16)
                        dve.tensor_scalar(message[:, b, :], from_src[:, b, :], weight[:, b:b + 1], None, ALU.mult).then_inc(message_ready, 1)

                over_chunks(dve, chunk)

            @block.gpsimd
            def _(pool):
                @over_pairs(pool, chunks, k["irregular"])
                def _(pair):
                    for b in range(2):
                        pool.wait_ge(index_ready, (pair * 2 + b + 1) * 4)
                        pool.sem_inc(passed, 1)
                        pool.indirect_dma_start(out=from_src[:, b, :], out_offset=None, in_=y,
                                                in_offset=bass.IndirectOffsetOnAxis(ap=src_row[:, b:b + 1], axis=0)
                                                ).then_inc(src_in[b], 16)
                        if edge_net is not None:
                            pool.indirect_dma_start(out=from_dst[:, b, :], out_offset=None, in_=y,
                                                    in_offset=bass.IndirectOffsetOnAxis(ap=dst_row[:, b:b + 1], axis=0)
                                                    ).then_inc(dst_in[b], 16)
                    for b in range(2):
                        pool.wait_ge(out_ready, pair * 2 + b + 1)
                        if b or not_first(pair):
                            pool.wait_ge(added[1 - b], (pair + b) * 16)
                        pool.sem_inc(passed, 1)
                        pool.indirect_dma_start(
                            out=sums, out_offset=bass.IndirectOffsetOnAxis(ap=target[:, b:b + 1], axis=0),
                            in_=out[:, b, :], in_offset=None, compute_op=ALU.add).then_inc(added[b], 16)
                with pool.If(k["irregular"]):
                    for b in range(2):
                        pool.wait_ge(added[b], chunks // 2 * 16)

            @block.tensor
            def _(pe):
                def chunk(pair, b, c):
                    pe.wait_ge(index_ready, c * 4 + 1)
                    pe.matmul(row[:, b, 0:P], dstf[:, b:b + 1].to_broadcast([P, P]), k["ident"][:],
                              start=True, stop=True).then_inc(row_ready, 1)
                    pe.wait_ge(src_in[b], (pair + 1) * 16)
                    if edge_net is not None:
                        pe.wait_ge(dst_in[b], (pair + 1) * 16)
                        if not_first(c):
                            pe.wait_ge(bothT_ready, c)
                        pe.transpose(turned[:, 0:P], from_src[:, b, :], k["ident"][:])
                        pe.transpose(turned[:, P:2 * P], from_dst[:, b, :], k["ident"][:]).then_inc(turned_ready, 1)
                        pe.wait_ge(bothT_ready, c + 1)
                        if not_first(c):
                            pe.wait_ge(hidden_ready, c)
                        for half in range(2):
                            last = pe.matmul(pre[:, 0:P], edge_net["We1"][:, half, :], bothT[:, b, half, :],
                                             start=(half == 0), stop=(half == 1))
                        last.then_inc(pre_ready, 1)
                        pe.wait_ge(hidden_ready, c + 1)
                        if not_first(c):
                            pe.wait_ge(weight_ready, c)
                        pe.matmul(dots[:, 0:1], hidden[:, b, :], edge_net["We2"][:], start=True, stop=True).then_inc(dot_ready, 1)
                        pe.wait_ge(message_ready, c + 1)
                    pe.wait_ge(same_ready, c + 1)
                    pe.matmul(total[:, b, 0:D], same[:, b, :], from_src[:, b, :] if edge_net is None else message[:, b, :],
                              start=True, stop=True).then_inc(total_ready, 1)

                over_chunks(pe, chunk)

            @block.scalar
            def _(act):
                def chunk(pair, b, c):
                    if edge_net is not None:
                        act.wait_ge(turned_ready, c + 1)
                        act.activation(bothT[:, b].rearrange("p a b -> p (a b)"), turned[:, 0:2 * P], ACT.Copy).then_inc(bothT_ready, 1)
                        act.wait_ge(pre_ready, c + 1)
                        act.activation(hidden[:, b, :], pre[:, 0:P], ACT.Relu, bias=edge_net["be1"][:]).then_inc(hidden_ready, 1)
                        act.wait_ge(dot_ready, c + 1)
                        act.activation(weight[:, b:b + 1], dots[:, 0:1], ACT.Sigmoid, bias=edge_net["be2"][:]).then_inc(weight_ready, 1)
                    act.wait_ge(total_ready, c + 1)
                    act.activation(out[:, b, :], total[:, b, 0:D], ACT.Copy).then_inc(out_ready, 1)

                over_chunks(act, chunk)


def convolve(nc, k, y, sums, outT, units, nodes):
    Y, SUMS = by_unit(y), by_unit(sums[0:units * UNIT, :])
    STAT_OWN = 4
    last_valid = nodes - (units - 1) * UNIT
    with ExitStack() as stack:
        m = Memory(nc, stack, "conv")
        y_in = m.sb("y_in", [P, RING, TILES, D])
        s_in = m.sb("s_in", [P, RING, TILES, D])
        gathered = m.sb("gathered", [P, 2, TILES, D])
        rows = m.sb("rows", [P, RING, TILES, D])
        hot = m.sb("hot", [P, 2, TILES, P])
        slot_src = m.sb("slot_src", [P, RING, TILES], I32)
        sum_ps = m.ps("sum_ps", [P, 2, UNIT])
        rows_loaded = m.sems("rows_loaded", RING)
        (rows_clear, slots_ready, hot_ready, sums_ready, passed) = (
            m.sem(n) for n in ("rows_clear", "slots_ready", "hot_ready", "sums_ready", "passed"))
        own_x = m.sb("own_x", [P, 2, TILES, D])
        gT = m.sb("gT", [P, 2, UNIT])
        xT = m.sb("xT", [P, 2, UNIT])
        o_out = m.sb("o_out", [P, RING, UNIT])
        stats = m.sb("stats", [P, units, 6])
        bn = m.sb("bn", [P, 8])
        g_turned, x_turned, o_ps = (m.ps(n, [P, 2, UNIT]) for n in ("g_turned", "x_turned", "o_ps"))
        y_loaded, s_loaded, o_stored = (m.sems(n, RING) for n in ("y_loaded", "s_loaded", "o_stored"))
        summed, scaled, turned, copied, product, o_ready, measured, bn_own, bn_var, bn_rstd = (
            m.sem(n) for n in ("summed", "scaled", "turned", "copied", "product", "o_ready", "measured", "bn_own", "bn_var", "bn_rstd"))
        with nc.Block() as block:
            @block.sync
            def _(sp):
                def load(s):
                    if late(s, RING):
                        sp.wait_ge(scaled, (s.u - RING + 1) * 2)
                    sp.dma_start(y_in[:, s.slot], Y[s.u]).then_inc(y_loaded[s.slot], 16)

                def load_both(s):
                    load(s)
                    sp.dma_start(s_in[:, s.slot], SUMS[s.u]).then_inc(s_loaded[s.slot], 16)

                def store(s):
                    sp.wait_ge(o_ready, s.u + 1)
                    sp.dma_start(outT[:, bass.ds(s.u * UNIT, UNIT)], o_out[:, s.slot]).then_inc(o_stored[s.slot], 16)

                with sp.If(k["is_regular"]):
                    over_units(sp, units, [(4, store), (0, load)])
                with sp.If(k["irregular"]):
                    over_units(sp, units, [(4, store), (0, load_both)])
                for q in o_stored:
                    sp.wait_ge(q, units // RING * 16)

            @block.vector
            def _(dve):
                def one_hot(s):
                    if late(s, 2):
                        dve.wait_ge(sums_ready, s.u - 1)
                    dve.tensor_tensor(hot[:, s.slot % 2], k["lane"][:].unsqueeze(1).to_broadcast([P, TILES, P]),
                                      spread(k["slot_rel"][:, bass.ds(s.u * TILES, TILES)], P), ALU.is_equal).then_inc(hot_ready, 1)

                def scale_made(s):
                    dve.wait_ge(y_loaded[s.slot], (s.lap + 1) * 16)
                    dve.wait_ge(sums_ready, s.u + 1)
                    if late(s, RING):
                        dve.wait_ge(scaled, (s.u - RING + 1) * 2)
                    dve.scalar_tensor_tensor(s_in[:, s.slot], y_in[:, s.slot], 2.0,
                                             sum_ps[:, s.slot % 2].rearrange("p (t f) -> p t f", t=TILES), ALU.mult, ALU.add).then_inc(summed, 1)
                    scale(s)

                def scale_read(s):
                    dve.wait_ge(y_loaded[s.slot], (s.lap + 1) * 16)
                    dve.wait_ge(s_loaded[s.slot], (s.lap + 1) * 16)
                    dve.tensor_tensor(s_in[:, s.slot], s_in[:, s.slot], y_in[:, s.slot], ALU.add).then_inc(summed, 1)
                    scale(s)

                def scale(s):
                    b = s.slot % 2
                    if late(s, 2):
                        dve.wait_ge(turned, s.u - 1)
                    dve.tensor_tensor(own_x[:, b], y_in[:, s.slot], spread(k["root"][:, bass.ds(s.u * TILES, TILES)], D),
                                      ALU.mult).then_inc(scaled, 1)
                    dve.wait_ge(summed, s.u + 1)
                    dve.tensor_tensor(gathered[:, b], s_in[:, s.slot], spread(k["dinv"][:, bass.ds(s.u * TILES, TILES)], D),
                                      ALU.mult).then_inc(scaled, 1)

                def measure(s):
                    dve.wait_ge(o_ready, s.u + 1)
                    dve.bn_stats(stats[:, bass.ds(s.u, 1), :].rearrange("p a b -> p (a b)"), o_out[:, s.slot]).then_inc(measured, 1)

                with dve.If(k["is_regular"]):
                    dve.memset(rows[:], 0.0).then_inc(rows_clear, 1)
                    over_units(dve, units, [(0, one_hot), (2, scale_made), (5, measure)])
                with dve.If(k["irregular"]):
                    over_units(dve, units, [(2, measure), (0, scale_read)])
                dve.wait_ge(measured, units)
                dve.bn_stats(stats[:, units - 1, :], o_out[:, RING - 1, 0:last_valid]).then_inc(bn_own, 1)
                dve.wait_ge(bn_own, 1)
                dve.bn_aggr(bn[:, 0:2], stats[:].rearrange("p a b -> p (a b)")).then_inc(bn_own, 1)
                dve.wait_ge(bn_own, 2)
                dve.tensor_scalar(bn[:, 2:3], bn[:, 1:2], EPS, None, ALU.add).then_inc(bn_var, 1)
                dve.wait_ge(bn_rstd, 1)
                dve.tensor_tensor(k["bn_scale"][:], bn[:, 3:4], k["bn_g"][:], ALU.mult).then_inc(bn_own, 1)
                dve.wait_ge(bn_own, 3)
                dve.tensor_tensor(bn[:, 4:5], bn[:, 0:1], k["bn_scale"][:], ALU.mult).then_inc(bn_own, 1)
                dve.wait_ge(bn_own, 4)
                dve.tensor_tensor(k["bn_shift"][:], k["bn_b"][:], bn[:, 4:5], ALU.subtract)

            @block.gpsimd
            def _(pool):
                def gather(s):
                    if late(s, RING):
                        pool.wait_ge(rows_loaded[s.slot], s.lap * 16 * TILES)
                        pool.wait_ge(sums_ready, s.u - RING + 1)
                    pool.tensor_copy(slot_src[:, s.slot, :], k["slot_src"][:, bass.ds(s.u * TILES, TILES)]).then_inc(slots_ready, 1)
                    pool.wait_ge(slots_ready, s.u + 1)
                    pool.sem_inc(passed, 1)
                    for t in range(TILES):
                        pool.indirect_dma_start(out=rows[:, s.slot, t, :], out_offset=None, in_=y,
                                                in_offset=bass.IndirectOffsetOnAxis(ap=slot_src[:, s.slot, t:t + 1], axis=0),
                                                bounds_check=units * UNIT - 1, oob_is_err=False).then_inc(rows_loaded[s.slot], 16)

                with pool.If(k["is_regular"]):
                    pool.wait_ge(rows_clear, 1)
                    over_units(pool, units, [(0, gather)])
                pool.wait_ge(bn_var, 1)
                pool.tensor_tensor(bn[:, 3:4], bn[:, 2:3], k["power"][:, 0:1], ALU.pow).then_inc(bn_rstd, 1)

            @block.tensor
            def _(pe):
                def turn(s):
                    b = s.slot % 2
                    pe.wait_ge(scaled, (s.u + 1) * 2)
                    if late(s, 2):
                        pe.wait_ge(copied, (s.u - 1) * 2)
                    for t in range(TILES):
                        pe.transpose(g_turned[:, b, t * P:(t + 1) * P], gathered[:, b, t, :], k["ident"][:])
                        last = pe.transpose(x_turned[:, b, t * P:(t + 1) * P], own_x[:, b, t, :], k["ident"][:])
                    last.then_inc(turned, 1)

                def multiply(s):
                    b = s.slot % 2
                    pe.wait_ge(copied, (s.u + 1) * 2)
                    if late(s, 2):
                        pe.wait_ge(o_ready, s.u - 1)
                    pe.matmul(o_ps[:, b], k["gcn_w"][:], gT[:, b], start=True, stop=False)
                    pe.matmul(o_ps[:, b], k["rs_w"][:], xT[:, b], start=False, stop=True).then_inc(product, 1)

                def gather_sums(s):
                    b = s.slot % 2
                    pe.wait_ge(hot_ready, s.u + 1)
                    pe.wait_ge(rows_loaded[s.slot], (s.lap + 1) * 16 * TILES)
                    if late(s, 2):
                        pe.wait_ge(summed, s.u - 1)
                    for t in range(TILES):
                        last = pe.matmul(sum_ps[:, b, t * P:(t + 1) * P], hot[:, b, t, :], rows[:, s.slot, t, :], start=True, stop=True)
                    last.then_inc(sums_ready, 1)

                with pe.If(k["is_regular"]):
                    over_units(pe, units, [(0, gather_sums), (3, multiply), (2, turn)])
                with pe.If(k["irregular"]):
                    over_units(pe, units, [(1, multiply), (0, turn)])

            @block.scalar
            def _(act):
                def copy(s):
                    b = s.slot % 2
                    act.wait_ge(turned, s.u + 1)
                    if late(s, 2):
                        act.wait_ge(product, s.u - 1)
                    act.activation(gT[:, b], g_turned[:, b], ACT.Copy).then_inc(copied, 1)
                    act.activation(xT[:, b], x_turned[:, b], ACT.Copy).then_inc(copied, 1)

                def bias(s):
                    b = s.slot % 2
                    act.wait_ge(product, s.u + 1)
                    if late(s, RING):
                        act.wait_ge(o_stored[s.slot], s.lap * 16)
                        act.wait_ge(measured, s.u - RING + 1)
                    act.activation(o_out[:, s.slot], o_ps[:, b], ACT.Identity, bias=k["conv_b"][:]).then_inc(o_ready, 1)

                over_units(act, units, [(1, bias), (0, copy)])


def embed(nc, k, x, outT, x1, h, units):
    X, X1, H = by_unit(x), by_unit(x1), by_unit(h)
    NEXT = 3
    with ExitStack() as stack:
        m = Memory(nc, stack, "emb")
        x_in = m.sb("x_in", [P, RING, TILES, D])
        o_in = m.sb("o_in", [P, RING, UNIT])
        bnT, leaky = (m.sb(n, [P, 2, UNIT]) for n in ("bnT", "leaky"))
        mixed, hidden, hn, centred = (m.sb(n, [P, 2, TILES, D]) for n in ("mixed", "hidden", "hn", "centred"))
        stats = m.sb("stats", [P, 2, 2 * TILES, 6])
        small = m.sb("small", [P, 2, 6, 2 * TILES])
        x1_out, h_out = (m.sb(n, [P, RING, TILES, D]) for n in ("x1_out", "h_out"))
        x1T, hT, pair_hidden = (m.sb(n, [P, 2, UNIT]) for n in ("x1T", "hT", "pair_hidden"))
        leaky_ps = m.ps("leaky_ps", [P, 2, UNIT])
        x1_turned, w1_ps, h_turned, h_back, pair_ps, dots = (
            m.ps(n, [P, UNIT]) for n in ("x1_turned", "w1_ps", "h_turned", "h_back", "pair_ps", "dots"))
        x_loaded, o_loaded, x1_stored, h_stored = (m.sems(n, RING) for n in ("x_loaded", "o_loaded", "x1_stored", "h_stored"))
        (cleared, bn_ready, leaky_ready, leaky_turned, mixed_ready, measured1, measured2, own, rooted, inverted, shifted,
         x1_ready, x1_turn_ready, x1T_ready, w1_ready, hidden_ready, centred_ready, hn_ready, h_turn_ready, hT_ready,
         h_back_ready, h_ready, pair_product, pair_ready, dot_product, dot_kept) = (
            m.sem(n) for n in ("cleared", "bn_ready", "leaky_ready", "leaky_turned", "mixed_ready", "measured1",
                               "measured2", "own", "rooted", "inverted", "shifted", "x1_ready", "x1_turn_ready", "x1T_ready",
                               "w1_ready", "hidden_ready", "centred_ready", "hn_ready", "h_turn_ready", "hT_ready",
                               "h_back_ready", "h_ready", "pair_product", "pair_ready", "dot_product", "dot_kept"))
        tiled = lambda ap: ap.rearrange("p (t f) -> p t f", t=TILES)
        with nc.Block() as block:
            @block.sync
            def _(sp):
                def load(s):
                    if late(s, RING):
                        sp.wait_ge(mixed_ready, s.u - RING + 1)
                        sp.wait_ge(bn_ready, s.u - RING + 1)
                    sp.dma_start(x_in[:, s.slot], X[s.u]).then_inc(x_loaded[s.slot], 16)
                    sp.dma_start(o_in[:, s.slot], outT[:, bass.ds(s.u * UNIT, UNIT)]).then_inc(o_loaded[s.slot], 16)

                def store_x1(s):
                    sp.wait_ge(x1_ready, s.u + 1)
                    sp.dma_start(X1[s.u], x1_out[:, s.slot]).then_inc(x1_stored[s.slot], 16)

                def store_h(s):
                    sp.wait_ge(h_ready, s.u + 1)
                    sp.dma_start(H[s.u], h_out[:, s.slot]).then_inc(h_stored[s.slot], 16)

                over_units(sp, units, [(0, load), (5, store_x1), (10, store_h)])
                for q in x1_stored + h_stored:
                    sp.wait_ge(q, units // RING * 16)

            @block.scalar
            def _(act):
                def affine(s):
                    act.wait_ge(h_turn_ready, s.u + 1)
                    if late(s, 2):
                        act.wait_ge(h_back_ready, s.u - 1)
                        act.wait_ge(pair_product, s.u - 1)
                    act.activation(hT[:, s.slot % 2], h_turned[:], ACT.Relu, bias=k["bt1"][:], scale=k["g1"][:]).then_inc(hT_ready, 1)

                def copy_h(s):
                    act.wait_ge(h_back_ready, s.u + 1)
                    if late(s, RING):
                        act.wait_ge(h_stored[s.slot], s.lap * 16)
                    act.activation(h_out[:, s.slot], tiled(h_back[:]), ACT.Copy).then_inc(h_ready, 1)

                def pair(s):
                    act.wait_ge(pair_product, s.u + 1)
                    if late(s, 2):
                        act.wait_ge(dot_product, s.u - 1)
                    act.activation(pair_hidden[:, s.slot % 2], pair_ps[:], ACT.Relu, bias=k["be1"][:]).then_inc(pair_ready, 1)

                def root(j):
                    b = j.slot % 2
                    act.wait_ge(own, (j.u + 1) * SMALLS)
                    act.activation(small[:, b, 4, :], small[:, b, 3, :], ACT.Sqrt).then_inc(rooted, 1)

                def copy_x1(s):
                    act.wait_ge(x1_turn_ready, s.u + 1)
                    if late(s, 2):
                        act.wait_ge(w1_ready, s.u - 1)
                    act.activation(x1T[:, s.slot % 2], x1_turned[:], ACT.Copy).then_inc(x1T_ready, 1)

                def normalise(s):
                    act.wait_ge(o_loaded[s.slot], (s.lap + 1) * 16)
                    if late(s, 2):
                        act.wait_ge(leaky_ready, s.u - 1)
                    act.activation(bnT[:, s.slot % 2], o_in[:, s.slot], ACT.Identity, bias=k["bn_shift"][:],
                                   scale=k["bn_scale"][:]).then_inc(bn_ready, 1)

                def apply1(s):
                    b = s.slot % 2
                    act.wait_ge(shifted, s.u + 1)
                    if late(s, RING):
                        act.wait_ge(x1_stored[s.slot], s.lap * 16)
                        act.wait_ge(x1_turn_ready, s.u - RING + 1)
                    for t in range(TILES):
                        last = act.activation(x1_out[:, s.slot, t, :], mixed[:, b, t, :], ACT.Identity,
                                              bias=small[:, b, 5, t:t + 1], scale=small[:, b, 4, t:t + 1])
                    last.then_inc(x1_ready, 1)

                over_units(act, units, [(7, affine), (8, copy_h), (8, pair), (3, root, NEXT), (4, copy_x1), (0, normalise),
                                        (3, apply1)])

            @block.vector
            def _(dve):
                norms = Norms(dve, own, stats, small)

                def hide(s):
                    dve.wait_ge(w1_ready, s.u + 1)
                    if late(s, 2):
                        dve.wait_ge(centred_ready, s.u - 1)
                    dve.tensor_tensor(hidden[:, s.slot % 2], tiled(w1_ps[:]), k["b1_row"][:].unsqueeze(1).to_broadcast([P, TILES, D]),
                                      ALU.add).then_inc(hidden_ready, 1)

                def means(j):
                    if before(j, units):
                        dve.wait_ge(measured1, j.u + 1)
                    if late(j, NEXT):
                        dve.wait_ge(measured2, j.u - NEXT + 1)
                    if late(j, 2):
                        dve.wait_ge(x1_ready, min(j.u - 1, units) if isinstance(j.u, int) else j.u - 1)
                    if late(j, NEXT + 2):
                        dve.wait_ge(hn_ready, j.u - NEXT - 1)
                    norms.means(j)

                def activate(s):
                    b = s.slot % 2
                    dve.wait_ge(bn_ready, s.u + 1)
                    if late(s, 2):
                        dve.wait_ge(leaky_turned, s.u - 1)
                    dve.scalar_tensor_tensor(leaky[:, b], bnT[:, b], SLOPE, bnT[:, b], ALU.mult, ALU.max).then_inc(leaky_ready, 1)

                def mix(s):
                    b = s.slot % 2
                    dve.wait_ge(leaky_turned, s.u + 1)
                    dve.wait_ge(x_loaded[s.slot], (s.lap + 1) * 16)
                    if late(s, 2):
                        dve.wait_ge(x1_ready, s.u - 1)
                    dve.tensor_tensor(mixed[:, b], tiled(leaky_ps[:, b]), x_in[:, s.slot], ALU.add).then_inc(mixed_ready, 1)

                def measure2(s):
                    dve.wait_ge(hidden_ready, s.u + 1)
                    for t in range(TILES):
                        last = dve.bn_stats(stats[:, (s.slot + NEXT) % 2, TILES + t, :], hidden[:, s.slot % 2, t, :])
                    last.then_inc(measured2, 1)

                def invert(j):
                    b = j.slot % 2
                    dve.wait_ge(rooted, j.u + 1)
                    dve.reciprocal(small[:, b, 4, :], small[:, b, 4, :]).then_inc(inverted, 1)

                def measure1(s, half):
                    if half == 0:
                        dve.wait_ge(mixed_ready, s.u + 1)
                    for t in range(2 * half, 2 * half + 2):
                        last = dve.bn_stats(stats[:, s.slot % 2, t, :], mixed[:, s.slot % 2, t, :])
                    if half:
                        last.then_inc(measured1, 1)

                def shift(j):
                    dve.wait_ge(inverted, j.u + 1)
                    norms.shift(j).then_inc(shifted, 1)

                def keep_dot(s):
                    dve.wait_ge(dot_product, s.u + 1)
                    dve.tensor_copy(k["loop_dot"][:, bass.ds(s.u * TILES, TILES)], dots[:, 0:TILES]).then_inc(dot_kept, 1)

                dve.memset(stats[:], 0.0).then_inc(cleared, 1)
                dve.wait_ge(cleared, 1)
                over_units(dve, units, [(5, hide), (3, means, NEXT), (1, activate), (3, norms.squares, NEXT), (2, mix),
                                        (3, norms.variance, NEXT), (5, measure2), (3, invert, NEXT), (2, lambda s: measure1(s, 0)),
                                        (3, shift, NEXT), (2, lambda s: measure1(s, 1)), (9, keep_dot)])

            @block.gpsimd
            def _(pool):
                def apply2(s):
                    b, c = s.slot % 2, (s.slot + NEXT) % 2
                    pool.wait_ge(shifted, s.u + NEXT + 1)
                    if late(s, 2):
                        pool.wait_ge(h_turn_ready, s.u - 1)
                    pool.tensor_tensor(centred[:, b], hidden[:, b], spread(small[:, c, 4, TILES:2 * TILES], D), ALU.mult).then_inc(centred_ready, 1)
                    pool.wait_ge(centred_ready, s.u + 1)
                    pool.tensor_tensor(hn[:, b], centred[:, b], spread(small[:, c, 5, TILES:2 * TILES], D), ALU.add).then_inc(hn_ready, 1)

                over_units(pool, units, [(0, apply2)])

            @block.tensor
            def _(pe):
                def turn_x1(s):
                    pe.wait_ge(x1_ready, s.u + 1)
                    if late(s, 1):
                        pe.wait_ge(x1T_ready, s.u)
                    for t in range(TILES):
                        last = pe.transpose(x1_turned[:, t * P:(t + 1) * P], x1_out[:, s.slot, t, :], k["ident"][:])
                    last.then_inc(x1_turn_ready, 1)

                def turn_h(s):
                    pe.wait_ge(hn_ready, s.u + 1)
                    if late(s, 1):
                        pe.wait_ge(hT_ready, s.u)
                    for t in range(TILES):
                        last = pe.transpose(h_turned[:, t * P:(t + 1) * P], hn[:, s.slot % 2, t, :], k["ident"][:])
                    last.then_inc(h_turn_ready, 1)

                def turn_leaky(s):
                    b = s.slot % 2
                    pe.wait_ge(leaky_ready, s.u + 1)
                    if late(s, 2):
                        pe.wait_ge(mixed_ready, s.u - 1)
                    for t in range(TILES):
                        last = pe.transpose(leaky_ps[:, b, t * P:(t + 1) * P], leaky[:, b, t * P:(t + 1) * P], k["ident"][:])
                    last.then_inc(leaky_turned, 1)

                def multiply(s):
                    pe.wait_ge(x1T_ready, s.u + 1)
                    if late(s, 1):
                        pe.wait_ge(hidden_ready, s.u)
                    for t in range(TILES):
                        last = pe.matmul(w1_ps[:, t * P:(t + 1) * P], x1T[:, s.slot % 2, t * P:(t + 1) * P], k["W1"][:], start=True, stop=True)
                    last.then_inc(w1_ready, 1)

                def turn_back(s):
                    pe.wait_ge(hT_ready, s.u + 1)
                    if late(s, 1):
                        pe.wait_ge(h_ready, s.u)
                    for t in range(TILES):
                        last = pe.transpose(h_back[:, t * P:(t + 1) * P], hT[:, s.slot % 2, t * P:(t + 1) * P], k["ident"][:])
                    last.then_inc(h_back_ready, 1)

                def pair(s):
                    if late(s, 1):
                        pe.wait_ge(pair_ready, s.u)
                    for half in range(2):
                        last = pe.matmul(pair_ps[:], k["We1"][:, half, :], hT[:, s.slot % 2], start=(half == 0), stop=(half == 1))
                    last.then_inc(pair_product, 1)

                def dot(s):
                    pe.wait_ge(pair_ready, s.u + 1)
                    if late(s, 1):
                        pe.wait_ge(dot_kept, s.u)
                    for t in range(TILES):
                        last = pe.matmul(dots[:, t:t + 1], pair_hidden[:, s.slot % 2, t * P:(t + 1) * P], k["We2"][:], start=True, stop=True)
                    last.then_inc(dot_product, 1)

                over_units(pe, units, [(4, turn_x1), (7, turn_h), (1, turn_leaky), (4, multiply), (7, turn_back), (7, pair), (8, dot)])


def gate(nc, k, x1, h, sums, out, units):
    X1, H, SUMS, OUT = by_unit(x1), by_unit(h), by_unit(sums[0:units * UNIT, :]), by_unit(out)
    MIX = 3
    with ExitStack() as stack:
        m = Memory(nc, stack, "gate")
        h_in, s_in, x1_in = (m.sb(n, [P, RING, TILES, D]) for n in ("h_in", "s_in", "x1_in"))
        hT, sT, gT, nT = (m.sb(n, [P, 2, UNIT]) for n in ("hT", "sT", "gT", "nT"))
        change, n1, n1n, n2 = (m.sb(n, [P, 2, TILES, D]) for n in ("change", "n1", "n1n", "n2"))
        out_sb = m.sb("out_sb", [P, RING, TILES, D])
        stats1, stats2 = (m.sb(n, [P, 2, TILES, 6]) for n in ("stats1", "stats2"))
        small1, small2 = (m.sb(n, [P, 2, 6, TILES]) for n in ("small1", "small2"))
        h_turned, s_turned, g_ps, n_turned = (m.ps(n, [P, UNIT]) for n in ("h_turned", "s_turned", "g_ps", "n_turned"))
        g_back, n_back = (m.ps(n, [P, 2, UNIT]) for n in ("g_back", "n_back"))
        h_loaded, s_loaded, x1_loaded, stored = (m.sems(n, RING) for n in ("h_loaded", "s_loaded", "x1_loaded", "stored"))
        (in_turned, in_copied, g_product, g_ready, g_turned, mix_own, stat1_own, stat2_own, rstd1, rstd2, n1_own, out_own,
         n_turn_ready, nT_ready, n_back_ready, n2_ready) = (
            m.sem(n) for n in ("in_turned", "in_copied", "g_product", "g_ready", "g_turned", "mix_own", "stat1_own",
                               "stat2_own", "rstd1", "rstd2", "n1_own", "out_own", "n_turn_ready", "nT_ready",
                               "n_back_ready", "n2_ready"))
        tiled = lambda ap: ap.rearrange("p (t f) -> p t f", t=TILES)
        with nc.Block() as block:
            @block.sync
            def _(sp):
                def load(s):
                    if late(s, RING):
                        sp.wait_ge(mix_own, (s.u - RING + 1) * MIX)
                        sp.wait_ge(in_turned, s.u - RING + 1)
                    sp.dma_start(h_in[:, s.slot], H[s.u]).then_inc(h_loaded[s.slot], 16)
                    sp.dma_start(s_in[:, s.slot], SUMS[s.u]).then_inc(s_loaded[s.slot], 16)

                def load_x1(s):
                    if late(s, RING):
                        sp.wait_ge(n2_ready, s.u - RING + 1)
                    sp.dma_start(x1_in[:, s.slot], X1[s.u]).then_inc(x1_loaded[s.slot], 16)

                def store(s):
                    sp.wait_ge(out_own, (s.u + 1) * APPLY_STEPS)
                    sp.dma_start(OUT[s.u], out_sb[:, s.slot]).then_inc(stored[s.slot], 16)

                with sp.If(k["irregular"]):
                    over_units(sp, units, [(6, store), (2, load_x1), (0, load)])
                    for q in stored:
                        sp.wait_ge(q, units // RING * 16)

            @block.tensor
            def _(pe):
                def turn_in(s):
                    pe.wait_ge(h_loaded[s.slot], (s.lap + 1) * 16)
                    pe.wait_ge(s_loaded[s.slot], (s.lap + 1) * 16)
                    if late(s, 1):
                        pe.wait_ge(in_copied, s.u * 2)
                    for t in range(TILES):
                        pe.transpose(h_turned[:, t * P:(t + 1) * P], h_in[:, s.slot, t, :], k["ident"][:])
                        last = pe.transpose(s_turned[:, t * P:(t + 1) * P], s_in[:, s.slot, t, :], k["ident"][:])
                    last.then_inc(in_turned, 1)

                def multiply(s):
                    b = s.slot % 2
                    pe.wait_ge(in_copied, (s.u + 1) * 2)
                    if late(s, 1):
                        pe.wait_ge(g_ready, s.u)
                    pe.matmul(g_ps[:], k["Wg"][:, 0, :], hT[:, b], start=True, stop=False)
                    pe.matmul(g_ps[:], k["Wg"][:, 1, :], sT[:, b], start=False, stop=True).then_inc(g_product, 1)

                def turn_gate(s):
                    b = s.slot % 2
                    pe.wait_ge(g_ready, s.u + 1)
                    if late(s, 2):
                        pe.wait_ge(mix_own, (s.u - 1) * MIX)
                    for t in range(TILES):
                        last = pe.transpose(g_back[:, b, t * P:(t + 1) * P], gT[:, b, t * P:(t + 1) * P], k["ident"][:])
                    last.then_inc(g_turned, 1)

                def turn_n(s):
                    b = s.slot % 2
                    pe.wait_ge(n1_own, (s.u + 1) * APPLY_STEPS)
                    if late(s, 1):
                        pe.wait_ge(nT_ready, s.u)
                    for t in range(TILES):
                        last = pe.transpose(n_turned[:, t * P:(t + 1) * P], n1n[:, b, t, :], k["ident"][:])
                    last.then_inc(n_turn_ready, 1)

                def turn_back(s):
                    b = s.slot % 2
                    pe.wait_ge(nT_ready, s.u + 1)
                    if late(s, 2):
                        pe.wait_ge(n2_ready, s.u - 1)
                    for t in range(TILES):
                        last = pe.transpose(n_back[:, b, t * P:(t + 1) * P], nT[:, b, t * P:(t + 1) * P], k["ident"][:])
                    last.then_inc(n_back_ready, 1)

                with pe.If(k["irregular"]):
                    over_units(pe, units, [(4, turn_back), (3, turn_n), (2, turn_gate), (1, multiply), (0, turn_in)])

            @block.scalar
            def _(act):
                def copy(s):
                    b = s.slot % 2
                    act.wait_ge(in_turned, s.u + 1)
                    if late(s, 2):
                        act.wait_ge(g_product, s.u - 1)
                    act.activation(hT[:, b], h_turned[:], ACT.Copy).then_inc(in_copied, 1)
                    act.activation(sT[:, b], s_turned[:], ACT.Copy).then_inc(in_copied, 1)

                def squash(s):
                    b = s.slot % 2
                    act.wait_ge(g_product, s.u + 1)
                    if late(s, 2):
                        act.wait_ge(g_turned, s.u - 1)
                    act.activation(gT[:, b], g_ps[:], ACT.Sigmoid, bias=k["bg"][:]).then_inc(g_ready, 1)

                def affine(s):
                    b = s.slot % 2
                    act.wait_ge(n_turn_ready, s.u + 1)
                    if late(s, 2):
                        act.wait_ge(n_back_ready, s.u - 1)
                    act.activation(nT[:, b], n_turned[:], ACT.Identity, bias=k["bt2"][:], scale=k["g2"][:]).then_inc(nT_ready, 1)

                with act.If(k["irregular"]):
                    over_units(act, units, [(3, affine), (1, squash), (0, copy)])

            @block.vector
            def _(dve):
                def mix(s):
                    b = s.slot % 2
                    chain = Chain(dve, mix_own, s.u * MIX)
                    dve.wait_ge(h_loaded[s.slot], (s.lap + 1) * 16)
                    dve.wait_ge(s_loaded[s.slot], (s.lap + 1) * 16)
                    chain.mark(dve.tensor_tensor(change[:, b], s_in[:, s.slot], h_in[:, s.slot], ALU.subtract))
                    chain.settle()
                    dve.wait_ge(g_turned, s.u + 1)
                    chain.mark(dve.tensor_tensor(change[:, b], tiled(g_back[:, b]), change[:, b], ALU.mult))
                    chain.settle()
                    chain.mark(dve.tensor_tensor(n1[:, b], change[:, b], h_in[:, s.slot], ALU.add))
                    chain.settle()
                    norm_stats(dve, Chain(dve, stat1_own, s.u * NORM_STEPS), n1[:, b], stats1[:, b], small1[:, b])

                def apply1(s):
                    b = s.slot % 2
                    dve.wait_ge(rstd1, s.u + 1)
                    if late(s, 2):
                        dve.wait_ge(n_turn_ready, s.u - 1)
                    norm_apply(dve, Chain(dve, n1_own, s.u * APPLY_STEPS), n1[:, b], n1n[:, b], small1[:, b])

                def residual(s):
                    b = s.slot % 2
                    dve.wait_ge(n_back_ready, s.u + 1)
                    dve.wait_ge(x1_loaded[s.slot], (s.lap + 1) * 16)
                    dve.tensor_tensor(n2[:, b], tiled(n_back[:, b]), x1_in[:, s.slot], ALU.add).then_inc(n2_ready, 1)
                    dve.wait_ge(n2_ready, s.u + 1)
                    norm_stats(dve, Chain(dve, stat2_own, s.u * NORM_STEPS), n2[:, b], stats2[:, b], small2[:, b])

                def apply2(s):
                    b = s.slot % 2
                    dve.wait_ge(rstd2, s.u + 1)
                    if late(s, RING):
                        dve.wait_ge(stored[s.slot], s.lap * 16)
                    norm_apply(dve, Chain(dve, out_own, s.u * APPLY_STEPS), n2[:, b], out_sb[:, s.slot], small2[:, b])

                with dve.If(k["irregular"]):
                    over_units(dve, units, [(5, apply2), (4, residual), (3, apply1), (2, mix)])

            @block.gpsimd
            def _(pool):
                def root1(s):
                    b = s.slot % 2
                    pool.wait_ge(stat1_own, (s.u + 1) * NORM_STEPS)
                    pool.tensor_tensor(small1[:, b, 4, :], small1[:, b, 3, :], k["power"][:, 0:TILES], ALU.pow).then_inc(rstd1, 1)

                def root2(s):
                    b = s.slot % 2
                    pool.wait_ge(stat2_own, (s.u + 1) * NORM_STEPS)
                    pool.tensor_tensor(small2[:, b, 4, :], small2[:, b, 3, :], k["power"][:, 0:TILES], ALU.pow).then_inc(rstd2, 1)

                with pool.If(k["irregular"]):
                    over_units(pool, units, [(4, root2), (2, root1)])


def attend(nc, k, x1, h, rel_rows, out, units):
    X1, H, OUT = by_unit(x1), by_unit(h), by_unit(out)
    REL = rel_rows.rearrange("(u t) s -> u (t s)", t=TILES)
    SUM, MIX, NEXT = TILES, 3, 3
    with ExitStack() as stack:
        m = Memory(nc, stack, "att")
        h_in, x1_in, rows = (m.sb(n, [P, RING, TILES, D]) for n in ("h_in", "x1_in", "rows"))
        rel_in = m.sb("rel_in", [P, RING, UNIT])
        slot_src = m.sb("slot_src", [P, RING, TILES], I32)
        hT, rowsT, value, pick, hidden, sT, gT, nT = (
            m.sb(n, [P, 2, UNIT]) for n in ("hT", "rowsT", "value", "pick", "hidden", "sT", "gT", "nT"))
        weight = m.sb("weight", [P, 2, 2, TILES])
        weighted = m.sb("weighted", [P, 2, TILES, P])
        sums, change, n1, n1n, n2 = (m.sb(n, [P, 2, TILES, D]) for n in ("sums", "change", "n1", "n1n", "n2"))
        out_sb = m.sb("out_sb", [P, RING, TILES, D])
        stats = m.sb("stats", [P, 2, 2 * TILES, 6])
        small = m.sb("small", [P, 2, 6, 2 * TILES])
        h_or_sums, rows_or_n, value_or_sums, pre, g_ps, g_back, n_back, dots = (
            m.ps(n, [P, UNIT]) for n in ("h_or_sums", "rows_or_n", "value_or_sums", "pre", "g_ps", "g_back", "n_back", "dots"))
        h_loaded, rel_loaded, x1_loaded, rows_loaded, stored = (
            m.sems(n, RING) for n in ("h_loaded", "rel_loaded", "x1_loaded", "rows_loaded", "stored"))
        (rows_clear, slots_ready, passed, h_turned, rows_turned, hT_ready, rowsT_ready, value_product, value_ready,
         pick_ready, pre_product, hidden_ready, dot_product, weight_ready, weighted_ready, sum_product, sums_own,
         sums_turned, sT_ready, g_product, g_ready, g_turned, mix_own, measured1, measured2, own, rooted, shifted, n1_ready, cleared,
         out_ready, n_turned, nT_ready, n_back_ready, n2_ready) = (
            m.sem(n) for n in ("rows_clear", "slots_ready", "passed", "h_turned", "rows_turned", "hT_ready", "rowsT_ready",
                               "value_product", "value_ready", "pick_ready", "pre_product", "hidden_ready", "dot_product",
                               "weight_ready", "weighted_ready", "sum_product", "sums_own", "sums_turned", "sT_ready",
                               "g_product", "g_ready", "g_turned", "mix_own", "measured1", "measured2", "own", "rooted", "shifted",
                               "n1_ready", "cleared", "out_ready", "n_turned", "nT_ready", "n_back_ready", "n2_ready"))
        tiled = lambda ap: ap.rearrange("p (t f) -> p t f", t=TILES)

        def ahead(s, n):
            return min(s.u + n + 1, units) if isinstance(s.u, int) else s.u + n + 1

        with nc.Block() as block:
            @block.sync
            def _(sp):
                def load(s):
                    if late(s, RING):
                        sp.wait_ge(mix_own, (s.u - RING + 1) * MIX)
                        sp.wait_ge(pick_ready, s.u - RING + 1)
                    sp.dma_start(h_in[:, s.slot], H[s.u]).then_inc(h_loaded[s.slot], 16)
                    sp.dma_start(rel_in[:, s.slot], REL[bass.ds(s.u, 1), :].to_broadcast([P, UNIT])).then_inc(rel_loaded[s.slot], 16)

                def load_x1(s):
                    if late(s, RING):
                        sp.wait_ge(n2_ready, s.u - RING + 1)
                    sp.dma_start(x1_in[:, s.slot], X1[s.u]).then_inc(x1_loaded[s.slot], 16)

                def store(s):
                    sp.wait_ge(out_ready, s.u + 1)
                    sp.dma_start(OUT[s.u], out_sb[:, s.slot]).then_inc(stored[s.slot], 16)

                with sp.If(k["is_regular"]):
                    over_units(sp, units, [(0, load), (3, load_x1), (9, store)])
                    for q in stored:
                        sp.wait_ge(q, units // RING * 16)

            @block.gpsimd
            def _(pool):
                def gather(s):
                    if late(s, RING):
                        pool.wait_ge(rows_loaded[s.slot], s.lap * 16 * TILES)
                        pool.wait_ge(sum_product, s.u - RING + 1)
                    pool.tensor_copy(slot_src[:, s.slot, :], k["slot_src"][:, bass.ds(s.u * TILES, TILES)]).then_inc(slots_ready, 1)
                    pool.wait_ge(slots_ready, s.u + 1)
                    pool.sem_inc(passed, 1)
                    for t in range(TILES):
                        pool.indirect_dma_start(out=rows[:, s.slot, t, :], out_offset=None, in_=h,
                                                in_offset=bass.IndirectOffsetOnAxis(ap=slot_src[:, s.slot, t:t + 1], axis=0),
                                                bounds_check=units * UNIT - 1, oob_is_err=False).then_inc(rows_loaded[s.slot], 16)

                def root(j):
                    b = j.slot % 2
                    pool.wait_ge(own, (j.u + 1) * SMALLS)
                    pool.tensor_tensor(small[:, b, 4, :], small[:, b, 3, :], k["power"][:], ALU.pow).then_inc(rooted, 1)

                with pool.If(k["is_regular"]):
                    pool.wait_ge(rows_clear, 1)
                    over_units(pool, units, [(0, gather), (5, root, NEXT)])

            @block.tensor
            def _(pe):
                def turn_in(s):
                    pe.wait_ge(h_loaded[s.slot], (s.lap + 1) * 16)
                    if late(s, 2):
                        pe.wait_ge(sT_ready, s.u - 1)
                    for t in range(TILES):
                        last = pe.transpose(h_or_sums[:, t * P:(t + 1) * P], h_in[:, s.slot, t, :], k["ident"][:])
                    last.then_inc(h_turned, 1)
                    pe.wait_ge(rows_loaded[s.slot], (s.lap + 1) * 16 * TILES)
                    if late(s, RING + 1):
                        pe.wait_ge(nT_ready, s.u - 4)
                    for t in range(TILES):
                        last = pe.transpose(rows_or_n[:, t * P:(t + 1) * P], rows[:, s.slot, t, :], k["ident"][:])
                    last.then_inc(rows_turned, 1)

                def dot(s):
                    b = s.slot % 2
                    pe.wait_ge(hidden_ready, s.u + 1)
                    if late(s, 2):
                        pe.wait_ge(weight_ready, (s.u - 1) * 2)
                    for t in range(TILES):
                        last = pe.matmul(dots[:, b * TILES + t:b * TILES + t + 1], hidden[:, b, t * P:(t + 1) * P], k["We2"][:], start=True, stop=True)
                    last.then_inc(dot_product, 1)

                def values(s):
                    b = s.slot % 2
                    pe.wait_ge(hT_ready, s.u + 1)
                    if late(s, 2):
                        pe.wait_ge(sums_own, (s.u - 1) * SUM)
                    for t in range(TILES):
                        last = pe.matmul(value_or_sums[:, t * P:(t + 1) * P], hT[:, b, t * P:(t + 1) * P], k["We1"][:, 1, :], start=True, stop=True)
                    last.then_inc(value_product, 1)

                def turn_n(s):
                    b = s.slot % 2
                    pe.wait_ge(n1_ready, s.u + 1)
                    pe.wait_ge(rowsT_ready, ahead(s, 4))
                    for t in range(TILES):
                        last = pe.transpose(rows_or_n[:, t * P:(t + 1) * P], n1n[:, b, t, :], k["ident"][:])
                    last.then_inc(n_turned, 1)

                def sum_rows(s):
                    b = s.slot % 2
                    pe.wait_ge(weighted_ready, s.u + 1)
                    pe.wait_ge(value_ready, ahead(s, 1))
                    for t in range(TILES):
                        last = pe.matmul(value_or_sums[:, t * P:(t + 1) * P], weighted[:, b, t, :], rows[:, s.slot, t, :], start=True, stop=True)
                    last.then_inc(sum_product, 1)

                def turn_gate(s):
                    b = s.slot % 2
                    pe.wait_ge(g_ready, s.u + 1)
                    if late(s, 1):
                        pe.wait_ge(mix_own, s.u * MIX)
                    for t in range(TILES):
                        last = pe.transpose(g_back[:, t * P:(t + 1) * P], gT[:, b, t * P:(t + 1) * P], k["ident"][:])
                    last.then_inc(g_turned, 1)

                def pairs(s):
                    b = s.slot % 2
                    pe.wait_ge(rowsT_ready, s.u + 1)
                    if late(s, 1):
                        pe.wait_ge(hidden_ready, s.u)
                    pe.matmul(pre[:], k["We1"][:, 0, :], rowsT[:, b], start=True, stop=False, skip_group_check=True)
                    pe.wait_ge(value_ready, s.u + 1)
                    pe.wait_ge(pick_ready, s.u + 1)
                    for t in range(TILES):
                        last = pe.matmul(pre[:, t * P:(t + 1) * P], value[:, b, t * P:(t + 1) * P], pick[:, b, t * P:(t + 1) * P],
                                         start=False, stop=(t == TILES - 1), skip_group_check=True)
                    last.then_inc(pre_product, 1)

                def turn_sums(s):
                    b = s.slot % 2
                    pe.wait_ge(sums_own, (s.u + 1) * SUM)
                    pe.wait_ge(hT_ready, ahead(s, 1))
                    for t in range(TILES):
                        last = pe.transpose(h_or_sums[:, t * P:(t + 1) * P], sums[:, b, t, :], k["ident"][:])
                    last.then_inc(sums_turned, 1)

                def turn_back(s):
                    b = s.slot % 2
                    pe.wait_ge(nT_ready, s.u + 1)
                    if late(s, 1):
                        pe.wait_ge(n2_ready, s.u)
                    for t in range(TILES):
                        last = pe.transpose(n_back[:, t * P:(t + 1) * P], nT[:, b, t * P:(t + 1) * P], k["ident"][:])
                    last.then_inc(n_back_ready, 1)

                def gates(s):
                    b = s.slot % 2
                    if late(s, 1):
                        pe.wait_ge(g_ready, s.u)
                    pe.matmul(g_ps[:], k["Wg"][:, 0, :], hT[:, b], start=True, stop=False)
                    pe.wait_ge(sT_ready, s.u + 1)
                    pe.matmul(g_ps[:], k["Wg"][:, 1, :], sT[:, b], start=False, stop=True).then_inc(g_product, 1)

                with pe.If(k["is_regular"]):
                    over_units(pe, units, [(0, turn_in), (1, dot), (0, values), (4, turn_n), (1, sum_rows), (2, turn_gate),
                                           (0, pairs), (1, turn_sums), (4, turn_back), (1, gates)])

            @block.scalar
            def _(act):
                def copy_in(s):
                    b = s.slot % 2
                    act.wait_ge(h_turned, s.u + 1)
                    if late(s, 2):
                        act.wait_ge(g_product, s.u - 1)
                    act.activation(hT[:, b], h_or_sums[:], ACT.Copy).then_inc(hT_ready, 1)
                    act.wait_ge(rows_turned, s.u + 1)
                    if late(s, 2):
                        act.wait_ge(pre_product, s.u - 1)
                    act.activation(rowsT[:, b], rows_or_n[:], ACT.Copy).then_inc(rowsT_ready, 1)

                def weigh(s):
                    b = s.slot % 2
                    act.wait_ge(dot_product, s.u + 1)
                    if late(s, 2):
                        act.wait_ge(weighted_ready, s.u - 1)
                        act.wait_ge(sums_own, (s.u - 1) * SUM)
                    act.activation(weight[:, b, 0, :], dots[:, b * TILES:(b + 1) * TILES], ACT.Sigmoid, bias=k["be2"][:]).then_inc(weight_ready, 1)
                    act.activation(weight[:, b, 1, :], k["loop_dot"][:, bass.ds(s.u * TILES, TILES)], ACT.Sigmoid, bias=k["be2"][:]).then_inc(weight_ready, 1)

                def copy_values(s):
                    b = s.slot % 2
                    act.wait_ge(value_product, s.u + 1)
                    if late(s, 2):
                        act.wait_ge(pre_product, s.u - 1)
                    act.activation(value[:, b], value_or_sums[:], ACT.Copy).then_inc(value_ready, 1)

                def affine(s):
                    b = s.slot % 2
                    act.wait_ge(n_turned, s.u + 1)
                    if late(s, 2):
                        act.wait_ge(n_back_ready, s.u - 1)
                    act.activation(nT[:, b], rows_or_n[:], ACT.Identity, bias=k["bt2"][:], scale=k["g2"][:]).then_inc(nT_ready, 1)

                def rectify(s):
                    b = s.slot % 2
                    act.wait_ge(pre_product, s.u + 1)
                    if late(s, 2):
                        act.wait_ge(dot_product, s.u - 1)
                    act.activation(hidden[:, b], pre[:], ACT.Relu, bias=k["be1"][:]).then_inc(hidden_ready, 1)

                def copy_sums(s):
                    b = s.slot % 2
                    act.wait_ge(sums_turned, s.u + 1)
                    if late(s, 2):
                        act.wait_ge(g_product, s.u - 1)
                    act.activation(sT[:, b], h_or_sums[:], ACT.Copy).then_inc(sT_ready, 1)

                def squash(s):
                    b = s.slot % 2
                    act.wait_ge(g_product, s.u + 1)
                    if late(s, 2):
                        act.wait_ge(g_turned, s.u - 1)
                    act.activation(gT[:, b], g_ps[:], ACT.Sigmoid, bias=k["bg"][:]).then_inc(g_ready, 1)

                def apply1(s):
                    b = s.slot % 2
                    act.wait_ge(shifted, s.u + 1)
                    if late(s, 2):
                        act.wait_ge(n_turned, s.u - 1)
                    for t in range(TILES):
                        last = act.activation(n1n[:, b, t, :], n1[:, b, t, :], ACT.Identity, bias=small[:, b, 5, t:t + 1],
                                              scale=small[:, b, 4, t:t + 1])
                    last.then_inc(n1_ready, 1)

                with act.If(k["is_regular"]):
                    over_units(act, units, [(0, copy_in), (1, weigh), (0, copy_values), (4, affine), (0, rectify),
                                            (1, copy_sums), (1, squash), (3, apply1)])

            @block.vector
            def _(dve):
                norms = Norms(dve, own, stats, small)

                def picks(s):
                    b = s.slot % 2
                    dve.wait_ge(rel_loaded[s.slot], (s.lap + 1) * 16)
                    if late(s, 2):
                        dve.wait_ge(pre_product, s.u - 1)
                    dve.tensor_scalar(pick[:, b], rel_in[:, s.slot], k["trash"][:], None, ALU.is_equal).then_inc(pick_ready, 1)

                def weigh_hot(s):
                    b = s.slot % 2
                    dve.wait_ge(weight_ready, (s.u + 1) * 2)
                    if late(s, 2):
                        dve.wait_ge(sum_product, s.u - 1)
                    for t in range(TILES):
                        last = dve.tensor_scalar(weighted[:, b, t, :], k["lane"][:], k["slot_rel"][:, bass.ds(s.u * TILES + t, 1)],
                                                 weight[:, b, 0, t:t + 1], ALU.is_equal, ALU.mult)
                    last.then_inc(weighted_ready, 1)

                def add_loops(s):
                    b = s.slot % 2
                    dve.wait_ge(sum_product, s.u + 1)
                    dve.wait_ge(h_loaded[s.slot], (s.lap + 1) * 16)
                    if late(s, 2):
                        dve.wait_ge(mix_own, (s.u - 1) * MIX)
                        dve.wait_ge(sums_turned, s.u - 1)
                    for t in range(TILES):
                        dve.scalar_tensor_tensor(sums[:, b, t, :], h_in[:, s.slot, t, :], weight[:, b, 1, t:t + 1],
                                                 value_or_sums[:, t * P:(t + 1) * P], ALU.mult, ALU.add).then_inc(sums_own, 1)

                def differ(s):
                    b = s.slot % 2
                    dve.wait_ge(sums_own, (s.u + 1) * SUM)
                    dve.tensor_tensor(change[:, b], sums[:, b], h_in[:, s.slot], ALU.subtract).then_inc(mix_own, 1)

                def multiply(s):
                    b = s.slot % 2
                    dve.wait_ge(mix_own, s.u * MIX + 1)
                    dve.wait_ge(g_turned, s.u + 1)
                    dve.tensor_tensor(change[:, b], tiled(g_back[:]), change[:, b], ALU.mult).then_inc(mix_own, 1)

                def mix(s):
                    b = s.slot % 2
                    dve.wait_ge(mix_own, s.u * MIX + 2)
                    if late(s, 2):
                        dve.wait_ge(n1_ready, s.u - 1)
                    dve.tensor_tensor(n1[:, b], change[:, b], h_in[:, s.slot], ALU.add).then_inc(mix_own, 1)

                def measure1(s):
                    dve.wait_ge(mix_own, (s.u + 1) * MIX)
                    for t in range(TILES):
                        last = dve.bn_stats(stats[:, s.slot % 2, t, :], n1[:, s.slot % 2, t, :])
                    last.then_inc(measured1, 1)

                def means(j):
                    if before(j, units):
                        dve.wait_ge(measured1, j.u + 1)
                    if late(j, NEXT):
                        dve.wait_ge(measured2, j.u - NEXT + 1)
                    if late(j, 2):
                        dve.wait_ge(n1_ready, min(j.u - 1, units) if isinstance(j.u, int) else j.u - 1)
                    if late(j, NEXT + 2):
                        dve.wait_ge(out_ready, j.u - NEXT - 1)
                    norms.means(j)

                def shift(j):
                    dve.wait_ge(rooted, j.u + 1)
                    norms.shift(j).then_inc(shifted, 1)

                def residual(s):
                    b = s.slot % 2
                    dve.wait_ge(n_back_ready, s.u + 1)
                    dve.wait_ge(x1_loaded[s.slot], (s.lap + 1) * 16)
                    if late(s, 2):
                        dve.wait_ge(out_ready, s.u - 1)
                    dve.tensor_tensor(n2[:, b], tiled(n_back[:]), x1_in[:, s.slot], ALU.add).then_inc(n2_ready, 1)

                def measure2(s):
                    dve.wait_ge(n2_ready, s.u + 1)
                    for t in range(TILES):
                        last = dve.bn_stats(stats[:, (s.slot + NEXT) % 2, TILES + t, :], n2[:, s.slot % 2, t, :])
                    last.then_inc(measured2, 1)

                def apply2(s, half):
                    b, c = s.slot % 2, (s.slot + NEXT) % 2
                    if half == 0:
                        dve.wait_ge(shifted, s.u + NEXT + 1)
                        if late(s, RING):
                            dve.wait_ge(stored[s.slot], s.lap * 16)
                    for t in range(2 * half, 2 * half + 2):
                        last = dve.tensor_scalar(out_sb[:, s.slot, t, :], n2[:, b, t, :], small[:, c, 4, TILES + t:TILES + t + 1],
                                                 small[:, c, 5, TILES + t:TILES + t + 1], ALU.mult, ALU.add)
                    if half:
                        last.then_inc(out_ready, 1)

                with dve.If(k["is_regular"]):
                    dve.memset(rows[:], 0.0).then_inc(rows_clear, 1)
                    dve.memset(stats[:], 0.0).then_inc(cleared, 1)
                    dve.wait_ge(cleared, 1)
                    over_units(dve, units, [(5, residual), (3, means, NEXT), (0, picks), (3, norms.squares, NEXT), (2, differ),
                                            (3, norms.variance, NEXT), (1, weigh_hot), (5, measure2), (1, add_loops),
                                            (3, shift, NEXT), (2, multiply), (6, lambda s: apply2(s, 0)), (2, mix),
                                            (6, lambda s: apply2(s, 1)), (2, measure1)])


VECTORS = {"ln_g": "L0_gnn_ln_g", "ln_b": "L0_gnn_ln_b", "gcn_b": "L0_gnn_gcn_b", "rs_b": "L0_gnn_rs_b",
           "bn_g": "L0_gnn_bn_g", "bn_b": "L0_gnn_bn_b", "g1": "L1_gnn_g1", "bt1": "L1_gnn_bt1",
           "be1": "L1_gnn_be1", "bg": "L1_gnn_bg", "g2": "L1_gnn_g2", "bt2": "L1_gnn_bt2", "be2": "L1_gnn_be2"}
MATRICES = {"gcn_w": "L0_gnn_gcn_w", "rs_w": "L0_gnn_rs_w", "W1": "L1_gnn_W1", "We1": "L1_gnn_We1",
            "We2": "L1_gnn_We2", "Wg": "L1_gnn_Wg"}


def load_edges(nc, stack, src, dst, chunks, tiles, b1, k):
    m = Memory(nc, stack, "k")
    for name in ("src", "dst", "place"):
        k[name] = m.sb(name, [P, chunks], I32)
    k["slot_src"], k["slot_rel"] = m.sb("slot_src", [P, tiles], I32), m.sb("slot_rel", [P, tiles])
    k["regular"] = m.sb("regular", [1, 2], I32)
    for name in ("dinv", "root", "edges", "loop_dot"):
        k[name] = m.sb(name, [P, tiles])
    for name in ("bn_scale", "bn_shift", "conv_b"):
        k[name] = m.sb(name, [P, 1])
    k["b1_row"] = m.sb("b1_row", [P, D])
    loaded = m.sem("loaded")
    with nc.Block() as block:
        @block.sync
        def _(sp):
            sp.dma_start(k["src"][:], src).then_inc(loaded, 16)
            sp.dma_start(k["dst"][:], dst).then_inc(loaded, 16)
            sp.dma_start(k["b1_row"][:], b1.rearrange("(a f) -> a f", a=1).to_broadcast([P, D])).then_inc(loaded, 16)
            sp.wait_ge(loaded, 48)

        @block.vector
        def _(dve):
            dve.tensor_tensor(k["conv_b"][:], k["gcn_b"][:], k["rs_b"][:], ALU.add)


def build(nc, nodes, x, src, dst, ends, heads, line, b1, weights, out):
    padded = x.shape[0]
    tiles, units, chunks = padded // P, padded // UNIT, src.shape[1]
    table = lambda name, shape: nc.dram_tensor(name, shape, F32).ap()
    y, x1, h = (table(n, [padded, D]) for n in ("messages", "x1", "h"))
    sums1, sums2 = (table(n, [padded + P, D]) for n in ("sums1", "sums2"))
    counts = table("counts", [padded + P, 1])
    outT = table("outT", [D, padded])
    with ExitStack() as stack:
        k = build_constants(nc, Memory(nc, stack, "k0"), weights)
        load_edges(nc, stack, src, dst, chunks, tiles, b1, k)
        rel_rows = table("rel_rows", [tiles, SLOTS])
        index_edges(nc, k, ends, heads, line, rel_rows, tiles)
        k["is_regular"] = nc.values_load(k["regular"][0:1, 0:1], min_val=0, max_val=1)
        k["irregular"] = nc.values_load(k["regular"][0:1, 1:2], min_val=0, max_val=1)
        count_slots(nc, k, tiles)
        clear_tables(nc, k, [sums1, sums2, counts])
        count_edges(nc, k, counts, chunks, padded, tiles)
        degrees(nc, k, tiles)
        make_messages(nc, k, x, y, units)
        add_messages(nc, k, y, sums1, chunks)
        convolve(nc, k, y, sums1, outT, units, nodes)
        embed(nc, k, x, outT, x1, h, units)
        attend(nc, k, x1, h, rel_rows, out, units)
        add_messages(nc, k, h, sums2, chunks, k)
        gate(nc, k, x1, h, sums2, out, units)


def kernel(**inputs):
    import concourse.bacc as bacc
    from concourse.bass_utils import run_bass_kernel_spmd

    nc = bacc.Bacc("TRN2", target_bir_lowering=False, num_devices=1)
    x = np.asarray(inputs["x"])
    nodes, edges = x.shape[0], inputs["src"].shape[0]
    padded = -(-nodes // (UNIT * RING)) * UNIT * RING
    chunks = -(-(edges + padded - nodes) // (2 * P)) * 2
    spare = chunks * P - edges
    arrays = {"x": np.zeros((padded, D), x.dtype)}
    arrays["x"][:nodes] = x
    loops = (nodes + np.arange(spare) * (padded - nodes) // spare).astype(np.int32)
    lines = {name: np.concatenate([np.asarray(inputs[name]), loops]) for name in ("src", "dst")}
    for name, ends in lines.items():
        arrays[name] = np.ascontiguousarray(ends.reshape(chunks, P).T)
    beyond = np.full((WINDOW_ROWS, 2 * HALF), padded, np.int32)
    arrays["ends"] = np.concatenate([np.hstack([lines["dst"].reshape(-1, HALF), lines["src"].reshape(-1, HALF)]), beyond])
    arrays["heads"] = np.ascontiguousarray(lines["dst"][::HALF])
    arrays["line"] = np.stack([lines["dst"], np.append(lines["dst"][1:], lines["dst"][-1:])])
    arrays["b1"] = np.asarray(inputs["L1_gnn_b1"])
    names = {**MATRICES, **VECTORS}
    for short, name in names.items():
        arrays[short] = np.ascontiguousarray(inputs[name])
    ap = {n: nc.dram_tensor(f"in_{n}", a.shape, mybir.dt.from_np(a.dtype), kind="ExternalInput").ap()
          for n, a in arrays.items()}
    out = nc.dram_tensor("out", (padded, D), F32, kind="ExternalOutput").ap()
    build(nc, nodes, ap["x"], ap["src"], ap["dst"], ap["ends"], ap["heads"], ap["line"], ap["b1"], {n: ap[n] for n in names}, out)
    result = run_bass_kernel_spmd(nc, [{f"in_{n}": a for n, a in arrays.items()}], core_ids=[0])
    return np.asarray(result.results[0]["out"])[:nodes]
```

```python
from contextlib import ExitStack

import numpy as np

import concourse.bass as bass
from concourse import mybir

P = 128
D = 128
TILES = 4
UNIT = TILES * P
RING = 4
EPS = 1e-5
SLOPE = 0.01

ALU = mybir.AluOpType
ACT = mybir.ActivationFunctionType
F32 = mybir.dt.float32
I32 = mybir.dt.int32


class Step:

    def __init__(self, lap, slot, ring):
        self.lap, self.slot, self.ring = lap, slot, ring
        self.u = lap * ring + slot

    def back(self, lag):
        slot = self.slot - lag
        return Step(self.lap + slot // self.ring, slot % self.ring, self.ring)


def over_units(eng, units, stages, ring=RING):
    stages = [(lag, stage, (more or [0])[0]) for lag, stage, *more in stages]
    peeled = ring * (1 + -(-max(lag for lag, _, _ in stages) // ring))
    last = max(lag + more for lag, _, more in stages)
    looped = units // ring * ring
    assert looped > peeled
    for u in range(peeled):
        for lag, stage, _ in stages:
            if u >= lag:
                stage(Step(u // ring, u % ring, ring).back(lag))
    with eng.Fori(peeled // ring, looped // ring) as lap:
        for slot in range(ring):
            for lag, stage, _ in stages:
                stage(Step(lap, slot, ring).back(lag))
    for u in range(looped, units + last):
        for lag, stage, more in stages:
            if u - lag < units + more:
                stage(Step(u // ring, u % ring, ring).back(lag))


def delayed(lag, stages):
    return [(lag + own, *rest) for own, *rest in stages]


def late(s, n):
    return not (isinstance(s.u, int) and s.u < n)


def over_pairs(eng, chunks, wanted):
    def run(body):
        with eng.If(wanted):
            body(0)
            with eng.Fori(1, chunks // 2) as pair:
                body(pair)
    return run


def not_first(n):
    return not (isinstance(n, int) and n == 0)


def before(s, n):
    return not (isinstance(s.u, int) and s.u >= n)


class Chain:

    def __init__(self, eng, sem, start):
        self.eng, self.sem, self.value, self.given = eng, sem, start, 0

    def mark(self, instruction):
        instruction.then_inc(self.sem, 1)
        self.given += 1
        self.value = self.value + 1

    def settle(self):
        self.eng.wait_ge(self.sem, self.value)


class Memory:

    def __init__(self, nc, stack, name):
        self.nc, self.stack, self.name, self.semaphores = nc, stack, name, []
        stack.callback(self.clear)

    def sb(self, name, shape, dtype=F32):
        return self.stack.enter_context(self.nc.sbuf_tensor(f"{self.name}_{name}", shape, dtype))

    def ps(self, name, shape, dtype=F32):
        return self.stack.enter_context(self.nc.psum_tensor(f"{self.name}_{name}", shape, dtype))

    def sem(self, name):
        self.semaphores.append(self.nc.alloc_semaphore(name=f"{self.name}_{name}"))
        return self.semaphores[-1]

    def sems(self, name, n):
        return [self.sem(f"{name}{i}") for i in range(n)]

    def clear(self):
        if self.semaphores:
            self.nc.clear_and_free_semaphores(self.semaphores)
            self.nc.all_engine_barrier()


NORM_STEPS = 10


def norm_stats(dve, chain, source, stats, small):
    for t in range(TILES):
        chain.mark(dve.bn_stats(stats[:, t, :], source[:, t, :]))
    chain.settle()
    chain.mark(dve.tensor_tensor(small[:, 0, :], stats[:, :, 1], stats[:, :, 4], ALU.add))
    chain.mark(dve.tensor_tensor(small[:, 1, :], stats[:, :, 1], stats[:, :, 4], ALU.subtract))
    chain.mark(dve.tensor_tensor(small[:, 2, :], stats[:, :, 2], stats[:, :, 5], ALU.add))
    chain.settle()
    chain.mark(dve.tensor_tensor(small[:, 1, :], small[:, 1, :], small[:, 1, :], ALU.mult))
    chain.mark(dve.tensor_scalar(small[:, 2, :], small[:, 2, :], 1.0 / D, EPS, ALU.mult, ALU.add))
    chain.settle()
    chain.mark(dve.scalar_tensor_tensor(small[:, 3, :], small[:, 1, :], 0.25, small[:, 2, :],
                                        ALU.mult, ALU.add))


MEANS, SQUARES, SMALLS = 3, 2, 6


class Norms:

    def __init__(self, dve, own, stats, small):
        self.dve, self.own, self.stats, self.small, self.depth = dve, own, stats, small, small.shape[1]

    def means(self, j):
        stats, small = self.stats[:, j.slot % 2], self.small[:, j.slot % self.depth]
        for row, (a, b), op in ((0, (1, 4), ALU.add), (1, (1, 4), ALU.subtract), (2, (2, 5), ALU.add)):
            self.dve.tensor_tensor(small[:, row, :], stats[:, :, a], stats[:, :, b], op).then_inc(self.own, 1)

    def squares(self, j):
        small = self.small[:, j.slot % self.depth]
        self.dve.wait_ge(self.own, j.u * SMALLS + MEANS)
        self.dve.tensor_tensor(small[:, 1, :], small[:, 1, :], small[:, 1, :], ALU.mult).then_inc(self.own, 1)
        self.dve.tensor_scalar(small[:, 2, :], small[:, 2, :], 1.0 / D, EPS, ALU.mult, ALU.add).then_inc(self.own, 1)

    def variance(self, j):
        small = self.small[:, j.slot % self.depth]
        self.dve.wait_ge(self.own, j.u * SMALLS + MEANS + SQUARES)
        self.dve.scalar_tensor_tensor(small[:, 3, :], small[:, 1, :], 0.25, small[:, 2, :], ALU.mult, ALU.add).then_inc(self.own, 1)

    def shift(self, j):
        small = self.small[:, j.slot % self.depth]
        return self.dve.scalar_tensor_tensor(small[:, 5, :], small[:, 0, :], -0.5, small[:, 4, :], ALU.mult, ALU.mult)


APPLY_STEPS = 1 + TILES


def norm_apply(dve, chain, source, out, small):
    chain.mark(dve.scalar_tensor_tensor(small[:, 5, :], small[:, 0, :], -0.5, small[:, 4, :],
                                        ALU.mult, ALU.mult))
    chain.settle()
    for t in range(TILES):
        chain.mark(dve.tensor_scalar(out[:, t, :], source[:, t, :], small[:, 4, t:t + 1],
                                     small[:, 5, t:t + 1], ALU.mult, ALU.add))


def spread(column, width):
    return column.unsqueeze(2).to_broadcast([P, column.shape[1], width])


def by_unit(table):
    return table.rearrange("(u t p) f -> u p t f", t=TILES, p=P)


def build_constants(nc, memory, weights):
    m = Memory(nc, memory.stack, "c")
    ident = m.sb("ident", [P, P])
    earlier = m.sb("earlier", [P, P])
    trash = m.sb("trash", [P, 1])
    power = m.sb("power", [P, 2 * TILES])
    lane = m.sb("lane", [P, P])
    ones = m.sb("ones", [P, 1])
    zero = m.sb("zero", [P, 1])
    held = {n: m.sb(n, [P, a.shape[1]]) for n, a in weights.items() if len(a.shape) == 2 and a.shape[0] == P}
    loaded, made = m.sem("loaded"), m.sem("made")
    for n, a in weights.items():
        if len(a.shape) == 1:
            held[n] = m.sb(n, [P, 1])
        elif a.shape[0] == 2 * P:
            held[n] = m.sb(n, [P, 2, a.shape[1]])
    with nc.Block() as block:
        @block.sync
        def _(sp):
            for n, a in weights.items():
                if len(a.shape) == 1 and a.shape[0] == 1:
                    src = a.rearrange("(a b) -> a b", a=1).to_broadcast([P, 1])
                elif len(a.shape) == 1:
                    src = a.rearrange("(a b) -> a b", b=1)
                elif a.shape[0] == 2 * P:
                    src = a.rearrange("(h p) f -> p h f", h=2)
                else:
                    src = a
                sp.dma_start(held[n][:], src).then_inc(loaded, 16)
            sp.wait_ge(loaded, 16 * len(weights))

        @block.vector
        def _(dve):
            dve.memset(power[:], -0.5)
            dve.memset(ones[:], 1.0)
            dve.memset(zero[:], 0.0)

        @block.gpsimd
        def _(pool):
            pool.memset(ident[:], 1.0).then_inc(made, 1)
            pool.memset(earlier[:], 1.0).then_inc(made, 1)
            pool.iota(trash[:], [[0, 1]], base=0, channel_multiplier=1,
                      allow_small_or_imprecise_dtypes=True).then_inc(made, 1)
            pool.iota(lane[:], [[1, P]], base=0, channel_multiplier=0, allow_small_or_imprecise_dtypes=True)
            pool.wait_ge(made, 3)
            pool.affine_select(out=ident[:], in_=ident[:], compare_op=ALU.is_equal, fill=0.0,
                               base=0, pattern=[[1, P]], channel_multiplier=-1)
            pool.affine_select(out=earlier[:], in_=earlier[:], compare_op=ALU.is_gt, fill=0.0,
                               base=0, pattern=[[-1, P]], channel_multiplier=1)
    return dict(held, ident=ident, earlier=earlier, trash=trash, power=power, lane=lane, ones=ones, zero=zero)


WINDOW_ROWS = 5
HALF = 64
WINDOW = WINDOW_ROWS * HALF
SLOTS = P
SRC_BITS = 17


def index_edges(nc, k, ends, heads, line, rel_rows, tiles):
    rows = heads.shape[0]
    per = next(q for q in range(P, 0, -1) if tiles % q == 0)
    batches = tiles // per
    span = line.shape[1] // P
    ROUND = 2 * batches + 1
    with ExitStack() as stack:
        m = Memory(nc, stack, "idx")
        head = m.sb("head", [per, rows], I32)
        below = m.sb("below", [per, rows])
        base = m.sb("base", [per, batches])
        start = m.sb("start", [per, batches])
        row_of = m.sb("row_of", [per, batches, WINDOW_ROWS], I32)
        window = m.sb("window", [per, batches, WINDOW_ROWS, 2 * HALF], I32)
        shape = [per, batches, WINDOW_ROWS, HALF]
        dstw, srcw, inside, after, loop, key = (m.sb(n, [per, batches, WINDOW]) for n in ("dstw", "srcw", "inside", "after", "loop", "key"))
        count = m.sb("count", [per, 4, batches])
        bad = m.sb("bad", [P, 4])
        top = m.sb("top", [per, batches, 8])
        keys = m.sb("keys", [per, batches, SLOTS])
        keys_int = m.sb("keys_int", [per, batches, SLOTS], I32)
        rel_out = m.sb("rel_out", [per, batches, SLOTS])
        slot_key = m.sb("slot_key", [P, batches, per], I32)
        order = m.sb("order", [P, 2, span], I32)
        orderf = m.sb("orderf", [P, span])
        turned = m.ps("turned", [P, -(-batches // 4) * 4, P])
        wrong = m.ps("wrong", [P, 512])
        loaded, based, started, gathered, own, round_own, passed, keys_turned, summed, rel_stored = (
            m.sem(n) for n in ("loaded", "based", "started", "gathered", "own", "round_own", "passed", "keys_turned", "summed", "rel_stored"))
        with nc.Block() as block:
            @block.sync
            def _(sp):
                sp.dma_start(head[:], heads.rearrange("(a r) -> a r", a=1).to_broadcast([per, rows])).then_inc(loaded, 16)
                for i in range(2):
                    sp.dma_start(order[:, i, :], line[i].rearrange("(p e) -> p e", p=P)).then_inc(loaded, 16)
                sp.wait_ge(summed, 1)
                sp.dma_start(rel_rows.rearrange("(b q) s -> q b s", q=per), rel_out[:]).then_inc(rel_stored, 16)
                sp.wait_ge(rel_stored, 16)

            @block.gpsimd
            def _(pool):
                pool.iota(base[:], [[per * P, batches]], base=0, channel_multiplier=P,
                          allow_small_or_imprecise_dtypes=True).then_inc(based, 1)
                pool.wait_ge(started, 1)
                for b in range(batches):
                    for r in range(WINDOW_ROWS):
                        pool.indirect_dma_start(out=window[:, b, r, :], out_offset=None, in_=ends,
                                                in_offset=bass.IndirectOffsetOnAxis(ap=row_of[:, b, r:r + 1], axis=0)
                                                ).then_inc(gathered, 16)

            @block.vector
            def _(dve):
                chain = Chain(dve, own, 0)

                def do(*instructions):
                    for instruction in instructions:
                        chain.mark(instruction)
                    chain.settle()

                dve.wait_ge(loaded, 48)
                dve.wait_ge(based, 1)
                do(dve.memset(bad[:], 0.0))
                do(dve.tensor_tensor(orderf[:], order[:, 1, :], order[:, 0, :], ALU.is_lt))
                do(dve.tensor_reduce(bad[:, 3:4], orderf[:], mybir.AxisListType.X, ALU.add))
                for b in range(batches):
                    do(dve.tensor_scalar(below[:], head[:], base[:, b:b + 1], None, ALU.is_lt))
                    do(dve.tensor_reduce(start[:, b:b + 1], below[:], mybir.AxisListType.X, ALU.add))
                do(dve.tensor_scalar(start[:], start[:], -1.0, 0.0, ALU.add, ALU.max))
                for r in range(WINDOW_ROWS):
                    last = dve.tensor_scalar(row_of[:, :, r], start[:], float(r), None, ALU.add)
                    chain.mark(last)
                chain.settle()
                dve.sem_inc(started, 1)
                dve.wait_ge(gathered, 16 * batches * WINDOW_ROWS)
                split = lambda ap: ap.rearrange("q b (r e) -> q b r e", e=HALF)
                for b in range(batches):
                    chain.mark(dve.tensor_copy(dstw[:, b].rearrange("q (r e) -> q r e", e=HALF), window[:, b, :, 0:HALF]))
                    chain.mark(dve.tensor_copy(srcw[:, b].rearrange("q (r e) -> q r e", e=HALF), window[:, b, :, HALF:2 * HALF]))
                chain.settle()
                do(dve.memset(after[:, :, WINDOW - 1:WINDOW], 0.0),
                   dve.tensor_tensor(after[:, :, 0:WINDOW - 1], dstw[:, :, 1:WINDOW], dstw[:, :, 0:WINDOW - 1], ALU.not_equal),
                   dve.tensor_tensor(loop[:], srcw[:], dstw[:], ALU.is_equal))
                do(dve.tensor_tensor(dstw[:], dstw[:], base[:].unsqueeze(2).to_broadcast([per, batches, WINDOW]), ALU.subtract))
                do(dve.tensor_tensor(loop[:], loop[:], after[:], ALU.mult))
                do(dve.tensor_scalar(inside[:], dstw[:], 0.0, None, ALU.is_ge),
                   dve.tensor_scalar(after[:], dstw[:], float(P), None, ALU.is_lt),
                   dve.scalar_tensor_tensor(key[:], dstw[:], float(1 << SRC_BITS), srcw[:], ALU.mult, ALU.add),
                   dve.tensor_scalar(count[:, 2, :], dstw[:, :, WINDOW - 1], float(P), None, ALU.is_lt))
                do(dve.tensor_tensor(inside[:], inside[:], after[:], ALU.mult))
                do(dve.tensor_tensor(loop[:], loop[:], inside[:], ALU.mult))
                do(dve.tensor_tensor(inside[:], inside[:], loop[:], ALU.subtract),
                   dve.tensor_reduce(count[:, 0, :], loop[:], mybir.AxisListType.X, ALU.add))
                do(dve.scalar_tensor_tensor(key[:], key[:], 1.0, inside[:], ALU.add, ALU.mult),
                   dve.tensor_reduce(count[:, 1, :], inside[:], mybir.AxisListType.X, ALU.add))
                do(dve.tensor_scalar(key[:], key[:], -1.0, None, ALU.add),
                   dve.tensor_scalar(count[:, 0, :], count[:, 0, :], float(P), None, ALU.not_equal),
                   dve.tensor_scalar(count[:, 1, :], count[:, 1, :], float(SLOTS), None, ALU.is_gt))
                do(dve.tensor_reduce(bad[0:per, 0:3], count[:, 0:3, :], mybir.AxisListType.X, ALU.add))

                def take(r):
                    start_of = r * ROUND
                    if not_first(r):
                        dve.wait_ge(round_own, start_of)
                        dve.sem_inc(passed, 1)
                    for b in range(batches):
                        dve.max(top[:, b, :], key[:, b, :]).then_inc(round_own, 1)
                    dve.wait_ge(round_own, start_of + batches)
                    dve.tensor_copy(keys[:, :, bass.ds(r * 8, 8)], top[:]).then_inc(round_own, 1)
                    for b in range(batches):
                        dve.match_replace(key[:, b, :], top[:, b, :], key[:, b, :], -1.0).then_inc(round_own, 1)

                take(0)
                with dve.Fori(1, SLOTS // 8) as r:
                    take(r)
                dve.wait_ge(round_own, SLOTS // 8 * ROUND)
                do(dve.tensor_copy(keys_int[:], keys[:]))
                do(dve.tensor_scalar(keys_int[:], keys_int[:], SRC_BITS, None, ALU.arith_shift_right))
                dve.tensor_copy(rel_out[:], keys_int[:]).then_inc(summed, 1)
                dve.wait_ge(keys_turned, 2)
                shaped = lambda ap: ap.rearrange("p (b q) -> p b q", q=per)
                do(dve.tensor_copy(slot_key[:], turned[:, 0:batches, 0:per]),
                   dve.tensor_scalar(k["regular"][0:1, 0:1], wrong[0:1, 0:1], 0.0, None, ALU.is_equal),
                   dve.tensor_scalar(k["regular"][0:1, 1:2], wrong[0:1, 0:1], 0.0, None, ALU.not_equal))
                do(dve.tensor_scalar(shaped(k["slot_src"][:]), slot_key[:], (1 << SRC_BITS) - 1, None, ALU.bitwise_and),
                   dve.tensor_scalar(slot_key[:], slot_key[:], SRC_BITS, None, ALU.arith_shift_right))
                do(dve.tensor_copy(shaped(k["slot_rel"][:]), slot_key[:]))

            @block.tensor
            def _(pe):
                pe.wait_ge(summed, 1)
                for b in range(batches):
                    last = pe.transpose(turned[:, b, 0:per], keys[:, b, :], k["ident"][0:per, 0:per])
                last.then_inc(keys_turned, 1)
                for c in range(4):
                    last = pe.matmul(wrong[0:1, 0:1], bad[:, c:c + 1], k["ones"][:], start=(c == 0), stop=(c == 3))
                last.then_inc(keys_turned, 1)


def clear_tables(nc, k, tables):
    WIDTH = 8 * D
    with ExitStack() as stack:
        m = Memory(nc, stack, "clear")
        zeros = m.sb("zeros", [P, WIDTH])
        cleared, stored = m.sem("cleared"), m.sem("stored")
        with nc.Block() as block:
            @block.vector
            def _(dve):
                dve.memset(zeros[:], 0.0).then_inc(cleared, 1)

            @block.sync
            def _(sp):
                with sp.If(k["irregular"]):
                    sp.wait_ge(cleared, 1)
                    stores = 0
                    for table in tables:
                        flat = table.rearrange("a b -> (a b)")
                        size = P * WIDTH
                        whole, rest = divmod(flat.shape[0], size)
                        for i in range(whole + (rest > 0)):
                            n = size if i < whole else rest
                            sp.dma_start(flat[i * size:i * size + n].rearrange("(p f) -> p f", p=P),
                                         zeros[:, 0:n // P]).then_inc(stored, 16)
                        stores += whole + (rest > 0)
                    sp.wait_ge(stored, 16 * stores)


def count_edges(nc, k, counts, chunks, rows, tiles):
    dst, place = k["dst"], k["place"]
    with ExitStack() as stack:
        m = Memory(nc, stack, "cnt")
        dstf = m.sb("dstf", [P, 2])
        same = m.sb("same", [P, 2, P])
        ranks = m.sb("ranks", [P, 2, P])
        small = m.sb("small", [P, 2, 4])
        total = m.sb("total", [P, 2])
        target = m.sb("target", [P, 2], I32)
        row = m.ps("row", [P, 2, 512])
        dst_ready, row_ready, own, fetched = (m.sem(n) for n in ("dst_ready", "row_ready", "own", "fetched"))
        added = m.sems("added", 2)
        passed = m.sem("passed")
        with nc.Block() as block:
            @block.vector
            def _(dve):
                @over_pairs(dve, chunks, k["irregular"])
                def _(pair):
                    for b in range(2):
                        c = pair * 2 + b
                        chain = Chain(dve, own, c * 8)
                        if not_first(pair):
                            dve.wait_ge(added[b], pair * 16)
                        dve.tensor_copy(dstf[:, b:b + 1], dst[:, bass.ds(c, 1)]).then_inc(dst_ready, 1)
                        dve.wait_ge(row_ready, c + 1)
                        dve.wait_ge(dst_ready, c + 1)
                        chain.mark(dve.tensor_scalar(same[:, b, :], row[:, b, 0:P], dstf[:, b:b + 1], None, ALU.is_equal))
                        chain.settle()
                        chain.mark(dve.tensor_reduce(total[:, b:b + 1], same[:, b, :], mybir.AxisListType.X, ALU.add))
                        chain.mark(dve.tensor_tensor(ranks[:, b, :], same[:, b, :], k["earlier"][:], ALU.mult))
                        chain.settle()
                        chain.mark(dve.tensor_reduce(small[:, b, 0:1], ranks[:, b, :], mybir.AxisListType.X, ALU.max))
                        chain.mark(dve.scalar_tensor_tensor(small[:, b, 1:2], k["trash"][:], float(rows), dstf[:, b:b + 1], ALU.add, ALU.subtract))
                        chain.settle()
                        chain.mark(dve.tensor_tensor(small[:, b, 2:3], small[:, b, 0:1], small[:, b, 1:2], ALU.mult))
                        chain.settle()
                        chain.mark(dve.tensor_tensor(target[:, b:b + 1], small[:, b, 2:3], dstf[:, b:b + 1], ALU.add))
                        chain.settle()
                        chain.mark(dve.tensor_copy(place[:, bass.ds(c, 1)], target[:, b:b + 1]))

            @block.tensor
            def _(pe):
                @over_pairs(pe, chunks, k["irregular"])
                def _(pair):
                    for b in range(2):
                        c = pair * 2 + b
                        pe.wait_ge(dst_ready, c + 1)
                        pe.matmul(row[:, b, 0:P], dstf[:, b:b + 1].to_broadcast([P, P]), k["ident"][:],
                                  start=True, stop=True).then_inc(row_ready, 1)

            @block.gpsimd
            def _(pool):
                @over_pairs(pool, chunks, k["irregular"])
                def _(pair):
                    for b in range(2):
                        pool.wait_ge(own, (pair * 2 + b + 1) * 8)
                        if b or not_first(pair):
                            pool.wait_ge(added[1 - b], (pair + b) * 16)
                        pool.sem_inc(passed, 1)
                        pool.indirect_dma_start(
                            out=counts, out_offset=bass.IndirectOffsetOnAxis(ap=target[:, b:b + 1], axis=0),
                            in_=total[:, b:b + 1], in_offset=None, compute_op=ALU.add).then_inc(added[b], 16)
                with pool.If(k["irregular"]):
                    for b in range(2):
                        pool.wait_ge(added[b], chunks // 2 * 16)

            @block.sync
            def _(sp):
                with sp.If(k["irregular"]):
                    for b in range(2):
                        sp.wait_ge(added[b], chunks // 2 * 16)
                    sp.dma_start(k["edges"][:], counts[0:tiles * P, :].rearrange("(t p) o -> p (t o)", p=P),
                                 allow_slow_non_contiguous=True).then_inc(fetched, 16)
                    sp.wait_ge(fetched, 16)


def degrees(nc, k, tiles):
    with ExitStack() as stack:
        m = Memory(nc, stack, "deg")
        counted, rooted = m.sem("counted"), m.sem("rooted")
        with nc.Block() as block:
            @block.vector
            def _(dve):
                with dve.If(k["irregular"]):
                    dve.tensor_scalar(k["edges"][:], k["edges"][:], 1.0, 1.0, ALU.add, ALU.max).then_inc(counted, 1)
                    dve.wait_ge(rooted, 1)
                    dve.reciprocal(k["dinv"][:], k["root"][:])

            @block.scalar
            def _(act):
                with act.If(k["irregular"]):
                    act.wait_ge(counted, 1)
                    act.activation(k["root"][:], k["edges"][:], ACT.Sqrt).then_inc(rooted, 1)


def make_messages(nc, k, x, y, units):
    X, Y = by_unit(x), by_unit(y)
    RING = 8
    HALVES = slice(0, TILES // 2), slice(TILES // 2, TILES)
    with ExitStack() as stack:
        m = Memory(nc, stack, "msg")
        x_in = m.sb("x_in", [P, RING, TILES, D])
        stats = m.sb("stats", [P, 2, TILES, 6])
        small = m.sb("small", [P, 4, 6, TILES])
        hot = m.sb("hot", [P, 2, TILES, P])
        degree = m.sb("degree", [P, 2, TILES])
        scale = m.sb("scale", [P, 4, TILES])
        xn, xg, offset = (m.sb(n, [P, 2, TILES, D]) for n in ("xn", "xg", "offset"))
        y_out = m.sb("y_out", [P, RING, TILES, D])
        edges = m.ps("edges", [P, 2, UNIT])
        x_loaded, y_stored = m.sems("x_loaded", RING), m.sems("y_stored", RING)
        (measured, own, rooted, inverted, scale_ready, shifted, xn_ready, offset_ready, xg_ready, y_first, y_second, hot_ready,
         edges_counted, degree_ready, root_ready, dinv_ready) = (
            m.sem(n) for n in ("measured", "own", "rooted", "inverted", "scale_ready", "shifted", "xn_ready", "offset_ready",
                               "xg_ready", "y_first", "y_second", "hot_ready", "edges_counted", "degree_ready",
                               "root_ready", "dinv_ready"))
        of_unit = lambda table, s: table[:, bass.ds(s.u * TILES, TILES)]
        with nc.Block() as block:
            @block.sync
            def _(sp):
                def load(s):
                    if late(s, RING):
                        sp.wait_ge(xn_ready, s.u - RING + 1)
                    sp.dma_start(x_in[:, s.slot], X[s.u]).then_inc(x_loaded[s.slot], 16)

                def store(s):
                    sp.wait_ge(y_first, s.u + 1)
                    sp.wait_ge(y_second, s.u + 1)
                    sp.dma_start(Y[s.u], y_out[:, s.slot]).then_inc(y_stored[s.slot], 16)

                over_units(sp, units, [(0, load), (8, store)], RING)
                for slot, q in enumerate(y_stored):
                    sp.wait_ge(q, len(range(slot, units, RING)) * 16)

            @block.vector
            def _(dve):
                norms = Norms(dve, own, stats, small)

                def measure(s, half):
                    if half == 0:
                        dve.wait_ge(x_loaded[s.slot], (s.lap + 1) * 16)
                    for t in range(2 * half, 2 * half + 2):
                        last = dve.bn_stats(stats[:, s.slot % 2, t, :], x_in[:, s.slot, t, :])
                    if half:
                        last.then_inc(measured, 1)

                def means(s):
                    dve.wait_ge(measured, s.u + 1)
                    if late(s, 4):
                        dve.wait_ge(xn_ready, s.u - 3)
                    norms.means(s)

                def invert(s):
                    dve.wait_ge(rooted, s.u + 1)
                    dve.reciprocal(small[:, s.slot % 4, 4, :], small[:, s.slot % 4, 4, :]).then_inc(inverted, 1)

                def combine(s):
                    dve.wait_ge(inverted, s.u + 1)
                    dve.tensor_tensor(scale[:, s.slot % 4], small[:, s.slot % 4, 4, :], of_unit(k["dinv"], s), ALU.mult).then_inc(scale_ready, 1)

                def combine_counted(s):
                    dve.wait_ge(dinv_ready, s.u + 1)
                    combine(s)

                def shift(s):
                    b = s.slot % 4
                    dve.wait_ge(scale_ready, s.u + 1)
                    dve.scalar_tensor_tensor(small[:, b, 5, :], small[:, b, 0, :], -0.5, scale[:, b], ALU.mult, ALU.mult).then_inc(shifted, 1)

                def one_hot(s):
                    if late(s, 2):
                        dve.wait_ge(edges_counted, s.u - 1)
                    dve.tensor_tensor(hot[:, s.slot % 2], k["lane"][:].unsqueeze(1).to_broadcast([P, TILES, P]),
                                      spread(of_unit(k["slot_rel"], s), P), ALU.is_equal).then_inc(hot_ready, 1)

                def count(s):
                    b = s.slot % 2
                    dve.wait_ge(edges_counted, s.u + 1)
                    if late(s, 2):
                        dve.wait_ge(root_ready, s.u - 1)
                    dve.tensor_scalar(degree[:, b], edges[:, b, 0:TILES], 2.0, 1.0, ALU.add, ALU.max).then_inc(degree_ready, 1)

                def invert_root(s):
                    dve.wait_ge(root_ready, s.u + 1)
                    dve.reciprocal(of_unit(k["dinv"], s), of_unit(k["root"], s)).then_inc(dinv_ready, 1)

                def finish(s):
                    dve.wait_ge(xg_ready, s.u + 1)
                    if late(s, RING):
                        dve.wait_ge(y_stored[s.slot], s.lap * 16)
                    for t in range(TILES)[HALVES[0]]:
                        last = dve.scalar_tensor_tensor(y_out[:, s.slot, t, :], k["ln_b_row"][:], k["dinv"][:, bass.ds(s.u * TILES + t, 1)],
                                                        xg[:, s.slot % 2, t, :], ALU.mult, ALU.add)
                    last.then_inc(y_first, 1)

                first, second = (1, lambda s: measure(s, 0)), (1, lambda s: measure(s, 1))
                with dve.If(k["is_regular"]):
                    over_units(dve, units, [(4, invert), (4, invert_root), (2, means), first, (4, combine_counted), (0, one_hot),
                                            (2, norms.squares), (4, shift), second, (2, norms.variance), (2, count),
                                            (7, finish)], RING)
                with dve.If(k["irregular"]):
                    over_units(dve, units, [(4, invert), (2, means), first, (4, combine), (2, norms.squares), second, (4, shift),
                                            (2, norms.variance), (7, finish)], RING)

            @block.scalar
            def _(act):
                def root(s):
                    act.wait_ge(own, (s.u + 1) * SMALLS)
                    act.activation(small[:, s.slot % 4, 4, :], small[:, s.slot % 4, 3, :], ACT.Sqrt).then_inc(rooted, 1)

                def root_degree(s):
                    act.wait_ge(degree_ready, s.u + 1)
                    act.activation(of_unit(k["root"], s), degree[:, s.slot % 2], ACT.Sqrt).then_inc(root_ready, 1)

                def apply(s):
                    b = s.slot % 2
                    act.wait_ge(shifted, s.u + 1)
                    if late(s, 2):
                        act.wait_ge(xg_ready, s.u - 1)
                    for t in range(TILES):
                        last = act.activation(xn[:, b, t, :], x_in[:, s.slot, t, :], ACT.Identity,
                                              bias=small[:, s.slot % 4, 5, t:t + 1], scale=scale[:, s.slot % 4, t:t + 1])
                    last.then_inc(xn_ready, 1)

                def offsets(s):
                    if late(s, 2):
                        act.wait_ge(y_second, s.u - 1)
                    for t in range(TILES)[HALVES[1]]:
                        last = act.activation(offset[:, s.slot % 2, t, :], k["ln_b_row"][:], ACT.Identity,
                                              bias=k["zero"][:], scale=k["dinv"][:, bass.ds(s.u * TILES + t, 1)])
                    last.then_inc(offset_ready, 1)

                with act.If(k["is_regular"]):
                    over_units(act, units, [(3, root), (3, root_degree), (5, apply), (5, offsets)], RING)
                with act.If(k["irregular"]):
                    over_units(act, units, [(3, root), (5, apply), (5, offsets)], RING)

            @block.gpsimd
            def _(pool):
                def gain(s):
                    b = s.slot % 2
                    pool.wait_ge(xn_ready, s.u + 1)
                    if late(s, 2):
                        pool.wait_ge(y_first, s.u - 1)
                        pool.wait_ge(y_second, s.u - 1)
                    pool.tensor_tensor(xg[:, b], xn[:, b], k["ln_g_row"][:].unsqueeze(1).to_broadcast([P, TILES, D]), ALU.mult).then_inc(xg_ready, 1)

                def finish(s):
                    pool.wait_ge(offset_ready, s.u + 1)
                    pool.wait_ge(xg_ready, s.u + 1)
                    if late(s, RING):
                        pool.wait_ge(y_stored[s.slot], s.lap * 16)
                    pool.tensor_tensor(y_out[:, s.slot, HALVES[1], :], xg[:, s.slot % 2, HALVES[1], :],
                                       offset[:, s.slot % 2, HALVES[1], :], ALU.add).then_inc(y_second, 1)

                over_units(pool, units, [(5, gain), (6, finish)], RING)

            @block.tensor
            def _(pe):
                def count(s):
                    b = s.slot % 2
                    pe.wait_ge(hot_ready, s.u + 1)
                    if late(s, 2):
                        pe.wait_ge(degree_ready, s.u - 1)
                    for t in range(TILES):
                        last = pe.matmul(edges[:, b, t:t + 1], hot[:, b, t, :], k["ones"][:], start=True, stop=True)
                    last.then_inc(edges_counted, 1)

                with pe.If(k["is_regular"]):
                    over_units(pe, units, [(1, count)], RING)


def add_messages(nc, k, y, sums, chunks, edge_net=None):
    src, dst, place = k["src"], k["dst"], k["place"]
    with ExitStack() as stack:
        m = Memory(nc, stack, "add1" if edge_net is None else "add2")
        dstf = m.sb("dstf", [P, 2])
        src_row, dst_row, target = (m.sb(n, [P, 2], I32) for n in ("src_row", "dst_row", "target"))
        same = m.sb("same", [P, 2, P])
        from_src = m.sb("from_src", [P, 2, D])
        from_dst = m.sb("from_dst", [P, 2, D])
        bothT = m.sb("bothT", [P, 2, 2, P])
        hidden = m.sb("hidden", [P, 2, P])
        weight = m.sb("weight", [P, 2])
        message = m.sb("message", [P, 2, D])
        out = m.sb("out", [P, 2, D])
        row = m.ps("row", [P, 2, 512])
        total = m.ps("total", [P, 2, 512])
        turned = m.ps("turned", [P, 512])
        pre = m.ps("pre", [P, 512])
        dots = m.ps("dots", [P, 512])
        (index_ready, row_ready, same_ready, total_ready, out_ready, turned_ready, bothT_ready, pre_ready,
         hidden_ready, dot_ready, weight_ready, message_ready) = (
            m.sem(n) for n in ("index_ready", "row_ready", "same_ready", "total_ready", "out_ready", "turned_ready",
                               "bothT_ready", "pre_ready", "hidden_ready", "dot_ready", "weight_ready", "message_ready"))
        src_in, dst_in, added = m.sems("src_in", 2), m.sems("dst_in", 2), m.sems("added", 2)
        passed = m.sem("passed")

        def over_chunks(eng, body):
            @over_pairs(eng, chunks, k["irregular"])
            def _(pair):
                for b in range(2):
                    body(pair, b, pair * 2 + b)

        with nc.Block() as block:
            @block.vector
            def _(dve):
                def chunk(pair, b, c):
                    if not_first(pair):
                        dve.wait_ge(added[b], pair * 16)
                    dve.tensor_copy(dstf[:, b:b + 1], dst[:, bass.ds(c, 1)]).then_inc(index_ready, 1)
                    dve.tensor_copy(src_row[:, b:b + 1], src[:, bass.ds(c, 1)]).then_inc(index_ready, 1)
                    dve.tensor_copy(dst_row[:, b:b + 1], dst[:, bass.ds(c, 1)]).then_inc(index_ready, 1)
                    dve.tensor_copy(target[:, b:b + 1], place[:, bass.ds(c, 1)]).then_inc(index_ready, 1)
                    dve.wait_ge(row_ready, c + 1)
                    dve.wait_ge(index_ready, (c + 1) * 4)
                    dve.tensor_scalar(same[:, b, :], row[:, b, 0:P], dstf[:, b:b + 1], None, ALU.is_equal).then_inc(same_ready, 1)
                    if edge_net is not None:
                        dve.wait_ge(weight_ready, c + 1)
                        dve.wait_ge(src_in[b], (pair + 1) * 16)
                        dve.tensor_scalar(message[:, b, :], from_src[:, b, :], weight[:, b:b + 1], None, ALU.mult).then_inc(message_ready, 1)

                over_chunks(dve, chunk)

            @block.gpsimd
            def _(pool):
                @over_pairs(pool, chunks, k["irregular"])
                def _(pair):
                    for b in range(2):
                        pool.wait_ge(index_ready, (pair * 2 + b + 1) * 4)
                        pool.sem_inc(passed, 1)
                        pool.indirect_dma_start(out=from_src[:, b, :], out_offset=None, in_=y,
                                                in_offset=bass.IndirectOffsetOnAxis(ap=src_row[:, b:b + 1], axis=0)
                                                ).then_inc(src_in[b], 16)
                        if edge_net is not None:
                            pool.indirect_dma_start(out=from_dst[:, b, :], out_offset=None, in_=y,
                                                    in_offset=bass.IndirectOffsetOnAxis(ap=dst_row[:, b:b + 1], axis=0)
                                                    ).then_inc(dst_in[b], 16)
                    for b in range(2):
                        pool.wait_ge(out_ready, pair * 2 + b + 1)
                        if b or not_first(pair):
                            pool.wait_ge(added[1 - b], (pair + b) * 16)
                        pool.sem_inc(passed, 1)
                        pool.indirect_dma_start(
                            out=sums, out_offset=bass.IndirectOffsetOnAxis(ap=target[:, b:b + 1], axis=0),
                            in_=out[:, b, :], in_offset=None, compute_op=ALU.add).then_inc(added[b], 16)
                with pool.If(k["irregular"]):
                    for b in range(2):
                        pool.wait_ge(added[b], chunks // 2 * 16)

            @block.tensor
            def _(pe):
                def chunk(pair, b, c):
                    pe.wait_ge(index_ready, c * 4 + 1)
                    pe.matmul(row[:, b, 0:P], dstf[:, b:b + 1].to_broadcast([P, P]), k["ident"][:],
                              start=True, stop=True).then_inc(row_ready, 1)
                    pe.wait_ge(src_in[b], (pair + 1) * 16)
                    if edge_net is not None:
                        pe.wait_ge(dst_in[b], (pair + 1) * 16)
                        if not_first(c):
                            pe.wait_ge(bothT_ready, c)
                        pe.transpose(turned[:, 0:P], from_src[:, b, :], k["ident"][:])
                        pe.transpose(turned[:, P:2 * P], from_dst[:, b, :], k["ident"][:]).then_inc(turned_ready, 1)
                        pe.wait_ge(bothT_ready, c + 1)
                        if not_first(c):
                            pe.wait_ge(hidden_ready, c)
                        for half in range(2):
                            last = pe.matmul(pre[:, 0:P], edge_net["We1"][:, half, :], bothT[:, b, half, :],
                                             start=(half == 0), stop=(half == 1))
                        last.then_inc(pre_ready, 1)
                        pe.wait_ge(hidden_ready, c + 1)
                        if not_first(c):
                            pe.wait_ge(weight_ready, c)
                        pe.matmul(dots[:, 0:1], hidden[:, b, :], edge_net["We2"][:], start=True, stop=True).then_inc(dot_ready, 1)
                        pe.wait_ge(message_ready, c + 1)
                    pe.wait_ge(same_ready, c + 1)
                    pe.matmul(total[:, b, 0:D], same[:, b, :], from_src[:, b, :] if edge_net is None else message[:, b, :],
                              start=True, stop=True).then_inc(total_ready, 1)

                over_chunks(pe, chunk)

            @block.scalar
            def _(act):
                def chunk(pair, b, c):
                    if edge_net is not None:
                        act.wait_ge(turned_ready, c + 1)
                        act.activation(bothT[:, b].rearrange("p a b -> p (a b)"), turned[:, 0:2 * P], ACT.Copy).then_inc(bothT_ready, 1)
                        act.wait_ge(pre_ready, c + 1)
                        act.activation(hidden[:, b, :], pre[:, 0:P], ACT.Relu, bias=edge_net["be1"][:]).then_inc(hidden_ready, 1)
                        act.wait_ge(dot_ready, c + 1)
                        act.activation(weight[:, b:b + 1], dots[:, 0:1], ACT.Sigmoid, bias=edge_net["be2"][:]).then_inc(weight_ready, 1)
                    act.wait_ge(total_ready, c + 1)
                    act.activation(out[:, b, :], total[:, b, 0:D], ACT.Copy).then_inc(out_ready, 1)

                over_chunks(act, chunk)


def convolve(nc, k, y, sums, outT, units, nodes):
    Y, SUMS = by_unit(y), by_unit(sums[0:units * UNIT, :])
    STAT_OWN = 4
    last_valid = nodes - (units - 1) * UNIT
    with ExitStack() as stack:
        m = Memory(nc, stack, "conv")
        y_in = m.sb("y_in", [P, RING, TILES, D])
        s_in = m.sb("s_in", [P, RING, TILES, D])
        gathered = m.sb("gathered", [P, 2, TILES, D])
        rows = m.sb("rows", [P, RING, TILES, D])
        hot = m.sb("hot", [P, 2, TILES, P])
        slot_src = m.sb("slot_src", [P, RING, TILES], I32)
        sum_ps = m.ps("sum_ps", [P, 2, UNIT])
        rows_loaded = m.sems("rows_loaded", RING)
        (rows_clear, slots_ready, hot_ready, sums_ready, passed) = (
            m.sem(n) for n in ("rows_clear", "slots_ready", "hot_ready", "sums_ready", "passed"))
        own_x = m.sb("own_x", [P, 2, TILES, D])
        gT = m.sb("gT", [P, 2, UNIT])
        xT = m.sb("xT", [P, 2, UNIT])
        o_out = m.sb("o_out", [P, RING, UNIT])
        stats = m.sb("stats", [P, units, 6])
        bn = m.sb("bn", [P, 8])
        g_turned, x_turned, o_ps = (m.ps(n, [P, 2, UNIT]) for n in ("g_turned", "x_turned", "o_ps"))
        y_loaded, s_loaded, o_stored = (m.sems(n, RING) for n in ("y_loaded", "s_loaded", "o_stored"))
        summed, scaled, turned, copied, product, o_ready, measured, bn_own, bn_var, bn_rstd = (
            m.sem(n) for n in ("summed", "scaled", "turned", "copied", "product", "o_ready", "measured", "bn_own", "bn_var", "bn_rstd"))
        with nc.Block() as block:
            @block.sync
            def _(sp):
                def load(s):
                    if late(s, RING):
                        sp.wait_ge(scaled, (s.u - RING + 1) * 2)
                    sp.dma_start(y_in[:, s.slot], Y[s.u]).then_inc(y_loaded[s.slot], 16)

                def load_both(s):
                    load(s)
                    sp.dma_start(s_in[:, s.slot], SUMS[s.u]).then_inc(s_loaded[s.slot], 16)

                def store(s):
                    sp.wait_ge(o_ready, s.u + 1)
                    sp.dma_start(outT[:, bass.ds(s.u * UNIT, UNIT)], o_out[:, s.slot]).then_inc(o_stored[s.slot], 16)

                with sp.If(k["is_regular"]):
                    over_units(sp, units, [(4, store), (0, load)])
                with sp.If(k["irregular"]):
                    over_units(sp, units, [(4, store), (0, load_both)])
                for q in o_stored:
                    sp.wait_ge(q, units // RING * 16)

            @block.vector
            def _(dve):
                def one_hot(s):
                    if late(s, 2):
                        dve.wait_ge(sums_ready, s.u - 1)
                    dve.tensor_tensor(hot[:, s.slot % 2], k["lane"][:].unsqueeze(1).to_broadcast([P, TILES, P]),
                                      spread(k["slot_rel"][:, bass.ds(s.u * TILES, TILES)], P), ALU.is_equal).then_inc(hot_ready, 1)

                def copy_slots(s):
                    if late(s, RING):
                        dve.wait_ge(rows_loaded[s.slot], s.lap * 16 * TILES)
                    dve.tensor_copy(slot_src[:, s.slot, :], k["slot_src"][:, bass.ds(s.u * TILES, TILES)]).then_inc(slots_ready, 1)

                def scale_made(s):
                    dve.wait_ge(y_loaded[s.slot], (s.lap + 1) * 16)
                    dve.wait_ge(sums_ready, s.u + 1)
                    if late(s, RING):
                        dve.wait_ge(scaled, (s.u - RING + 1) * 2)
                    dve.scalar_tensor_tensor(s_in[:, s.slot], y_in[:, s.slot], 2.0,
                                             sum_ps[:, s.slot % 2].rearrange("p (t f) -> p t f", t=TILES), ALU.mult, ALU.add).then_inc(summed, 1)
                    scale(s)

                def scale_read(s):
                    dve.wait_ge(y_loaded[s.slot], (s.lap + 1) * 16)
                    dve.wait_ge(s_loaded[s.slot], (s.lap + 1) * 16)
                    dve.tensor_tensor(s_in[:, s.slot], s_in[:, s.slot], y_in[:, s.slot], ALU.add).then_inc(summed, 1)
                    scale(s)

                def scale(s):
                    b = s.slot % 2
                    if late(s, 2):
                        dve.wait_ge(turned, s.u - 1)
                    dve.tensor_tensor(own_x[:, b], y_in[:, s.slot], spread(k["root"][:, bass.ds(s.u * TILES, TILES)], D),
                                      ALU.mult).then_inc(scaled, 1)
                    dve.wait_ge(summed, s.u + 1)
                    dve.tensor_tensor(gathered[:, b], s_in[:, s.slot], spread(k["dinv"][:, bass.ds(s.u * TILES, TILES)], D),
                                      ALU.mult).then_inc(scaled, 1)

                def measure(s):
                    dve.wait_ge(o_ready, s.u + 1)
                    dve.bn_stats(stats[:, bass.ds(s.u, 1), :].rearrange("p a b -> p (a b)"), o_out[:, s.slot]).then_inc(measured, 1)

                with dve.If(k["is_regular"]):
                    dve.memset(rows[:], 0.0).then_inc(rows_clear, 1)
                    over_units(dve, units, [(2, one_hot), (4, scale_made), (0, copy_slots), (7, measure)])
                with dve.If(k["irregular"]):
                    over_units(dve, units, [(2, measure), (0, scale_read)])
                dve.wait_ge(measured, units)
                dve.bn_stats(stats[:, units - 1, :], o_out[:, RING - 1, 0:last_valid]).then_inc(bn_own, 1)
                dve.wait_ge(bn_own, 1)
                dve.bn_aggr(bn[:, 0:2], stats[:].rearrange("p a b -> p (a b)")).then_inc(bn_own, 1)
                dve.wait_ge(bn_own, 2)
                dve.tensor_scalar(bn[:, 2:3], bn[:, 1:2], EPS, None, ALU.add).then_inc(bn_var, 1)
                dve.wait_ge(bn_rstd, 1)
                dve.tensor_tensor(k["bn_scale"][:], bn[:, 3:4], k["bn_g"][:], ALU.mult).then_inc(bn_own, 1)
                dve.wait_ge(bn_own, 3)
                dve.tensor_tensor(bn[:, 4:5], bn[:, 0:1], k["bn_scale"][:], ALU.mult).then_inc(bn_own, 1)
                dve.wait_ge(bn_own, 4)
                dve.tensor_tensor(k["bn_shift"][:], k["bn_b"][:], bn[:, 4:5], ALU.subtract)

            @block.gpsimd
            def _(pool):
                def gather(s):
                    if late(s, RING):
                        pool.wait_ge(sums_ready, s.u - RING + 1)
                    pool.wait_ge(slots_ready, s.u + 1)
                    pool.sem_inc(passed, 1)
                    for t in range(TILES):
                        pool.indirect_dma_start(out=rows[:, s.slot, t, :], out_offset=None, in_=y,
                                                in_offset=bass.IndirectOffsetOnAxis(ap=slot_src[:, s.slot, t:t + 1], axis=0),
                                                bounds_check=units * UNIT - 1, oob_is_err=False).then_inc(rows_loaded[s.slot], 16)

                with pool.If(k["is_regular"]):
                    pool.wait_ge(rows_clear, 1)
                    over_units(pool, units, [(0, gather)])
                pool.wait_ge(bn_var, 1)
                pool.tensor_tensor(bn[:, 3:4], bn[:, 2:3], k["power"][:, 0:1], ALU.pow).then_inc(bn_rstd, 1)

            @block.tensor
            def _(pe):
                def turn(s):
                    b = s.slot % 2
                    pe.wait_ge(scaled, (s.u + 1) * 2)
                    if late(s, 2):
                        pe.wait_ge(copied, (s.u - 1) * 2)
                    for t in range(TILES):
                        pe.transpose(g_turned[:, b, t * P:(t + 1) * P], gathered[:, b, t, :], k["ident"][:])
                        last = pe.transpose(x_turned[:, b, t * P:(t + 1) * P], own_x[:, b, t, :], k["ident"][:])
                    last.then_inc(turned, 1)

                def multiply(s):
                    b = s.slot % 2
                    pe.wait_ge(copied, (s.u + 1) * 2)
                    if late(s, 2):
                        pe.wait_ge(o_ready, s.u - 1)
                    pe.matmul(o_ps[:, b], k["gcn_w"][:], gT[:, b], start=True, stop=False)
                    pe.matmul(o_ps[:, b], k["rs_w"][:], xT[:, b], start=False, stop=True).then_inc(product, 1)

                def gather_sums(s):
                    b = s.slot % 2
                    pe.wait_ge(hot_ready, s.u + 1)
                    pe.wait_ge(rows_loaded[s.slot], (s.lap + 1) * 16 * TILES)
                    if late(s, 2):
                        pe.wait_ge(summed, s.u - 1)
                    for t in range(TILES):
                        last = pe.matmul(sum_ps[:, b, t * P:(t + 1) * P], hot[:, b, t, :], rows[:, s.slot, t, :], start=True, stop=True)
                    last.then_inc(sums_ready, 1)

                with pe.If(k["is_regular"]):
                    over_units(pe, units, [(0, gather_sums), (3, multiply), (2, turn)])
                with pe.If(k["irregular"]):
                    over_units(pe, units, [(1, multiply), (0, turn)])

            @block.scalar
            def _(act):
                def copy(s):
                    b = s.slot % 2
                    act.wait_ge(turned, s.u + 1)
                    if late(s, 2):
                        act.wait_ge(product, s.u - 1)
                    act.activation(gT[:, b], g_turned[:, b], ACT.Copy).then_inc(copied, 1)
                    act.activation(xT[:, b], x_turned[:, b], ACT.Copy).then_inc(copied, 1)

                def bias(s):
                    b = s.slot % 2
                    act.wait_ge(product, s.u + 1)
                    if late(s, RING):
                        act.wait_ge(o_stored[s.slot], s.lap * 16)
                        act.wait_ge(measured, s.u - RING + 1)
                    act.activation(o_out[:, s.slot], o_ps[:, b], ACT.Identity, bias=k["conv_b"][:]).then_inc(o_ready, 1)

                over_units(act, units, [(1, bias), (0, copy)])


def embed(nc, k, x, outT, x1, h, units):
    X, X1, H = by_unit(x), by_unit(x1), by_unit(h)
    NEXT = 6
    with ExitStack() as stack:
        m = Memory(nc, stack, "emb")
        x_in = m.sb("x_in", [P, RING, TILES, D])
        o_in = m.sb("o_in", [P, RING, UNIT])
        bnT, leaky = (m.sb(n, [P, 2, UNIT]) for n in ("bnT", "leaky"))
        mixed, hidden = (m.sb(n, [P, RING, TILES, D]) for n in ("mixed", "hidden"))
        hn, centred = (m.sb(n, [P, 2, TILES, D]) for n in ("hn", "centred"))
        stats = m.sb("stats", [P, 2, 2 * TILES, 6])
        small = m.sb("small", [P, RING, 6, 2 * TILES])
        x1_out, x1_biased, h_out = (m.sb(n, [P, RING, TILES, D]) for n in ("x1_out", "x1_biased", "h_out"))
        x1_last = m.sb("x1_last", [P, 1, D])
        We1_sum = m.sb("We1_sum", [P, D])
        x1T, hT, pair_hidden = (m.sb(n, [P, 2, UNIT]) for n in ("x1T", "hT", "pair_hidden"))
        leaky_ps = m.ps("leaky_ps", [P, 2, UNIT])
        x1_turned, w1_ps, h_turned, h_back, pair_ps, dots = (
            m.ps(n, [P, UNIT]) for n in ("x1_turned", "w1_ps", "h_turned", "h_back", "pair_ps", "dots"))
        x_loaded, o_loaded, x1_stored, h_stored = (m.sems(n, RING) for n in ("x_loaded", "o_loaded", "x1_stored", "h_stored"))
        (cleared, bn_ready, leaky_ready, leaky_turned, mixed_ready, measured1, measured2, own, rooted, inverted, shifted,
         x1_ready, x1_scaled, x1_last_ready, biased, halves_summed, x1_turn_ready, x1T_ready, w1_ready, hidden_ready, centred_ready, hn_ready, h_turn_ready, hT_ready,
         h_back_ready, h_ready, pair_product, pair_ready, dot_product, dot_kept) = (
            m.sem(n) for n in ("cleared", "bn_ready", "leaky_ready", "leaky_turned", "mixed_ready", "measured1",
                               "measured2", "own", "rooted", "inverted", "shifted", "x1_ready", "x1_scaled", "x1_last_ready", "biased", "halves_summed", "x1_turn_ready", "x1T_ready",
                               "w1_ready", "hidden_ready", "centred_ready", "hn_ready", "h_turn_ready", "hT_ready",
                               "h_back_ready", "h_ready", "pair_product", "pair_ready", "dot_product", "dot_kept"))
        tiled = lambda ap: ap.rearrange("p (t f) -> p t f", t=TILES)
        with nc.Block() as block:
            @block.sync
            def _(sp):
                def load(s):
                    if late(s, RING):
                        sp.wait_ge(mixed_ready, s.u - RING + 1)
                        sp.wait_ge(bn_ready, s.u - RING + 1)
                    sp.dma_start(x_in[:, s.slot], X[s.u]).then_inc(x_loaded[s.slot], 16)
                    sp.dma_start(o_in[:, s.slot], outT[:, bass.ds(s.u * UNIT, UNIT)]).then_inc(o_loaded[s.slot], 16)

                def store_x1(s):
                    sp.wait_ge(biased, s.u + 1)
                    sp.dma_start(X1[s.u], x1_biased[:, s.slot]).then_inc(x1_stored[s.slot], 16)

                def store_h(s):
                    sp.wait_ge(h_ready, s.u + 1)
                    sp.dma_start(H[s.u], h_out[:, s.slot]).then_inc(h_stored[s.slot], 16)

                over_units(sp, units, [(0, load), (7, store_x1), (14, store_h)])
                for q in x1_stored + h_stored:
                    sp.wait_ge(q, units // RING * 16)

            @block.scalar
            def _(act):
                def affine(s):
                    act.wait_ge(h_turn_ready, s.u + 1)
                    if late(s, 2):
                        act.wait_ge(h_back_ready, s.u - 1)
                        act.wait_ge(pair_product, s.u - 1)
                    act.activation(hT[:, s.slot % 2], h_turned[:], ACT.Relu, bias=k["bt1"][:], scale=k["g1"][:]).then_inc(hT_ready, 1)

                def copy_h(s):
                    act.wait_ge(h_back_ready, s.u + 1)
                    if late(s, RING):
                        act.wait_ge(h_stored[s.slot], s.lap * 16)
                    act.activation(h_out[:, s.slot], tiled(h_back[:]), ACT.Copy).then_inc(h_ready, 1)

                def pair(s):
                    act.wait_ge(pair_product, s.u + 1)
                    if late(s, 2):
                        act.wait_ge(dot_product, s.u - 1)
                    act.activation(pair_hidden[:, s.slot % 2], pair_ps[:], ACT.Relu, bias=k["be1"][:]).then_inc(pair_ready, 1)

                def root(j):
                    b = j.slot
                    act.wait_ge(own, (j.u + 1) * SMALLS)
                    act.activation(small[:, b, 4, :], small[:, b, 3, :], ACT.Sqrt).then_inc(rooted, 1)

                def copy_x1(s):
                    act.wait_ge(x1_turn_ready, s.u + 1)
                    if late(s, 2):
                        act.wait_ge(w1_ready, s.u - 1)
                    act.activation(x1T[:, s.slot % 2], x1_turned[:], ACT.Copy).then_inc(x1T_ready, 1)

                def normalise(s):
                    act.wait_ge(o_loaded[s.slot], (s.lap + 1) * 16)
                    if late(s, 2):
                        act.wait_ge(leaky_ready, s.u - 1)
                    act.activation(bnT[:, s.slot % 2], o_in[:, s.slot], ACT.Identity, bias=k["bn_shift"][:],
                                   scale=k["bn_scale"][:]).then_inc(bn_ready, 1)

                def apply1(s):
                    b = s.slot
                    act.wait_ge(shifted, s.u + 1)
                    if late(s, RING):
                        act.wait_ge(biased, s.u - RING + 1)
                        act.wait_ge(x1_turn_ready, s.u - RING + 1)
                    for t in range(TILES - 1):
                        last = act.activation(x1_out[:, s.slot, t, :], mixed[:, b, t, :], ACT.Identity,
                                              bias=small[:, b, 5, t:t + 1], scale=small[:, b, 4, t:t + 1])
                    last.then_inc(x1_ready, 1)

                over_units(act, units, [(4, root, NEXT), (0, normalise), (13, copy_h), (13, pair), (12, affine), (6, copy_x1),
                                        (5, apply1)])

            @block.vector
            def _(dve):
                norms = Norms(dve, own, stats, small)

                def hide(s):
                    dve.wait_ge(w1_ready, s.u + 1)
                    if late(s, RING):
                        dve.wait_ge(centred_ready, s.u - RING + 1)
                    dve.tensor_tensor(hidden[:, s.slot], tiled(w1_ps[:]), k["b1_row"][:].unsqueeze(1).to_broadcast([P, TILES, D]),
                                      ALU.add).then_inc(hidden_ready, 1)

                def means(j):
                    if before(j, units):
                        dve.wait_ge(measured1, j.u + 1)
                    if late(j, NEXT):
                        dve.wait_ge(measured2, j.u - NEXT + 1)
                    if late(j, RING):
                        for applied in (x1_ready, x1_last_ready):
                            dve.wait_ge(applied, min(j.u - RING + 1, units) if isinstance(j.u, int) else j.u - RING + 1)
                    if late(j, NEXT + RING):
                        dve.wait_ge(hn_ready, j.u - NEXT - RING + 1)
                    norms.means(j)

                def activate(s):
                    b = s.slot % 2
                    dve.wait_ge(bn_ready, s.u + 1)
                    if late(s, 2):
                        dve.wait_ge(leaky_turned, s.u - 1)
                    dve.scalar_tensor_tensor(leaky[:, b], bnT[:, b], SLOPE, bnT[:, b], ALU.mult, ALU.max).then_inc(leaky_ready, 1)

                def mix(s):
                    b = s.slot % 2
                    dve.wait_ge(leaky_turned, s.u + 1)
                    dve.wait_ge(x_loaded[s.slot], (s.lap + 1) * 16)
                    if late(s, RING):
                        dve.wait_ge(x1_ready, s.u - RING + 1)
                        dve.wait_ge(x1_last_ready, s.u - RING + 1)
                    dve.tensor_tensor(mixed[:, s.slot], tiled(leaky_ps[:, b]), x_in[:, s.slot], ALU.add).then_inc(mixed_ready, 1)

                def measure2(s):
                    dve.wait_ge(hidden_ready, s.u + 1)
                    for t in range(TILES):
                        last = dve.bn_stats(stats[:, (s.slot + NEXT) % 2, TILES + t, :], hidden[:, s.slot, t, :])
                    last.then_inc(measured2, 1)

                def invert(j):
                    b = j.slot
                    dve.wait_ge(rooted, j.u + 1)
                    dve.reciprocal(small[:, b, 4, :], small[:, b, 4, :]).then_inc(inverted, 1)

                def measure1(s):
                    dve.wait_ge(mixed_ready, s.u + 1)
                    for t in range(TILES):
                        last = dve.bn_stats(stats[:, s.slot % 2, t, :], mixed[:, s.slot, t, :])
                    last.then_inc(measured1, 1)

                def shift(j):
                    dve.wait_ge(inverted, j.u + 1)
                    norms.shift(j).then_inc(shifted, 1)

                def keep_dot(s):
                    dve.wait_ge(dot_product, s.u + 1)
                    dve.tensor_copy(k["loop_dot"][:, bass.ds(s.u * TILES, TILES)], dots[:, 0:TILES]).then_inc(dot_kept, 1)

                dve.memset(stats[:], 0.0).then_inc(cleared, 1)
                dve.wait_ge(cleared, 1)
                dve.tensor_tensor(We1_sum[:], k["We1"][:, 0, :], k["We1"][:, 1, :], ALU.add).then_inc(halves_summed, 1)
                over_units(dve, units, [(8, hide), (15, keep_dot), (3, means, NEXT), (1, activate), (4, invert, NEXT), (3, norms.squares, NEXT),
                                        (2, mix), (4, shift, NEXT), (3, norms.variance, NEXT), (8, measure2), (2, measure1)])

            @block.gpsimd
            def _(pool):
                def apply2(s):
                    b, c = s.slot % 2, (s.slot + NEXT) % RING
                    pool.wait_ge(shifted, s.u + NEXT + 1)
                    if late(s, 2):
                        pool.wait_ge(h_turn_ready, s.u - 1)
                    pool.tensor_tensor(centred[:, b], hidden[:, s.slot], spread(small[:, c, 4, TILES:2 * TILES], D), ALU.mult).then_inc(centred_ready, 1)
                    pool.wait_ge(centred_ready, s.u + 1)
                    pool.tensor_tensor(hn[:, b], centred[:, b], spread(small[:, c, 5, TILES:2 * TILES], D), ALU.add).then_inc(hn_ready, 1)

                def apply1_last(s):
                    pool.wait_ge(shifted, s.u + 1)
                    if late(s, 1):
                        pool.wait_ge(x1_last_ready, s.u)
                    pool.tensor_tensor(x1_last[:], mixed[:, s.slot, TILES - 1:TILES, :], spread(small[:, s.slot, 4, TILES - 1:TILES], D),
                                       ALU.mult).then_inc(x1_scaled, 1)
                    if late(s, RING):
                        pool.wait_ge(x1_turn_ready, s.u - RING + 1)
                    pool.wait_ge(x1_scaled, s.u + 1)
                    pool.tensor_tensor(x1_out[:, s.slot, TILES - 1:TILES, :], x1_last[:], spread(small[:, s.slot, 5, TILES - 1:TILES], D),
                                       ALU.add).then_inc(x1_last_ready, 1)

                def bias(s):
                    pool.wait_ge(x1_ready, s.u + 1)
                    pool.wait_ge(x1_last_ready, s.u + 1)
                    if late(s, RING):
                        pool.wait_ge(x1_stored[s.slot], s.lap * 16)
                    pool.tensor_tensor(x1_biased[:, s.slot], x1_out[:, s.slot], k["bt2_row"][:].unsqueeze(1).to_broadcast([P, TILES, D]),
                                       ALU.add).then_inc(biased, 1)

                over_units(pool, units, [(5, apply1_last), (6, bias), (11, apply2)])

            @block.tensor
            def _(pe):
                def turn_x1(s):
                    pe.wait_ge(x1_ready, s.u + 1)
                    pe.wait_ge(x1_last_ready, s.u + 1)
                    if late(s, 1):
                        pe.wait_ge(x1T_ready, s.u)
                    for t in range(TILES):
                        last = pe.transpose(x1_turned[:, t * P:(t + 1) * P], x1_out[:, s.slot, t, :], k["ident"][:])
                    last.then_inc(x1_turn_ready, 1)

                def turn_h(s):
                    pe.wait_ge(hn_ready, s.u + 1)
                    if late(s, 1):
                        pe.wait_ge(hT_ready, s.u)
                    for t in range(TILES):
                        last = pe.transpose(h_turned[:, t * P:(t + 1) * P], hn[:, s.slot % 2, t, :], k["ident"][:])
                    last.then_inc(h_turn_ready, 1)

                def turn_leaky(s):
                    b = s.slot % 2
                    pe.wait_ge(leaky_ready, s.u + 1)
                    if late(s, 2):
                        pe.wait_ge(mixed_ready, s.u - 1)
                    for t in range(TILES):
                        last = pe.transpose(leaky_ps[:, b, t * P:(t + 1) * P], leaky[:, b, t * P:(t + 1) * P], k["ident"][:])
                    last.then_inc(leaky_turned, 1)

                def multiply(s):
                    pe.wait_ge(x1T_ready, s.u + 1)
                    if late(s, 1):
                        pe.wait_ge(hidden_ready, s.u)
                    for t in range(TILES):
                        last = pe.matmul(w1_ps[:, t * P:(t + 1) * P], x1T[:, s.slot % 2, t * P:(t + 1) * P], k["W1"][:], start=True, stop=True)
                    last.then_inc(w1_ready, 1)

                def turn_back(s):
                    pe.wait_ge(hT_ready, s.u + 1)
                    if late(s, 1):
                        pe.wait_ge(h_ready, s.u)
                    for t in range(TILES):
                        last = pe.transpose(h_back[:, t * P:(t + 1) * P], hT[:, s.slot % 2, t * P:(t + 1) * P], k["ident"][:])
                    last.then_inc(h_back_ready, 1)

                def pair(s):
                    if late(s, 1):
                        pe.wait_ge(pair_ready, s.u)
                    pe.matmul(pair_ps[:], We1_sum[:], hT[:, s.slot % 2], start=True, stop=True).then_inc(pair_product, 1)

                def dot(s):
                    pe.wait_ge(pair_ready, s.u + 1)
                    if late(s, 1):
                        pe.wait_ge(dot_kept, s.u)
                    for t in range(TILES):
                        last = pe.matmul(dots[:, t:t + 1], pair_hidden[:, s.slot % 2, t * P:(t + 1) * P], k["We2"][:], start=True, stop=True)
                    last.then_inc(dot_product, 1)

                pe.wait_ge(halves_summed, 1)
                over_units(pe, units, [(13, turn_back), (13, pair), (12, turn_h), (6, turn_x1), (1, turn_leaky), (7, multiply), (14, dot)])


def gate(nc, k, x1, h, sums, out, units):
    X1, H, SUMS, OUT = by_unit(x1), by_unit(h), by_unit(sums[0:units * UNIT, :]), by_unit(out)
    MIX = 3
    with ExitStack() as stack:
        m = Memory(nc, stack, "gate")
        h_in, s_in, x1_in = (m.sb(n, [P, RING, TILES, D]) for n in ("h_in", "s_in", "x1_in"))
        hT, sT, gT, nT = (m.sb(n, [P, 2, UNIT]) for n in ("hT", "sT", "gT", "nT"))
        change, n1, n1n, n2 = (m.sb(n, [P, 2, TILES, D]) for n in ("change", "n1", "n1n", "n2"))
        out_sb = m.sb("out_sb", [P, RING, TILES, D])
        stats1, stats2 = (m.sb(n, [P, 2, TILES, 6]) for n in ("stats1", "stats2"))
        small1, small2 = (m.sb(n, [P, 2, 6, TILES]) for n in ("small1", "small2"))
        h_turned, s_turned, g_ps, n_turned = (m.ps(n, [P, UNIT]) for n in ("h_turned", "s_turned", "g_ps", "n_turned"))
        g_back, n_back = (m.ps(n, [P, 2, UNIT]) for n in ("g_back", "n_back"))
        h_loaded, s_loaded, x1_loaded, stored = (m.sems(n, RING) for n in ("h_loaded", "s_loaded", "x1_loaded", "stored"))
        (in_turned, in_copied, g_product, g_ready, g_turned, mix_own, stat1_own, stat2_own, rstd1, rstd2, n1_own, out_own,
         n_turn_ready, nT_ready, n_back_ready, n2_ready) = (
            m.sem(n) for n in ("in_turned", "in_copied", "g_product", "g_ready", "g_turned", "mix_own", "stat1_own",
                               "stat2_own", "rstd1", "rstd2", "n1_own", "out_own", "n_turn_ready", "nT_ready",
                               "n_back_ready", "n2_ready"))
        tiled = lambda ap: ap.rearrange("p (t f) -> p t f", t=TILES)
        with nc.Block() as block:
            @block.sync
            def _(sp):
                def load(s):
                    if late(s, RING):
                        sp.wait_ge(mix_own, (s.u - RING + 1) * MIX)
                        sp.wait_ge(in_turned, s.u - RING + 1)
                    sp.dma_start(h_in[:, s.slot], H[s.u]).then_inc(h_loaded[s.slot], 16)
                    sp.dma_start(s_in[:, s.slot], SUMS[s.u]).then_inc(s_loaded[s.slot], 16)

                def load_x1(s):
                    if late(s, RING):
                        sp.wait_ge(n2_ready, s.u - RING + 1)
                    sp.dma_start(x1_in[:, s.slot], X1[s.u]).then_inc(x1_loaded[s.slot], 16)

                def store(s):
                    sp.wait_ge(out_own, (s.u + 1) * APPLY_STEPS)
                    sp.dma_start(OUT[s.u], out_sb[:, s.slot]).then_inc(stored[s.slot], 16)

                with sp.If(k["irregular"]):
                    over_units(sp, units, [(6, store), (2, load_x1), (0, load)])
                    for q in stored:
                        sp.wait_ge(q, units // RING * 16)

            @block.tensor
            def _(pe):
                def turn_in(s):
                    pe.wait_ge(h_loaded[s.slot], (s.lap + 1) * 16)
                    pe.wait_ge(s_loaded[s.slot], (s.lap + 1) * 16)
                    if late(s, 1):
                        pe.wait_ge(in_copied, s.u * 2)
                    for t in range(TILES):
                        pe.transpose(h_turned[:, t * P:(t + 1) * P], h_in[:, s.slot, t, :], k["ident"][:])
                        last = pe.transpose(s_turned[:, t * P:(t + 1) * P], s_in[:, s.slot, t, :], k["ident"][:])
                    last.then_inc(in_turned, 1)

                def multiply(s):
                    b = s.slot % 2
                    pe.wait_ge(in_copied, (s.u + 1) * 2)
                    if late(s, 1):
                        pe.wait_ge(g_ready, s.u)
                    pe.matmul(g_ps[:], k["Wg"][:, 0, :], hT[:, b], start=True, stop=False)
                    pe.matmul(g_ps[:], k["Wg"][:, 1, :], sT[:, b], start=False, stop=True).then_inc(g_product, 1)

                def turn_gate(s):
                    b = s.slot % 2
                    pe.wait_ge(g_ready, s.u + 1)
                    if late(s, 2):
                        pe.wait_ge(mix_own, (s.u - 1) * MIX)
                    for t in range(TILES):
                        last = pe.transpose(g_back[:, b, t * P:(t + 1) * P], gT[:, b, t * P:(t + 1) * P], k["ident"][:])
                    last.then_inc(g_turned, 1)

                def turn_n(s):
                    b = s.slot % 2
                    pe.wait_ge(n1_own, (s.u + 1) * APPLY_STEPS)
                    if late(s, 1):
                        pe.wait_ge(nT_ready, s.u)
                    for t in range(TILES):
                        last = pe.transpose(n_turned[:, t * P:(t + 1) * P], n1n[:, b, t, :], k["ident"][:])
                    last.then_inc(n_turn_ready, 1)

                def turn_back(s):
                    b = s.slot % 2
                    pe.wait_ge(nT_ready, s.u + 1)
                    if late(s, 2):
                        pe.wait_ge(n2_ready, s.u - 1)
                    for t in range(TILES):
                        last = pe.transpose(n_back[:, b, t * P:(t + 1) * P], nT[:, b, t * P:(t + 1) * P], k["ident"][:])
                    last.then_inc(n_back_ready, 1)

                with pe.If(k["irregular"]):
                    over_units(pe, units, [(4, turn_back), (3, turn_n), (2, turn_gate), (1, multiply), (0, turn_in)])

            @block.scalar
            def _(act):
                def copy(s):
                    b = s.slot % 2
                    act.wait_ge(in_turned, s.u + 1)
                    if late(s, 2):
                        act.wait_ge(g_product, s.u - 1)
                    act.activation(hT[:, b], h_turned[:], ACT.Copy).then_inc(in_copied, 1)
                    act.activation(sT[:, b], s_turned[:], ACT.Copy).then_inc(in_copied, 1)

                def squash(s):
                    b = s.slot % 2
                    act.wait_ge(g_product, s.u + 1)
                    if late(s, 2):
                        act.wait_ge(g_turned, s.u - 1)
                    act.activation(gT[:, b], g_ps[:], ACT.Sigmoid, bias=k["bg"][:]).then_inc(g_ready, 1)

                def affine(s):
                    b = s.slot % 2
                    act.wait_ge(n_turn_ready, s.u + 1)
                    if late(s, 2):
                        act.wait_ge(n_back_ready, s.u - 1)
                    act.activation(nT[:, b], n_turned[:], ACT.Identity, bias=k["zero"][:], scale=k["g2"][:]).then_inc(nT_ready, 1)

                with act.If(k["irregular"]):
                    over_units(act, units, [(3, affine), (1, squash), (0, copy)])

            @block.vector
            def _(dve):
                def mix(s):
                    b = s.slot % 2
                    chain = Chain(dve, mix_own, s.u * MIX)
                    dve.wait_ge(h_loaded[s.slot], (s.lap + 1) * 16)
                    dve.wait_ge(s_loaded[s.slot], (s.lap + 1) * 16)
                    chain.mark(dve.tensor_tensor(change[:, b], s_in[:, s.slot], h_in[:, s.slot], ALU.subtract))
                    chain.settle()
                    dve.wait_ge(g_turned, s.u + 1)
                    chain.mark(dve.tensor_tensor(change[:, b], tiled(g_back[:, b]), change[:, b], ALU.mult))
                    chain.settle()
                    chain.mark(dve.tensor_tensor(n1[:, b], change[:, b], h_in[:, s.slot], ALU.add))
                    chain.settle()
                    norm_stats(dve, Chain(dve, stat1_own, s.u * NORM_STEPS), n1[:, b], stats1[:, b], small1[:, b])

                def apply1(s):
                    b = s.slot % 2
                    dve.wait_ge(rstd1, s.u + 1)
                    if late(s, 2):
                        dve.wait_ge(n_turn_ready, s.u - 1)
                    norm_apply(dve, Chain(dve, n1_own, s.u * APPLY_STEPS), n1[:, b], n1n[:, b], small1[:, b])

                def residual(s):
                    b = s.slot % 2
                    dve.wait_ge(n_back_ready, s.u + 1)
                    dve.wait_ge(x1_loaded[s.slot], (s.lap + 1) * 16)
                    dve.tensor_tensor(n2[:, b], tiled(n_back[:, b]), x1_in[:, s.slot], ALU.add).then_inc(n2_ready, 1)
                    dve.wait_ge(n2_ready, s.u + 1)
                    norm_stats(dve, Chain(dve, stat2_own, s.u * NORM_STEPS), n2[:, b], stats2[:, b], small2[:, b])

                def apply2(s):
                    b = s.slot % 2
                    dve.wait_ge(rstd2, s.u + 1)
                    if late(s, RING):
                        dve.wait_ge(stored[s.slot], s.lap * 16)
                    norm_apply(dve, Chain(dve, out_own, s.u * APPLY_STEPS), n2[:, b], out_sb[:, s.slot], small2[:, b])

                with dve.If(k["irregular"]):
                    over_units(dve, units, [(5, apply2), (4, residual), (3, apply1), (2, mix)])

            @block.gpsimd
            def _(pool):
                def root1(s):
                    b = s.slot % 2
                    pool.wait_ge(stat1_own, (s.u + 1) * NORM_STEPS)
                    pool.tensor_tensor(small1[:, b, 4, :], small1[:, b, 3, :], k["power"][:, 0:TILES], ALU.pow).then_inc(rstd1, 1)

                def root2(s):
                    b = s.slot % 2
                    pool.wait_ge(stat2_own, (s.u + 1) * NORM_STEPS)
                    pool.tensor_tensor(small2[:, b, 4, :], small2[:, b, 3, :], k["power"][:, 0:TILES], ALU.pow).then_inc(rstd2, 1)

                with pool.If(k["irregular"]):
                    over_units(pool, units, [(4, root2), (2, root1)])


def attend(nc, k, x1, h, rel_rows, out, units):
    X1, H, OUT = by_unit(x1), by_unit(h), by_unit(out)
    REL = rel_rows.rearrange("(u t) s -> u (t s)", t=TILES)
    SUM, NEXT = TILES, 5
    RING = 8
    with ExitStack() as stack:
        m = Memory(nc, stack, "att")
        h_in, x1_in, rows, out_sb = (m.sb(n, [P, RING, TILES, D]) for n in ("h_in", "x1_in", "rows", "out_sb"))
        rel_in = m.sb("rel_in", [P, RING, UNIT])
        slot_src = m.sb("slot_src", [P, RING, TILES], I32)
        hT = m.sb("hT", [P, RING, UNIT])
        rowsT, value, pick, hidden, sT, gT = (m.sb(n, [P, 2, UNIT]) for n in ("rowsT", "value", "pick", "hidden", "sT", "gT"))
        weight = m.sb("weight", [P, 2, 2, TILES])
        weighted = m.sb("weighted", [P, 2, TILES, P])
        sums, change, n1n, scaled = (m.sb(n, [P, 2, TILES, D]) for n in ("sums", "change", "n1n", "scaled"))
        n1, n2 = (m.sb(n, [P, 4, TILES, D]) for n in ("n1", "n2"))
        stats = m.sb("stats", [P, 2, 2 * TILES, 6])
        small = m.sb("small", [P, 4, 6, 2 * TILES])
        h_or_sums, row_ps, value_ps, sum_ps, pre, g_ps, g_back, dots = (
            m.ps(n, [P, UNIT]) for n in ("h_or_sums", "row_ps", "value_ps", "sum_ps", "pre", "g_ps", "g_back", "dots"))
        h_loaded, rel_loaded, x1_loaded, rows_loaded, stored = (
            m.sems(n, RING) for n in ("h_loaded", "rel_loaded", "x1_loaded", "rows_loaded", "stored"))
        (rows_clear, slots_ready, passed, h_turned, rows_turned, hT_ready, rowsT_ready, value_product, value_ready,
         pick_ready, pre_product, hidden_ready, dot_product, weight_ready, weighted_ready, sum_product, sums_own,
         sums_turned, sT_ready, g_product, g_ready, g_turned, differed, multiplied, mixed, measured1, measured2, own, rooted, shifted, n1_ready, cleared,
         out_ready, scaled_ready, n2_ready) = (
            m.sem(n) for n in ("rows_clear", "slots_ready", "passed", "h_turned", "rows_turned", "hT_ready", "rowsT_ready",
                               "value_product", "value_ready", "pick_ready", "pre_product", "hidden_ready", "dot_product",
                               "weight_ready", "weighted_ready", "sum_product", "sums_own", "sums_turned", "sT_ready",
                               "g_product", "g_ready", "g_turned", "differed", "multiplied", "mixed", "measured1", "measured2", "own", "rooted", "shifted",
                               "n1_ready", "cleared", "out_ready", "scaled_ready", "n2_ready"))
        LAG_NORM, LAG_SCALE = 6, 9
        AHEAD = 3
        LAG_OUT = LAG_NORM + 2 + NEXT
        tiled = lambda ap: ap.rearrange("p (t f) -> p t f", t=TILES)

        def ahead(s, n):
            return min(s.u + n + 1, units) if isinstance(s.u, int) else s.u + n + 1

        with nc.Block() as block:
            @block.sync
            def _(sp):
                def load(s):
                    if late(s, RING):
                        sp.wait_ge(mixed, s.u - RING + 1)
                        sp.wait_ge(pick_ready, s.u - RING + 1)
                    sp.dma_start(h_in[:, s.slot], H[s.u]).then_inc(h_loaded[s.slot], 16)
                    sp.dma_start(rel_in[:, s.slot], REL[bass.ds(s.u, 1), :].to_broadcast([P, UNIT])).then_inc(rel_loaded[s.slot], 16)

                def load_x1(s):
                    if late(s, RING):
                        sp.wait_ge(n2_ready, s.u - RING + 1)
                    sp.dma_start(x1_in[:, s.slot], X1[s.u]).then_inc(x1_loaded[s.slot], 16)

                def store(s):
                    sp.wait_ge(out_ready, s.u + 1)
                    sp.dma_start(OUT[s.u], out_sb[:, s.slot]).then_inc(stored[s.slot], 16)

                with sp.If(k["is_regular"]):
                    over_units(sp, units, [(2, load), (AHEAD + 4, load_x1), (AHEAD + LAG_OUT + 1, store)], RING)
                    for slot, q in enumerate(stored):
                        sp.wait_ge(q, len(range(slot, units, RING)) * 16)

            @block.gpsimd
            def _(pool):
                def gather(s):
                    if late(s, RING):
                        pool.wait_ge(sum_product, s.u - RING + 1)
                    pool.wait_ge(slots_ready, s.u + 1)
                    pool.sem_inc(passed, 1)
                    for t in range(TILES):
                        pool.indirect_dma_start(out=rows[:, s.slot, t, :], out_offset=None, in_=h,
                                                in_offset=bass.IndirectOffsetOnAxis(ap=slot_src[:, s.slot, t:t + 1], axis=0),
                                                bounds_check=units * UNIT - 1, oob_is_err=False).then_inc(rows_loaded[s.slot], 16)

                def root(j):
                    b = j.slot % 4
                    pool.wait_ge(own, (j.u + 1) * SMALLS)
                    pool.tensor_tensor(small[:, b, 4, :], small[:, b, 3, :], k["power"][:], ALU.pow).then_inc(rooted, 1)

                def scale(s):
                    b = s.slot % 2
                    pool.wait_ge(n1_ready, s.u + 1)
                    if late(s, 2):
                        pool.wait_ge(n2_ready, s.u - 1)
                    pool.tensor_tensor(scaled[:, b], n1n[:, b], k["g2_row"][:].unsqueeze(1).to_broadcast([P, TILES, D]),
                                       ALU.mult).then_inc(scaled_ready, 1)

                with pool.If(k["is_regular"]):
                    pool.wait_ge(rows_clear, 1)
                    over_units(pool, units, [(1, gather), (AHEAD + LAG_NORM + 1, root, NEXT), (AHEAD + LAG_SCALE + 1, scale)], RING)

            @block.tensor
            def _(pe):
                def turn_in(s):
                    pe.wait_ge(h_loaded[s.slot], (s.lap + 1) * 16)
                    if late(s, 4):
                        pe.wait_ge(sT_ready, s.u - 3)
                    for t in range(TILES):
                        last = pe.transpose(h_or_sums[:, t * P:(t + 1) * P], h_in[:, s.slot, t, :], k["ident"][:])
                    last.then_inc(h_turned, 1)
                    pe.wait_ge(rows_loaded[s.slot], (s.lap + 1) * 16 * TILES)
                    if late(s, 1):
                        pe.wait_ge(rowsT_ready, s.u)
                    for t in range(TILES):
                        last = pe.transpose(row_ps[:, t * P:(t + 1) * P], rows[:, s.slot, t, :], k["ident"][:])
                    last.then_inc(rows_turned, 1)

                def dot(s):
                    b = s.slot % 2
                    pe.wait_ge(hidden_ready, s.u + 1)
                    if late(s, 2):
                        pe.wait_ge(weight_ready, (s.u - 1) * 2)
                    for t in range(TILES):
                        last = pe.matmul(dots[:, b * TILES + t:b * TILES + t + 1], hidden[:, b, t * P:(t + 1) * P], k["We2"][:], start=True, stop=True)
                    last.then_inc(dot_product, 1)

                def values(s):
                    b = s.slot % 2
                    pe.wait_ge(hT_ready, s.u + 1)
                    if late(s, 1):
                        pe.wait_ge(value_ready, s.u)
                    for t in range(TILES):
                        last = pe.matmul(value_ps[:, t * P:(t + 1) * P], hT[:, s.slot, t * P:(t + 1) * P], k["We1"][:, 1, :], start=True, stop=True)
                    last.then_inc(value_product, 1)

                def sum_rows(s):
                    b = s.slot % 2
                    pe.wait_ge(weighted_ready, s.u + 1)
                    if late(s, 1):
                        pe.wait_ge(sums_own, s.u * SUM)
                    for t in range(TILES):
                        last = pe.matmul(sum_ps[:, t * P:(t + 1) * P], weighted[:, b, t, :], rows[:, s.slot, t, :], start=True, stop=True)
                    last.then_inc(sum_product, 1)

                def turn_gate(s):
                    b = s.slot % 2
                    pe.wait_ge(g_ready, s.u + 1)
                    if late(s, 1):
                        pe.wait_ge(multiplied, s.u)
                    for t in range(TILES):
                        last = pe.transpose(g_back[:, t * P:(t + 1) * P], gT[:, b, t * P:(t + 1) * P], k["ident"][:])
                    last.then_inc(g_turned, 1)

                def pairs(s):
                    b = s.slot % 2
                    pe.wait_ge(rowsT_ready, s.u + 1)
                    if late(s, 1):
                        pe.wait_ge(hidden_ready, s.u)
                    pe.matmul(pre[:], k["We1"][:, 0, :], rowsT[:, b], start=True, stop=False, skip_group_check=True)
                    pe.wait_ge(value_ready, s.u + 1)
                    pe.wait_ge(pick_ready, s.u + 1)
                    for t in range(TILES):
                        last = pe.matmul(pre[:, t * P:(t + 1) * P], value[:, b, t * P:(t + 1) * P], pick[:, b, t * P:(t + 1) * P],
                                         start=False, stop=(t == TILES - 1), skip_group_check=True)
                    last.then_inc(pre_product, 1)

                def turn_sums(s):
                    b = s.slot % 2
                    pe.wait_ge(sums_own, (s.u + 1) * SUM)
                    pe.wait_ge(hT_ready, ahead(s, 3))
                    for t in range(TILES):
                        last = pe.transpose(h_or_sums[:, t * P:(t + 1) * P], sums[:, b, t, :], k["ident"][:])
                    last.then_inc(sums_turned, 1)

                def gates(s):
                    b = s.slot % 2
                    if late(s, 1):
                        pe.wait_ge(g_ready, s.u)
                    pe.matmul(g_ps[:], k["Wg"][:, 0, :], hT[:, s.slot], start=True, stop=False)
                    pe.wait_ge(sT_ready, s.u + 1)
                    pe.matmul(g_ps[:], k["Wg"][:, 1, :], sT[:, b], start=False, stop=True).then_inc(g_product, 1)

                with pe.If(k["is_regular"]):
                    over_units(pe, units, delayed(AHEAD, [
                        (2, dot), (0, turn_in), (4, gates), (0, values), (3, turn_sums), (2, sum_rows),
                        (0, pairs), (4, turn_gate)]), RING)

            @block.scalar
            def _(act):
                def copy_in(s):
                    b = s.slot % 2
                    act.wait_ge(h_turned, s.u + 1)
                    if late(s, RING):
                        act.wait_ge(g_product, s.u - RING + 1)
                    act.activation(hT[:, s.slot], h_or_sums[:], ACT.Copy).then_inc(hT_ready, 1)
                    act.wait_ge(rows_turned, s.u + 1)
                    if late(s, 2):
                        act.wait_ge(pre_product, s.u - 1)
                    act.activation(rowsT[:, b], row_ps[:], ACT.Copy).then_inc(rowsT_ready, 1)

                def weigh(s):
                    b = s.slot % 2
                    act.wait_ge(dot_product, s.u + 1)
                    if late(s, 2):
                        act.wait_ge(weighted_ready, s.u - 1)
                        act.wait_ge(sums_own, (s.u - 1) * SUM)
                    act.activation(weight[:, b, 0, :], dots[:, b * TILES:(b + 1) * TILES], ACT.Sigmoid, bias=k["be2"][:]).then_inc(weight_ready, 1)
                    act.activation(weight[:, b, 1, :], k["loop_dot"][:, bass.ds(s.u * TILES, TILES)], ACT.Sigmoid, bias=k["be2"][:]).then_inc(weight_ready, 1)

                def copy_values(s):
                    b = s.slot % 2
                    act.wait_ge(value_product, s.u + 1)
                    if late(s, 2):
                        act.wait_ge(pre_product, s.u - 1)
                    act.activation(value[:, b], value_ps[:], ACT.Copy).then_inc(value_ready, 1)

                def rectify(s):
                    b = s.slot % 2
                    act.wait_ge(pre_product, s.u + 1)
                    if late(s, 2):
                        act.wait_ge(dot_product, s.u - 1)
                    act.activation(hidden[:, b], pre[:], ACT.Relu, bias=k["be1"][:]).then_inc(hidden_ready, 1)

                def copy_sums(s):
                    b = s.slot % 2
                    act.wait_ge(sums_turned, s.u + 1)
                    if late(s, 2):
                        act.wait_ge(g_product, s.u - 1)
                    act.activation(sT[:, b], h_or_sums[:], ACT.Copy).then_inc(sT_ready, 1)

                def squash(s):
                    b = s.slot % 2
                    act.wait_ge(g_product, s.u + 1)
                    if late(s, 2):
                        act.wait_ge(g_turned, s.u - 1)
                    act.activation(gT[:, b], g_ps[:], ACT.Sigmoid, bias=k["bg"][:]).then_inc(g_ready, 1)

                def apply1(s, half):
                    b = s.slot % 2
                    if half == 0:
                        act.wait_ge(shifted, s.u + 1)
                        if late(s, 2):
                            act.wait_ge(scaled_ready, s.u - 1)
                    for t in range(2 * half, 2 * half + 2):
                        last = act.activation(n1n[:, b, t, :], n1[:, s.slot % 4, t, :], ACT.Identity, bias=small[:, s.slot % 4, 5, t:t + 1],
                                              scale=small[:, s.slot % 4, 4, t:t + 1])
                    if half:
                        last.then_inc(n1_ready, 1)

                def apply2(s, half):
                    c = (s.slot + NEXT) % 4
                    if half == 0:
                        act.wait_ge(shifted, s.u + NEXT + 1)
                        if late(s, RING):
                            act.wait_ge(stored[s.slot], s.lap * 16)
                    for t in range(2 * half, 2 * half + 2):
                        last = act.activation(out_sb[:, s.slot, t, :], n2[:, s.slot % 4, t, :], ACT.Identity,
                                              bias=small[:, c, 5, TILES + t:TILES + t + 1], scale=small[:, c, 4, TILES + t:TILES + t + 1])
                    if half:
                        last.then_inc(out_ready, 1)

                with act.If(k["is_regular"]):
                    over_units(act, units, delayed(AHEAD, [
                        (2, weigh), (0, copy_in), (LAG_NORM + 2, lambda s: apply1(s, 0)), (4, squash),
                        (0, copy_values), (LAG_NORM + 2, lambda s: apply1(s, 1)), (3, copy_sums),
                        (LAG_OUT, lambda s: apply2(s, 0)), (0, rectify),
                        (LAG_OUT, lambda s: apply2(s, 1))]), RING)

            @block.vector
            def _(dve):
                norms = Norms(dve, own, stats, small)

                def picks(s):
                    b = s.slot % 2
                    dve.wait_ge(rel_loaded[s.slot], (s.lap + 1) * 16)
                    if late(s, 2):
                        dve.wait_ge(pre_product, s.u - 1)
                    dve.tensor_scalar(pick[:, b], rel_in[:, s.slot], k["trash"][:], None, ALU.is_equal).then_inc(pick_ready, 1)

                def copy_slots(s):
                    if late(s, RING):
                        dve.wait_ge(rows_loaded[s.slot], s.lap * 16 * TILES)
                    dve.tensor_copy(slot_src[:, s.slot, :], k["slot_src"][:, bass.ds(s.u * TILES, TILES)]).then_inc(slots_ready, 1)

                def weigh_hot(s):
                    b = s.slot % 2
                    dve.wait_ge(weight_ready, (s.u + 1) * 2)
                    if late(s, 2):
                        dve.wait_ge(sum_product, s.u - 1)
                    for t in range(TILES):
                        last = dve.tensor_scalar(weighted[:, b, t, :], k["lane"][:], k["slot_rel"][:, bass.ds(s.u * TILES + t, 1)],
                                                 weight[:, b, 0, t:t + 1], ALU.is_equal, ALU.mult)
                    last.then_inc(weighted_ready, 1)

                def add_loops(s):
                    b = s.slot % 2
                    dve.wait_ge(sum_product, s.u + 1)
                    dve.wait_ge(h_loaded[s.slot], (s.lap + 1) * 16)
                    if late(s, 2):
                        dve.wait_ge(differed, s.u - 1)
                        dve.wait_ge(sums_turned, s.u - 1)
                    for t in range(TILES):
                        dve.scalar_tensor_tensor(sums[:, b, t, :], h_in[:, s.slot, t, :], weight[:, b, 1, t:t + 1],
                                                 sum_ps[:, t * P:(t + 1) * P], ALU.mult, ALU.add).then_inc(sums_own, 1)

                def differ(s):
                    b = s.slot % 2
                    dve.wait_ge(sums_own, (s.u + 1) * SUM)
                    if late(s, 2):
                        dve.wait_ge(mixed, s.u - 1)
                    dve.tensor_tensor(change[:, b], sums[:, b], h_in[:, s.slot], ALU.subtract).then_inc(differed, 1)

                def multiply(s):
                    b = s.slot % 2
                    dve.wait_ge(differed, s.u + 1)
                    dve.wait_ge(g_turned, s.u + 1)
                    dve.tensor_tensor(change[:, b], tiled(g_back[:]), change[:, b], ALU.mult).then_inc(multiplied, 1)

                def mix(s):
                    b = s.slot % 2
                    dve.wait_ge(multiplied, s.u + 1)
                    if late(s, 4):
                        dve.wait_ge(n1_ready, s.u - 3)
                    dve.tensor_tensor(n1[:, s.slot % 4], change[:, b], h_in[:, s.slot], ALU.add).then_inc(mixed, 1)

                def measure1(s):
                    dve.wait_ge(mixed, s.u + 1)
                    for t in range(TILES):
                        last = dve.bn_stats(stats[:, s.slot % 2, t, :], n1[:, s.slot % 4, t, :])
                    last.then_inc(measured1, 1)

                def means(j):
                    if before(j, units):
                        dve.wait_ge(measured1, j.u + 1)
                    if late(j, NEXT):
                        dve.wait_ge(measured2, j.u - NEXT + 1)
                    if late(j, 4):
                        dve.wait_ge(n1_ready, min(j.u - 3, units) if isinstance(j.u, int) else j.u - 3)
                    if late(j, NEXT + 4):
                        dve.wait_ge(out_ready, j.u - NEXT - 3)
                    norms.means(j)

                def shift(j):
                    dve.wait_ge(rooted, j.u + 1)
                    norms.shift(j).then_inc(shifted, 1)

                def residual(s):
                    b = s.slot % 2
                    dve.wait_ge(scaled_ready, s.u + 1)
                    dve.wait_ge(x1_loaded[s.slot], (s.lap + 1) * 16)
                    if late(s, 4):
                        dve.wait_ge(out_ready, s.u - 3)
                    dve.tensor_tensor(n2[:, s.slot % 4], scaled[:, b], x1_in[:, s.slot], ALU.add).then_inc(n2_ready, 1)

                def measure2(s):
                    dve.wait_ge(n2_ready, s.u + 1)
                    for t in range(TILES):
                        last = dve.bn_stats(stats[:, (s.slot + NEXT) % 2, TILES + t, :], n2[:, s.slot % 4, t, :])
                    last.then_inc(measured2, 1)

                with dve.If(k["is_regular"]):
                    dve.memset(rows[:], 0.0).then_inc(rows_clear, 1)
                    dve.memset(stats[:], 0.0).then_inc(cleared, 1)
                    dve.wait_ge(cleared, 1)
                    over_units(dve, units, [(0, copy_slots)] + delayed(AHEAD, [
                        (LAG_NORM + 2, shift, NEXT), (3, add_loops), (0, picks), (LAG_NORM, means, NEXT),
                        (2, weigh_hot), (LAG_NORM, norms.squares, NEXT), (4, differ),
                        (LAG_NORM, norms.variance, NEXT), (5, multiply), (LAG_SCALE + 1, residual), (5, mix),
                        (LAG_SCALE + 1, measure2), (5, measure1)]), RING)


VECTORS = {"gcn_b": "L0_gnn_gcn_b", "rs_b": "L0_gnn_rs_b",
           "bn_g": "L0_gnn_bn_g", "bn_b": "L0_gnn_bn_b", "g1": "L1_gnn_g1", "bt1": "L1_gnn_bt1",
           "be1": "L1_gnn_be1", "bg": "L1_gnn_bg", "g2": "L1_gnn_g2", "be2": "L1_gnn_be2"}
ROWS = {"ln_g_row": "L0_gnn_ln_g", "ln_b_row": "L0_gnn_ln_b", "b1_row": "L1_gnn_b1", "g2_row": "L1_gnn_g2", "bt2_row": "L1_gnn_bt2"}
MATRICES = {"gcn_w": "L0_gnn_gcn_w", "rs_w": "L0_gnn_rs_w", "W1": "L1_gnn_W1", "We1": "L1_gnn_We1",
            "We2": "L1_gnn_We2", "Wg": "L1_gnn_Wg"}


def load_edges(nc, stack, src, dst, chunks, tiles, rows, k):
    m = Memory(nc, stack, "k")
    for name in ("src", "dst", "place"):
        k[name] = m.sb(name, [P, chunks], I32)
    k["slot_src"], k["slot_rel"] = m.sb("slot_src", [P, tiles], I32), m.sb("slot_rel", [P, tiles])
    k["regular"] = m.sb("regular", [1, 2], I32)
    for name in ("dinv", "root", "edges", "loop_dot"):
        k[name] = m.sb(name, [P, tiles])
    for name in ("bn_scale", "bn_shift", "conv_b"):
        k[name] = m.sb(name, [P, 1])
    for name in rows:
        k[name] = m.sb(name, [P, D])
    loaded = m.sem("loaded")
    with nc.Block() as block:
        @block.sync
        def _(sp):
            sp.dma_start(k["src"][:], src).then_inc(loaded, 16)
            sp.dma_start(k["dst"][:], dst).then_inc(loaded, 16)
            for name, row in rows.items():
                sp.dma_start(k[name][:], row.rearrange("(a f) -> a f", a=1).to_broadcast([P, D])).then_inc(loaded, 16)
            sp.wait_ge(loaded, 16 * (2 + len(rows)))

        @block.vector
        def _(dve):
            dve.tensor_tensor(k["conv_b"][:], k["gcn_b"][:], k["rs_b"][:], ALU.add)


def build(nc, nodes, x, src, dst, ends, heads, line, rows, weights, out):
    padded = x.shape[0]
    tiles, units, chunks = padded // P, padded // UNIT, src.shape[1]
    table = lambda name, shape: nc.dram_tensor(name, shape, F32).ap()
    y, x1, h = (table(n, [padded, D]) for n in ("messages", "x1", "h"))
    sums1, sums2 = (table(n, [padded + P, D]) for n in ("sums1", "sums2"))
    counts = table("counts", [padded + P, 1])
    outT = table("outT", [D, padded])
    with ExitStack() as stack:
        k = build_constants(nc, Memory(nc, stack, "k0"), weights)
        load_edges(nc, stack, src, dst, chunks, tiles, rows, k)
        rel_rows = table("rel_rows", [tiles, SLOTS])
        index_edges(nc, k, ends, heads, line, rel_rows, tiles)
        k["is_regular"] = nc.values_load(k["regular"][0:1, 0:1], min_val=0, max_val=1)
        k["irregular"] = nc.values_load(k["regular"][0:1, 1:2], min_val=0, max_val=1)
        clear_tables(nc, k, [sums1, sums2, counts])
        count_edges(nc, k, counts, chunks, padded, tiles)
        degrees(nc, k, tiles)
        make_messages(nc, k, x, y, units)
        add_messages(nc, k, y, sums1, chunks)
        convolve(nc, k, y, sums1, outT, units, nodes)
        embed(nc, k, x, outT, x1, h, units)
        attend(nc, k, x1, h, rel_rows, out, units)
        add_messages(nc, k, h, sums2, chunks, k)
        gate(nc, k, x1, h, sums2, out, units)


def kernel(**inputs):
    import concourse.bacc as bacc
    from concourse.bass_utils import run_bass_kernel_spmd

    nc = bacc.Bacc("TRN2", target_bir_lowering=False, num_devices=1)
    x = np.asarray(inputs["x"])
    nodes, edges = x.shape[0], inputs["src"].shape[0]
    padded = -(-nodes // (UNIT * RING)) * UNIT * RING
    chunks = -(-(edges + padded - nodes) // (2 * P)) * 2
    spare = chunks * P - edges
    arrays = {"x": np.zeros((padded, D), x.dtype)}
    arrays["x"][:nodes] = x
    loops = (nodes + np.arange(spare) * (padded - nodes) // spare).astype(np.int32)
    lines = {name: np.concatenate([np.asarray(inputs[name]), loops]) for name in ("src", "dst")}
    for name, ends in lines.items():
        arrays[name] = np.ascontiguousarray(ends.reshape(chunks, P).T)
    beyond = np.full((WINDOW_ROWS, 2 * HALF), padded, np.int32)
    arrays["ends"] = np.concatenate([np.hstack([lines["dst"].reshape(-1, HALF), lines["src"].reshape(-1, HALF)]), beyond])
    arrays["heads"] = np.ascontiguousarray(lines["dst"][::HALF])
    arrays["line"] = np.stack([lines["dst"], np.append(lines["dst"][1:], lines["dst"][-1:])])
    names = {**MATRICES, **VECTORS}
    for short, name in {**names, **ROWS}.items():
        arrays[short] = np.ascontiguousarray(inputs[name])
    ap = {n: nc.dram_tensor(f"in_{n}", a.shape, mybir.dt.from_np(a.dtype), kind="ExternalInput").ap()
          for n, a in arrays.items()}
    out = nc.dram_tensor("out", (padded, D), F32, kind="ExternalOutput").ap()
    build(nc, nodes, ap["x"], ap["src"], ap["dst"], ap["ends"], ap["heads"], ap["line"], {n: ap[n] for n in ROWS},
          {n: ap[n] for n in names}, out)
    result = run_bass_kernel_spmd(nc, [{f"in_{n}": a for n, a in arrays.items()}], core_ids=[0])
    return np.asarray(result.results[0]["out"])[:nodes]
```
